# Optimizing a Trainium2 kernel written in Bass

```python
import numpy as np
import jax
import jax.numpy as jnp

def _softmax(x, axis=-1):
    return jax.nn.softmax(x, axis=axis)

def _gelu(x):
    return jax.nn.gelu(x, approximate=True)

def _silu(x):
    return jax.nn.silu(x)

def _sigmoid(x):
    return jax.nn.sigmoid(x)

def _layernorm(x, axis=-1, eps=1e-05):
    m = jnp.mean(x, axis=axis, keepdims=True)
    v = jnp.var(x, axis=axis, keepdims=True)
    return (x - m) / jnp.sqrt(v + eps)

def _scatter_add(tgt, idx, src, axis=0):
    return tgt.at[idx].add(src)

def _segment_sum(src, seg, n):
    return jax.ops.segment_sum(src, seg, n)
kernel_name = 'mk_xattn_ffn_d2_seqx_r8_a9e6c0'

def setup_inputs(seed: int=0):
    np.random.seed(seed)
    _w = jnp.asarray

    def _rec_inputs():
        import jax
        import jax.numpy as jnp
        _rk = jax.random.key(seed)
        x = 0.002226 + 0.9996 * jax.random.normal(jax.random.fold_in(_rk, 1), (32, 128, 128), jnp.float32)
        _lenS = 128 - jax.random.randint(jax.random.fold_in(_rk, 7), (32,), 0, max(1, 128 // 4) + 1, jnp.int32)
        _lenS2 = 120 - jax.random.randint(jax.random.fold_in(_rk, 8), (32,), 0, max(1, 120 // 4) + 1, jnp.int32)
        _ctx_1024P = jax.random.normal(jax.random.fold_in(_rk, 11), (32, 16, 128), jnp.float32)
        _ctx_1024c = jax.random.dirichlet(jax.random.fold_in(_rk, 511), 0.3 * jnp.ones((16,), jnp.float32), (32, 120))
        _ctx_1024t = jnp.einsum('bsk,bkd->bsd', _ctx_1024c, _ctx_1024P)
        _ctx_1024t = _ctx_1024t * jax.lax.rsqrt(jnp.mean(jnp.square(_ctx_1024t)) + 1e-12) * 0.953939
        ctx_1024 = -7.10856e-05 + 0.999911 * (_ctx_1024t + 0.3 * jax.random.normal(jax.random.fold_in(_rk, 611), (32, 120, 128), jnp.float32))
        _validS = jnp.arange(128)[None, :] < _lenS[:, None]
        _validS2 = jnp.arange(120)[None, :] < _lenS2[:, None]
        _causal = jnp.tril(jnp.ones((128, 128), dtype=bool))
        mask_BxS2_bk0 = jnp.logical_not(jnp.broadcast_to(_validS2[:, :], (32, 120)))
        mask_1x1xSxS2_ik0 = jnp.where(jnp.broadcast_to(_validS2[0:1, None, None, :], (1, 1, 128, 120)), 0, 1).astype(jnp.int32)
        return (x, ctx_1024, mask_BxS2_bk0, mask_1x1xSxS2_ik0)
    x, ctx_1024, mask_BxS2_bk0, mask_1x1xSxS2_ik0 = _rec_inputs()

    def _L0_xattn_setup():
        import jax, jax.numpy as jnp
        import numpy as np
        DIM, DIM_HEAD, HEADS, SCALE = (128, 64, 8, 8.0)
        INNER = DIM_HEAD * HEADS
        LN_EPS = 1e-05
        L2_EPS = 1e-12

        def layer_norm(x, w, b):
            mu = jnp.mean(x, axis=-1, keepdims=True)
            var = jnp.mean(jnp.square(x - mu), axis=-1, keepdims=True)
            return (x - mu) * jax.lax.rsqrt(var + LN_EPS) * w + b

        def l2norm(t):
            n = jnp.sqrt(jnp.sum(jnp.square(t), axis=-1, keepdims=True))
            return t / jnp.maximum(n, L2_EPS)
        key = jax.random.key(seed)
        ks = jax.random.split(key, 8)
        b, n, m = (8, 1024, 64)
        x = jax.random.normal(ks[0], (b, n, DIM), dtype=jnp.float32)
        latents = jax.random.normal(ks[1], (b, m, DIM), dtype=jnp.float32)
        mask = jax.random.randint(ks[2], (b, n), 0, 2) > 0
        Wq = jax.random.normal(ks[3], (DIM, INNER), dtype=jnp.float32) * DIM ** (-0.5)
        Wkv = jax.random.normal(ks[4], (DIM, 2 * INNER), dtype=jnp.float32) * DIM ** (-0.5)
        Wo = jax.random.normal(ks[5], (INNER, DIM), dtype=jnp.float32) * INNER ** (-0.5)
        return {'x': x, 'latents': latents, 'mask': mask, 'ln_x_w': jnp.ones((DIM,)), 'ln_x_b': jnp.zeros((DIM,)), 'ln_l_w': jnp.ones((DIM,)), 'ln_l_b': jnp.zeros((DIM,)), 'Wq': Wq, 'Wkv': Wkv, 'q_scale': jnp.ones((DIM_HEAD,)), 'k_scale': jnp.ones((DIM_HEAD,)), 'Wo': Wo, 'ln_o_w': jnp.ones((DIM,)), 'ln_o_b': jnp.zeros((DIM,))}
    _L0_xattn_all = _L0_xattn_setup()
    _L0_xattn_in = {k: v for k, v in _L0_xattn_all.items() if k in ('ln_x_w', 'ln_x_b', 'ln_l_w', 'ln_l_b', 'Wq', 'Wkv', 'q_scale', 'k_scale', 'Wo', 'ln_o_w', 'ln_o_b')}
    del _L0_xattn_all

    def _L0_ffn_setup():
        import jax, jax.numpy as jnp
        import numpy as np
        N_EMBD = 128
        ITER_SIZE = 4 * N_EMBD
        FULL_SIZE = 3 * ITER_SIZE
        R = 0.7

        def _topk_mask(ck, k):
            probs = jax.nn.softmax(ck, axis=-1)
            _, idx = jax.lax.top_k(probs, k)
            b = jnp.arange(probs.shape[0])[:, None]
            return jnp.zeros_like(probs).at[b, idx].set(1.0)

        def _forward(x, Wm, Wp, Wc1, Wc2):
            B = x.shape[0]
            base = jnp.zeros((B, FULL_SIZE), x.dtype).at[:, :ITER_SIZE].set(1.0)

            def step(carry, _):
                xc, active, history, done = carry
                h = jnp.einsum('btc,fc->btf', xc, Wm) * active[:, None, :]
                h = jax.nn.relu(h)
                x_new = jnp.einsum('btf,cf->btc', h, Wp)
                pooled = x_new.mean(axis=1)
                ck = jnp.einsum('bd,fd->bf', jax.nn.relu(jnp.einsum('bc,dc->bd', pooled, Wc1)), Wc2)
                new_mask = _topk_mask(ck, ITER_SIZE)
                combined = jnp.clip(history + new_mask, 0.0, 1.0)
                novelty = (combined - history).sum(axis=1).mean() / ITER_SIZE
                done_next = jnp.logical_or(done, novelty < R)
                x_out = jnp.where(done, xc, x_new)
                active_out = jnp.where(done, active, new_mask)
                history_out = jnp.where(done, history, combined)
                return ((x_out, active_out, history_out, done_next), None)
            init = (x, base, base, jnp.array(False))
            (x_fin, _, _, _), _ = jax.lax.scan(step, init, None, length=3)
            return x_fin
        key = jax.random.key(seed)
        ks = jax.random.split(key, 5)
        B, T = (8, 128)
        s = 0.02
        return {'x': jax.random.normal(ks[0], (B, T, N_EMBD), jnp.float32), 'Wm': jax.random.normal(ks[1], (FULL_SIZE, N_EMBD), jnp.float32) * s, 'Wp': jax.random.normal(ks[2], (N_EMBD, FULL_SIZE), jnp.float32) * s, 'Wc1': jax.random.normal(ks[3], (N_EMBD // 4, N_EMBD), jnp.float32) * s, 'Wc2': jax.random.normal(ks[4], (FULL_SIZE, N_EMBD // 4), jnp.float32) * s}
    _L0_ffn_all = _L0_ffn_setup()
    _L0_ffn_in = {k: v for k, v in _L0_ffn_all.items() if k in ('Wm', 'Wp', 'Wc1', 'Wc2')}
    del _L0_ffn_all

    def _L1_xattn_setup():
        import jax, jax.numpy as jnp
        import numpy as np
        D_MODEL = 128
        H = 16
        D_K = D_MODEL // H
        MASK_VALUE = -2000000000.0
        key = jax.random.key(seed)
        ks = jax.random.split(key, 7)
        B, S = (2, 256)
        scale = 1.0 / np.sqrt(D_MODEL)
        inp = {'q': jax.random.normal(ks[0], (B, S, D_MODEL), jnp.float32), 'k': jax.random.normal(ks[1], (B, S, D_MODEL), jnp.float32), 'v': jax.random.normal(ks[2], (B, S, D_MODEL), jnp.float32), 'mask': jnp.tril(jnp.ones((1, 1, S, S), jnp.int32)), 'w_q': jax.random.normal(ks[3], (D_MODEL, D_MODEL), jnp.float32) * scale, 'w_k': jax.random.normal(ks[4], (D_MODEL, D_MODEL), jnp.float32) * scale, 'w_v': jax.random.normal(ks[5], (D_MODEL, D_MODEL), jnp.float32) * scale, 'w_o': jax.random.normal(ks[6], (D_MODEL, D_MODEL), jnp.float32) * scale}
        return inp
    _L1_xattn_all = _L1_xattn_setup()
    _L1_xattn_in = {k: v for k, v in _L1_xattn_all.items() if k in ('w_q', 'w_k', 'w_v', 'w_o')}
    del _L1_xattn_all

    def _L1_ffn_setup():
        import jax, jax.numpy as jnp
        import numpy as np
        EMB = 128
        HEADS = 16
        SEQ = 256
        LATENT = 64
        N_EXP = 8
        TOP_K = 2
        EXP_DIM = 256
        BATCH = 2
        EPS = 1e-06

        def _rmsnorm(x, g):
            return x * jax.lax.rsqrt(jnp.mean(x * x, axis=-1, keepdims=True) + EPS) * g

        def _mla(h, Wq, Wdkv, Wuk, Wuv, Wo):
            B, S, D = h.shape
            hd = D // HEADS
            q = (h @ Wq).reshape(B, S, HEADS, hd)
            c = h @ Wdkv
            k = (c @ Wuk).reshape(B, S, HEADS, hd)
            v = (c @ Wuv).reshape(B, S, HEADS, hd)
            scores = jnp.einsum('bqhd,bkhd->bhqk', q, k) / jnp.sqrt(jnp.asarray(hd, h.dtype))
            causal = jnp.tril(jnp.ones((S, S), bool))
            scores = jnp.where(causal, scores, jnp.asarray(-1000000000.0, h.dtype))
            a = jax.nn.softmax(scores, axis=-1)
            out = jnp.einsum('bhqk,bkhd->bqhd', a, v).reshape(B, S, D)
            return out @ Wo

        def _moe(h, gate_w, w1, w2):
            B, S, D = h.shape
            t = h.reshape(B * S, D)
            logits = t @ gate_w
            top_v, top_i = jax.lax.top_k(logits, TOP_K)
            gates = jax.nn.softmax(top_v, axis=-1)
            T = t.shape[0]
            combine = jnp.zeros((T, N_EXP), t.dtype).at[jnp.arange(T)[:, None], top_i].add(gates)
            hid = jax.nn.silu(jnp.einsum('td,edh->teh', t, w1))
            ye = jnp.einsum('teh,ehd->ted', hid, w2)
            out = jnp.einsum('te,ted->td', combine, ye)
            return out.reshape(B, S, D)
        key = jax.random.key(seed)
        ks = jax.random.split(key, 12)
        s = 0.02
        return {'x': jax.random.normal(ks[0], (BATCH, SEQ, EMB), jnp.float32), 'g1': jnp.ones((EMB,), jnp.float32), 'Wq': jax.random.normal(ks[1], (EMB, EMB), jnp.float32) * s, 'Wdkv': jax.random.normal(ks[2], (EMB, LATENT), jnp.float32) * s, 'Wuk': jax.random.normal(ks[3], (LATENT, EMB), jnp.float32) * s, 'Wuv': jax.random.normal(ks[4], (LATENT, EMB), jnp.float32) * s, 'Wo': jax.random.normal(ks[5], (EMB, EMB), jnp.float32) * s, 'g2': jnp.ones((EMB,), jnp.float32), 'gate_w': jax.random.normal(ks[6], (EMB, N_EXP), jnp.float32) * s, 'w1': jax.random.normal(ks[7], (N_EXP, EMB, EXP_DIM), jnp.float32) * s, 'w2': jax.random.normal(ks[8], (N_EXP, EXP_DIM, EMB), jnp.float32) * s}
    _L1_ffn_all = _L1_ffn_setup()
    _L1_ffn_in = {k: v for k, v in _L1_ffn_all.items() if k in ('g1', 'Wq', 'Wdkv', 'Wuk', 'Wuv', 'Wo', 'g2', 'gate_w', 'w1', 'w2')}
    del _L1_ffn_all
    return {'x': x, 'ctx_1024': ctx_1024, 'mask_BxS2_bk0': mask_BxS2_bk0, 'mask_1x1xSxS2_ik0': mask_1x1xSxS2_ik0, 'L0_xattn_ln_x_w': _L0_xattn_in['ln_x_w'], 'L0_xattn_ln_x_b': _L0_xattn_in['ln_x_b'], 'L0_xattn_ln_l_w': _L0_xattn_in['ln_l_w'], 'L0_xattn_ln_l_b': _L0_xattn_in['ln_l_b'], 'L0_xattn_Wq': _L0_xattn_in['Wq'], 'L0_xattn_Wkv': _L0_xattn_in['Wkv'], 'L0_xattn_q_scale': _L0_xattn_in['q_scale'], 'L0_xattn_k_scale': _L0_xattn_in['k_scale'], 'L0_xattn_Wo': _L0_xattn_in['Wo'], 'L0_xattn_ln_o_w': _L0_xattn_in['ln_o_w'], 'L0_xattn_ln_o_b': _L0_xattn_in['ln_o_b'], 'L0_ffn_Wm': _L0_ffn_in['Wm'], 'L0_ffn_Wp': _L0_ffn_in['Wp'], 'L0_ffn_Wc1': _L0_ffn_in['Wc1'], 'L0_ffn_Wc2': _L0_ffn_in['Wc2'], 'L1_xattn_w_q': _L1_xattn_in['w_q'], 'L1_xattn_w_k': _L1_xattn_in['w_k'], 'L1_xattn_w_v': _L1_xattn_in['w_v'], 'L1_xattn_w_o': _L1_xattn_in['w_o'], 'L1_ffn_g1': _L1_ffn_in['g1'], 'L1_ffn_Wq': _L1_ffn_in['Wq'], 'L1_ffn_Wdkv': _L1_ffn_in['Wdkv'], 'L1_ffn_Wuk': _L1_ffn_in['Wuk'], 'L1_ffn_Wuv': _L1_ffn_in['Wuv'], 'L1_ffn_Wo': _L1_ffn_in['Wo'], 'L1_ffn_g2': _L1_ffn_in['g2'], 'L1_ffn_gate_w': _L1_ffn_in['gate_w'], 'L1_ffn_w1': _L1_ffn_in['w1'], 'L1_ffn_w2': _L1_ffn_in['w2']}

def reference(x, ctx_1024, mask_BxS2_bk0, mask_1x1xSxS2_ik0, L0_xattn_ln_x_w, L0_xattn_ln_x_b, L0_xattn_ln_l_w, L0_xattn_ln_l_b, L0_xattn_Wq, L0_xattn_Wkv, L0_xattn_q_scale, L0_xattn_k_scale, L0_xattn_Wo, L0_xattn_ln_o_w, L0_xattn_ln_o_b, L0_ffn_Wm, L0_ffn_Wp, L0_ffn_Wc1, L0_ffn_Wc2, L1_xattn_w_q, L1_xattn_w_k, L1_xattn_w_v, L1_xattn_w_o, L1_ffn_g1, L1_ffn_Wq, L1_ffn_Wdkv, L1_ffn_Wuk, L1_ffn_Wuv, L1_ffn_Wo, L1_ffn_g2, L1_ffn_gate_w, L1_ffn_w1, L1_ffn_w2):
    import jax
    import jax.numpy as jnp

    def _L0_xattn_ref(x, latents, mask, ln_x_w, ln_x_b, ln_l_w, ln_l_b, Wq, Wkv, q_scale, k_scale, Wo, ln_o_w, ln_o_b):
        import jax, jax.numpy as jnp
        import numpy as np
        DIM, DIM_HEAD, HEADS, SCALE = (128, 64, 8, 8.0)
        INNER = DIM_HEAD * HEADS
        LN_EPS = 1e-05
        L2_EPS = 1e-12

        def layer_norm(x, w, b):
            mu = jnp.mean(x, axis=-1, keepdims=True)
            var = jnp.mean(jnp.square(x - mu), axis=-1, keepdims=True)
            return (x - mu) * jax.lax.rsqrt(var + LN_EPS) * w + b

        def l2norm(t):
            n = jnp.sqrt(jnp.sum(jnp.square(t), axis=-1, keepdims=True))
            return t / jnp.maximum(n, L2_EPS)
        b, n, _ = x.shape
        m = latents.shape[1]
        x = layer_norm(x, ln_x_w, ln_x_b)
        latents = layer_norm(latents, ln_l_w, ln_l_b)
        q = latents @ Wq
        kv_input = jnp.concatenate([x, latents], axis=1)
        kv = kv_input @ Wkv
        k, v = jnp.split(kv, 2, axis=-1)

        def to_heads(t):
            return t.reshape(t.shape[0], t.shape[1], HEADS, DIM_HEAD).transpose(0, 2, 1, 3)
        q, k, v = map(to_heads, (q, k, v))
        q = l2norm(q) * q_scale
        k = l2norm(k) * k_scale
        sim = jnp.einsum('bhid,bhjd->bhij', q, k) * SCALE
        full_mask = jnp.concatenate([mask, jnp.ones((b, m), dtype=bool)], axis=1)[:, None, None, :]
        max_neg = -jnp.finfo(sim.dtype).max
        sim = jnp.where(full_mask, sim, max_neg)
        attn = jax.nn.softmax(sim.astype(jnp.float32), axis=-1).astype(sim.dtype)
        out = jnp.einsum('bhij,bhjd->bhid', attn, v)
        out = out.transpose(0, 2, 1, 3).reshape(b, m, INNER)
        return layer_norm(out @ Wo, ln_o_w, ln_o_b)

    def _L0_ffn_ref(x, Wm, Wp, Wc1, Wc2):
        import jax, jax.numpy as jnp
        import numpy as np
        N_EMBD = 128
        ITER_SIZE = 4 * N_EMBD
        FULL_SIZE = 3 * ITER_SIZE
        R = 0.7

        def _topk_mask(ck, k):
            probs = jax.nn.softmax(ck, axis=-1)
            _, idx = jax.lax.top_k(probs, k)
            b = jnp.arange(probs.shape[0])[:, None]
            return jnp.zeros_like(probs).at[b, idx].set(1.0)

        def _forward(x, Wm, Wp, Wc1, Wc2):
            B = x.shape[0]
            base = jnp.zeros((B, FULL_SIZE), x.dtype).at[:, :ITER_SIZE].set(1.0)

            def step(carry, _):
                xc, active, history, done = carry
                h = jnp.einsum('btc,fc->btf', xc, Wm) * active[:, None, :]
                h = jax.nn.relu(h)
                x_new = jnp.einsum('btf,cf->btc', h, Wp)
                pooled = x_new.mean(axis=1)
                ck = jnp.einsum('bd,fd->bf', jax.nn.relu(jnp.einsum('bc,dc->bd', pooled, Wc1)), Wc2)
                new_mask = _topk_mask(ck, ITER_SIZE)
                combined = jnp.clip(history + new_mask, 0.0, 1.0)
                novelty = (combined - history).sum(axis=1).mean() / ITER_SIZE
                done_next = jnp.logical_or(done, novelty < R)
                x_out = jnp.where(done, xc, x_new)
                active_out = jnp.where(done, active, new_mask)
                history_out = jnp.where(done, history, combined)
                return ((x_out, active_out, history_out, done_next), None)
            init = (x, base, base, jnp.array(False))
            (x_fin, _, _, _), _ = jax.lax.scan(step, init, None, length=3)
            return x_fin
        return _forward(x, Wm, Wp, Wc1, Wc2)

    def _L1_xattn_ref(q, k, v, mask, w_q, w_k, w_v, w_o):
        import jax, jax.numpy as jnp
        import numpy as np
        D_MODEL = 128
        H = 16
        D_K = D_MODEL // H
        MASK_VALUE = -2000000000.0
        B, S, _ = q.shape

        def proj(x, w):
            y = jnp.einsum('bsd,ed->bse', x, w)
            return y.reshape(B, -1, H, D_K).transpose(0, 2, 1, 3)
        Q = proj(q, w_q)
        K = proj(k, w_k)
        V = proj(v, w_v)
        scores = jnp.einsum('bhsd,bhtd->bhst', Q, K) * D_K ** (-0.5)
        scores = jnp.where(mask == 0, MASK_VALUE, scores)
        attn = jax.nn.softmax(scores, axis=-1)
        x = jnp.einsum('bhst,bhtd->bhsd', attn, V)
        x = x.transpose(0, 2, 1, 3).reshape(B, -1, D_MODEL)
        return jnp.einsum('bsd,ed->bse', x, w_o)

    def _L1_ffn_ref(x, g1, Wq, Wdkv, Wuk, Wuv, Wo, g2, gate_w, w1, w2):
        import jax, jax.numpy as jnp
        import numpy as np
        EMB = 128
        HEADS = 16
        SEQ = 256
        LATENT = 64
        N_EXP = 8
        TOP_K = 2
        EXP_DIM = 256
        BATCH = 2
        EPS = 1e-06

        def _rmsnorm(x, g):
            return x * jax.lax.rsqrt(jnp.mean(x * x, axis=-1, keepdims=True) + EPS) * g

        def _mla(h, Wq, Wdkv, Wuk, Wuv, Wo):
            B, S, D = h.shape
            hd = D // HEADS
            q = (h @ Wq).reshape(B, S, HEADS, hd)
            c = h @ Wdkv
            k = (c @ Wuk).reshape(B, S, HEADS, hd)
            v = (c @ Wuv).reshape(B, S, HEADS, hd)
            scores = jnp.einsum('bqhd,bkhd->bhqk', q, k) / jnp.sqrt(jnp.asarray(hd, h.dtype))
            causal = jnp.tril(jnp.ones((S, S), bool))
            scores = jnp.where(causal, scores, jnp.asarray(-1000000000.0, h.dtype))
            a = jax.nn.softmax(scores, axis=-1)
            out = jnp.einsum('bhqk,bkhd->bqhd', a, v).reshape(B, S, D)
            return out @ Wo

        def _moe(h, gate_w, w1, w2):
            B, S, D = h.shape
            t = h.reshape(B * S, D)
            logits = t @ gate_w
            top_v, top_i = jax.lax.top_k(logits, TOP_K)
            gates = jax.nn.softmax(top_v, axis=-1)
            T = t.shape[0]
            combine = jnp.zeros((T, N_EXP), t.dtype).at[jnp.arange(T)[:, None], top_i].add(gates)
            hid = jax.nn.silu(jnp.einsum('td,edh->teh', t, w1))
            ye = jnp.einsum('teh,ehd->ted', hid, w2)
            out = jnp.einsum('te,ted->td', combine, ye)
            return out.reshape(B, S, D)
        x = x + _mla(_rmsnorm(x, g1), Wq, Wdkv, Wuk, Wuv, Wo)
        x = x + _moe(_rmsnorm(x, g2), gate_w, w1, w2)
        return x
    x = x + _L0_xattn_ref(ctx_1024, _layernorm(x, axis=-1), mask_BxS2_bk0, L0_xattn_ln_x_w, L0_xattn_ln_x_b, L0_xattn_ln_l_w, L0_xattn_ln_l_b, L0_xattn_Wq, L0_xattn_Wkv, L0_xattn_q_scale, L0_xattn_k_scale, L0_xattn_Wo, L0_xattn_ln_o_w, L0_xattn_ln_o_b)
    x = x + _L0_ffn_ref(_layernorm(x, axis=-1), L0_ffn_Wm, L0_ffn_Wp, L0_ffn_Wc1, L0_ffn_Wc2)
    x = x + _L1_xattn_ref(_layernorm(x, axis=-1), ctx_1024, ctx_1024, mask_1x1xSxS2_ik0, L1_xattn_w_q, L1_xattn_w_k, L1_xattn_w_v, L1_xattn_w_o)
    x = x + _L1_ffn_ref(_layernorm(x, axis=-1), L1_ffn_g1, L1_ffn_Wq, L1_ffn_Wdkv, L1_ffn_Wuk, L1_ffn_Wuv, L1_ffn_Wo, L1_ffn_g2, L1_ffn_gate_w, L1_ffn_w1, L1_ffn_w2)
    return x

_drawn_inputs = setup_inputs


def setup_inputs(seed=0):
    import zlib

    import numpy as np

    out = dict(_drawn_inputs(seed))
    spreads = {'L0_xattn_ln_x_w': (1.0, 0.2),
     'L0_xattn_ln_x_b': (0.0, 0.1),
     'L0_xattn_ln_l_w': (1.0, 0.2),
     'L0_xattn_ln_l_b': (0.0, 0.1),
     'L0_xattn_q_scale': (1.0, 0.2),
     'L0_xattn_k_scale': (1.0, 0.2),
     'L0_xattn_ln_o_w': (1.0, 0.2),
     'L0_xattn_ln_o_b': (0.0, 0.1),
     'L1_ffn_g1': (1.0, 0.6),
     'L1_ffn_g2': (1.0, 0.6)}
    factors = {'L1_ffn_Wq': 8.0,
     'L1_ffn_Wdkv': 8.0,
     'L1_ffn_Wuk': 8.0,
     'L1_ffn_Wuv': 8.0,
     'L1_ffn_Wo': 8.0,
     'L1_ffn_gate_w': 6.491,
     'L1_ffn_w1': 5.805,
     'L1_ffn_w2': 5.781}
    for name, (base, spread) in spreads.items():
        noise = np.random.default_rng([zlib.crc32(name.encode()), seed]).standard_normal(out[name].shape)
        drawn = base * np.exp(spread * noise) if base else spread * noise
        out[name] = jnp.asarray(drawn.astype(out[name].dtype))
    for name, factor in factors.items():
        out[name] = (out[name] * factor).astype(out[name].dtype)
    return out
```

```python
from contextlib import ExitStack, contextmanager

import concourse.bass as bass
from concourse import mybir

ALU = mybir.AluOpType
ACT = mybir.ActivationFunctionType
AX = mybir.AxisListType
F32 = mybir.dt.float32
BF16 = mybir.dt.bfloat16
I32 = mybir.dt.int32
U32 = mybir.dt.uint32
U8 = mybir.dt.uint8

P = 128
B = 32
D = 128
C = 120
GB = 4
NG = B // GB
LN_EPS = 1e-5
RMS_EPS = 1e-6
F_ITER = 512
F_FULL = 3 * F_ITER
Q4 = F_FULL // 4
NEG_MAX = -3.0e38


def wait(eng, sem, value):
    if isinstance(value, int) and value <= 0:
        return
    eng.wait_ge(sem, value)


@contextmanager
def signals(nc, phase):
    given = []

    def sem(name):
        given.append(nc.alloc_semaphore(f"{phase}_{name}"))
        return given[-1]

    yield sem
    nc.clear_and_free_semaphores(given)
    nc.all_engine_barrier()


def mega_kernel(nc, x_in, ctx_in, ctxT_in, keep_in, qk_mask_in, cols_in, lnow_in, lnob_in, wq0_in, wkv0_in, wo0_in,
                wm_in, wp_in, wc1_in, wc2_in, wq1_in, wk1_in, wv1_in, wo1_in, wq2_in, wdkv_in, wuk_in, wuv_in,
                wo2_in, gate_in, w1_in, w2_in, out, stop_after=9):
    ctx = ExitStack()
    with ctx:
        def sb(name, shape, dt=F32, stack=ctx):
            return stack.enter_context(nc.sbuf_tensor(name, shape, dt))

        X = sb("X", [P, B, D])
        X2 = sb("X2", [P, B, D])
        X3 = sb("X3", [P, B, D])
        stats6 = sb("stats6", [P, B, 6])
        mean = sb("mean", [P, B])
        rstd = sb("rstd", [P, B])
        rms = sb("rms", [P, B])
        mhalf = sb("mhalf", [P, B])
        small = sb("small", [P, 4, B])
        ident = sb("ident", [P, P])
        ident_bf = sb("ident_bf", [P, P], BF16)
        ones = sb("ones", [P, P])
        ones_bf = sb("ones_bf", [P, P], BF16)
        cols = sb("cols", [P, 8])
        LNX_W, LNX_B, LNL_W, LNL_B, QS, KS, G1, G2 = (cols[:, i:i + 1] for i in range(8))
        psum = ctx.enter_context(nc.psum_tensor("psum", [P, 8, 512], F32))

        load_x_and_constants(nc, sb, X, x_in, cols, cols_in, ident, ident_bf, ones, ones_bf, mhalf, stats6)
        if stop_after >= 1:
            l0_attention(nc, psum, X, stats6, mean, rstd, mhalf, small, ident, ident_bf, ones, ones_bf, cols,
                         ctx_in, keep_in, lnow_in, lnob_in, wq0_in, wkv0_in, wo0_in)
        last = X
        if stop_after >= 2:
            l0_ffn(nc, psum, X, X2, X3, stats6, mean, rstd, mhalf, small, ident, ones, wm_in, wp_in, wc1_in, wc2_in)
            last = X2
        if stop_after >= 3:
            attention16(nc, "l1", psum, X2, X2, stats6, mean, rstd, rms, mhalf, small, ident, ident_bf, ones, cols,
                        (wq1_in, wk1_in, wv1_in, wo1_in), ctxT_in, qk_mask_in)
        if stop_after >= 4:
            attention16(nc, "mla", psum, X2, X3, stats6, mean, rstd, rms, mhalf, small, ident, ident_bf, ones, cols,
                        (wq2_in, wdkv_in, wuk_in, wuv_in, wo2_in), None, None)
            last = X3
        if stop_after >= 5:
            moe(nc, psum, X2, X3, stats6, mean, rms, mhalf, small, ident, cols, gate_in, w1_in, w2_in, out)
        else:
            with nc.semaphore("dump") as dump, nc.Block() as block:
                @block.sync
                def _(sp):
                    sp.dma_start(out.rearrange("b t d -> t b d"), last[:, :, :]).then_inc(dump, 16)
                    sp.wait_ge(dump, 16)


def load_x_and_constants(nc, sb, X, x_in, cols, cols_in, ident, ident_bf, ones, ones_bf, mhalf, stats6):
    with ExitStack() as sems, ExitStack() as st:
        sem = sems.enter_context(signals(nc, "load"))
        x_loaded = [sem(f"x_loaded{g}") for g in range(NG)]
        cols_loaded = sem("cols_loaded")
        zeroed = sem("zeroed")
        identity_made = sem("identity_made")
        block = st.enter_context(nc.Block())
        x_view = x_in.rearrange("b t d -> t b d")

        @block.sync
        def _(sp):
            for g in range(NG):
                sp.dma_start(X[:, g * GB:(g + 1) * GB, :], x_view[:, g * GB:(g + 1) * GB, :]).then_inc(x_loaded[g], 16)
            sp.dma_start(cols[:, :], cols_in).then_inc(cols_loaded, 16)
            sp.wait_ge(cols_loaded, 16)

        @block.gpsimd
        def _(pool):
            pool.memset(ident[:, :], 0.0).then_inc(zeroed, 1)
            pool.memset(ident_bf[:, :], 0.0).then_inc(zeroed, 1)
            pool.memset(ones[:, :], 1.0)
            pool.memset(ones_bf[:, :], 1.0)
            pool.memset(mhalf[:, :], -0.5)
            pool.wait_ge(zeroed, 2)
            for m in (ident, ident_bf):
                pool.affine_select(out=m[:, :], in_=m[:, :], compare_op=ALU.not_equal, fill=1.0, base=0,
                                   pattern=[[-1, P]], channel_multiplier=1).then_inc(identity_made, 1)
            pool.wait_ge(identity_made, 2)

        @block.vector
        def _(dve):
            for g in range(NG):
                dve.wait_ge(x_loaded[g], 16)
                for b in range(g * GB, (g + 1) * GB):
                    dve.bn_stats(stats6[:, b, :], X[:, b, :])



def softmax_units(nc, st, new_sem, psum, H, K, width, pt_plan, pv_plan, score, E, ident, ident_bf, ones, tag):
    def sem(name):
        return [new_sem(f"{name}{u}") for u in range(2)]

    def sb(name, shape, dt=F32):
        return st.enter_context(nc.sbuf_tensor(f"{tag}_{name}", shape, dt))

    HB = H // 2
    n_max = [sb(f"n_max{u}", [P, H]) for u in range(2)]
    n_max_parts = [sb(f"n_max_parts{u}", [P, 2, H], BF16) for u in range(2)]
    max_rows = [sb(f"max_rows{u}", [2 * H, P], BF16) for u in range(2)]
    probs = [sb(f"probs{u}", [P, H, K]) for u in range(2)]
    probsT = [sb(f"probsT{u}", [P, 2, 4, P]) for u in range(2)]
    r_sum = sb("r_sum", [P, 2, P])
    outT = sb("outT", [P, 4, P])

    scored = sem("scored")
    max_taken = sem("max_taken")
    max_hi = sem("max_hi")
    max_split = sem("max_split")
    max_turned = sem("max_turned")
    max_copied = sem("max_copied")
    max_subtracted = sem("max_subtracted")
    exp_done = sem("exp_done")
    pt0_turned = sem("pt0_turned")
    pt1_turned = sem("pt1_turned")
    pt0_copied = sem("pt0_copied")
    pt1_copied = sem("pt1_copied")
    pv_done = sem("pv_done")
    sum_inverted = sem("sum_inverted")
    out_scaled = sem("out_scaled")
    projected = new_sem("projected")
    projection_taken = new_sem("projection_taken")

    def banks(u):
        return psum[:, 2 * u:2 * u + 2, 0:HB * K].rearrange("p c (j k) -> p c j k", k=K)

    def pe_scores(pe, n, u):
        wait(pe, exp_done[u], n)
        score(pe, n, u).then_inc(scored[u], 1)

    def dve_max(dve, n, u):
        wait(dve, scored[u], n + 1)
        dve.tensor_reduce(n_max[u][:, :].rearrange("p (c j) -> p c j", c=2), banks(u), AX.X, ALU.max,
                          negate=True).then_inc(max_taken[u], 1)
        wait(dve, max_taken[u], n + 1)
        wait(dve, max_turned[u], n)
        dve.tensor_copy(n_max_parts[u][:, 0, :], n_max[u][:, :]).then_inc(max_hi[u], 1)
        wait(dve, max_hi[u], n + 1)
        dve.tensor_tensor(n_max_parts[u][:, 1, :], n_max[u][:, :], n_max_parts[u][:, 0, :],
                          ALU.subtract).then_inc(max_split[u], 1)

    def pe_turn_max(pe, n, u):
        wait(pe, max_split[u], n + 1)
        wait(pe, pt0_copied[1 - u], n if u == 0 else n + 1)
        bank4 = psum[:, 4, 0:P // 2].bitcast(BF16)
        pe.transpose(bank4[0:2 * H, :], n_max_parts[u][:, :, :].rearrange("p a h -> p (a h)"),
                     ident_bf[:, :]).then_inc(max_turned[u], 1)

    def act_copy_max(act, n, u):
        wait(act, max_turned[u], n + 1)
        wait(act, max_subtracted[u], n)
        act.copy(max_rows[u][:, :], psum[:, 4, 0:P // 2].bitcast(BF16)[0:2 * H, :]).then_inc(max_copied[u], 1)

    def pe_subtract_max(pe, n, u):
        wait(pe, max_copied[u], n + 1)
        for c in range(2):
            mm = pe.matmul(psum[:, 2 * u + c, 0:HB * K], max_rows[u][:, :],
                           E[:, HB * c:HB * (c + 1), :].rearrange("r h k -> r (h k)"), start=False, stop=True, skip_group_check=True)
        mm.then_inc(max_subtracted[u], 1)

    def act_exp(act, n, u):
        wait(act, max_subtracted[u], n + 1)
        wait(act, pt1_turned[u], n)
        act.activation(probs[u][:, :, :].rearrange("p (c j) k -> p c j k", c=2), banks(u), ACT.Exp).then_inc(exp_done[u], 1)

    def pe_turn_probs(pe, n, u):
        wait(pe, exp_done[u], n + 1)
        wait(pe, max_copied[u], n + 1)
        for j, (h, k0, kn) in enumerate(pt_plan[0]):
            t = pe.transpose(psum[0:kn, 4, j * P:(j + 1) * P], probs[u][:, h, k0:k0 + kn], ident[:, :])
        t.then_inc(pt0_turned[u], 1)
        if u == 0:
            wait(pe, projection_taken, n)
        else:
            wait(pe, out_scaled[0], n + 1)
        for j, (h, k0, kn) in enumerate(pt_plan[1]):
            t = pe.transpose(psum[0:kn, 5, j * P:(j + 1) * P], probs[u][:, h, k0:k0 + kn], ident[:, :])
        t.then_inc(pt1_turned[u], 1)

    KN = [pt_plan[0][0][2], pt_plan[1][0][2]]

    def act_copy_pt0(act, n, u):
        wait(act, pt0_turned[u], n + 1)
        wait(act, pv_done[u], n)
        act.copy(probsT[u][0:KN[0], 0, :, :], psum[0:KN[0], 4, :].rearrange("k (j q) -> k j q", j=4)).then_inc(pt0_copied[u], 1)

    def dve_copy_pt1(dve, n, u):
        wait(dve, pt1_turned[u], n + 1)
        wait(dve, pv_done[u], n)
        dve.tensor_copy(probsT[u][0:KN[1], 1, :, :], psum[0:KN[1], 5, :].rearrange("k (j q) -> k j q", j=4)).then_inc(pt1_copied[u], 1)

    def pe_pv(pe, n, u, v_of):
        wait(pe, pt0_copied[u], n + 1)
        wait(pe, pt1_copied[u], n + 1)
        for j, row, blk, parts in pv_plan:
            for base, values in ((0, True), (256, False)):
                o = psum[row:row + width, 5, base + blk * P:base + (blk + 1) * P]
                for i, (c, slot, kn) in enumerate(parts):
                    lhs = v_of(u * H + j, i) if values else ones[0:kn, 0:width]
                    mm = pe.matmul(o, lhs, probsT[u][0:kn, c, slot, :], start=(i == 0), stop=(i == len(parts) - 1),
                                   skip_group_check=True)
        mm.then_inc(pv_done[u], 1)

    def dve_scale(dve, n, u):
        wait(dve, pv_done[u], n + 1)
        wait(dve, out_scaled[1 - u], n if u == 0 else n + 1)
        dve.reciprocal(r_sum[:, :, :], psum[:, 5, 256:512].rearrange("p (b q) -> p b q", b=2)).then_inc(sum_inverted[u], 1)
        wait(dve, sum_inverted[u], n + 1)
        if u == 0:
            wait(dve, projected, n)
        dve.tensor_tensor(outT[:, 2 * u:2 * u + 2, :], psum[:, 5, 0:256].rearrange("p (b q) -> p b q", b=2), r_sum[:, :, :],
                          ALU.mult).then_inc(out_scaled[u], 1)

    def pe_project(pe, n, wo):
        wait(pe, out_scaled[1], n + 1)
        for c in range(4):
            mm = pe.matmul(psum[:, 5, 0:D], outT[:, c, :], wo[:, c, :], start=(c == 0), stop=(c == 3))
        mm.then_inc(projected, 1)

    return dict(locals())


def l0_attention(nc, psum, X, stats6, mean, rstd, mhalf, small, ident, ident_bf, ones, ones_bf, cols,
                 ctx_in, keep_in, lnow_in, lnob_in, wq_in, wkv_in, wo_in):
    H, HD = 8, 64
    K = C + P
    INNER = H * HD
    LNX_W, LNX_B, LNL_W, LNL_B, QS, KS = (cols[:, i:i + 1] for i in range(6))
    with ExitStack() as sems, ExitStack() as st:
        def sb(name, shape, dt=F32):
            return st.enter_context(nc.sbuf_tensor(name, shape, dt))

        sem = sems.enter_context(signals(nc, "l0"))
        CT = sb("CT", [P, B, D])
        keep8 = sb("keep8", [1, B * C], U8)
        keep_row = sb("keep_row", [P, B, K], BF16)
        stats6_c = sb("stats6_c", [P, B, 6])
        mean_c = sb("mean_c", [P, B])
        small_c = sb("small_c", [P, 4, B])
        rstd_c = sb("rstd_c", [P, B])
        wq = sb("wq", [D, INNER])
        wkv = sb("wkv", [D, 2 * INNER])
        wo = sb("wo", [P, 4, D])
        lnow = sb("lnow", [P, D])
        lnob = sb("lnob", [P, D])
        qk_scale = sb("qk_scale", [P, 1])
        first_row = sb("first_row", [P, P], BF16)
        E = sb("E", [8, 4, K], BF16)

        loaded = sem("l0_loaded")
        keep_loaded = sem("keep_loaded")
        c_loaded = [sem(f"c_loaded{g}") for g in range(NG)]
        const_step = sem("const_step")
        e_made = sem("e_made")
        c_stats = sem("c_stats")
        x_moments_step = sem("x_moments_step")
        c_moments_step = sem("c_moments_step")
        var_ready = sem("var_ready")
        pow_done = sem("pow_done")
        scale_done = sem("scale_done")
        with nc.Block() as block:
            @block.sync
            def _(sp):
                c_view = ctx_in.rearrange("b t d -> t b d")
                for g in range(NG):
                    sp.dma_start(CT[0:C, g * GB:(g + 1) * GB, :], c_view[:, g * GB:(g + 1) * GB, :]).then_inc(c_loaded[g], 16)
                sp.dma_start(keep8[:, :], keep_in).then_inc(keep_loaded, 16)
                sp.dma_start(wq[:, :], wq_in).then_inc(loaded, 16)
                sp.dma_start(wkv[:, :], wkv_in).then_inc(loaded, 16)
                sp.dma_start(wo[:, :, :], wo_in.rearrange("(c p) d -> p c d", p=P)).then_inc(loaded, 16)
                sp.dma_start(lnow[:, :], lnow_in.broadcast_to([P, D])).then_inc(loaded, 16)
                sp.dma_start(lnob[:, :], lnob_in.broadcast_to([P, D])).then_inc(loaded, 16)
                sp.wait_ge(loaded, 80)

            @block.gpsimd
            def _(pool):
                pool.memset(E[:, :, :], 0.0).then_inc(e_made, 1)
                pool.memset(first_row[:, :], 0.0).then_inc(e_made, 1)
                for part in range(2):
                    pool.wait_ge(e_made, part + (2 if part else 1))
                    pool.affine_select(out=E[:, :, :], in_=E[:, :, :], compare_op=ALU.not_equal, fill=1.0,
                                       base=-4 * part, pattern=[[-1, 4], [0, K]], channel_multiplier=1).then_inc(e_made, 1)
                pool.memset(first_row[0:1, :], 1.0)
                pool.wait_ge(var_ready, 2)
                pool.tensor_tensor(rstd[:, :], small[:, 0, :], mhalf[:, :], ALU.pow).then_inc(pow_done, 1)
                pool.tensor_tensor(rstd_c[0:C, :], small_c[0:C, 0, :], mhalf[0:C, :], ALU.pow).then_inc(pow_done, 1)
                pool.wait_ge(var_ready, 5)
                pool.tensor_tensor(small[:, 1, :], small[:, 2, :], mhalf[:, :], ALU.pow).then_inc(pow_done, 1)

            @block.vector
            def _(dve):
                dve.memset(keep_row[:, :, :].bitcast(U32), 0).then_inc(const_step, 1)
                for g in range(NG):
                    dve.wait_ge(c_loaded[g], 16)
                    for b in range(g * GB, (g + 1) * GB):
                        dve.bn_stats(stats6_c[0:C, b, :], CT[0:C, b, :]).then_inc(c_stats, 1)
                moments(dve, stats6, mean, small, x_moments_step)
                dve.wait_ge(c_stats, B)
                moments(dve, stats6_c[0:C], mean_c[0:C], small_c[0:C], c_moments_step)
                dve.tensor_scalar(small[:, 0, :], small[:, 3, :], LN_EPS, None, ALU.add).then_inc(var_ready, 1)
                dve.tensor_scalar(small_c[0:C, 0, :], small_c[0:C, 3, :], LN_EPS, None, ALU.add).then_inc(var_ready, 1)
                dve.wait_ge(keep_loaded, 16)
                dve.wait_ge(const_step, 1)
                dve.tensor_scalar(keep_row[0:1, :, 0:C], keep8[:, :].rearrange("a (b c) -> a b c", b=B), 1.0, -NEG_MAX,
                                  ALU.subtract, ALU.mult)
                dve.tensor_scalar(qk_scale[:, :], QS, KS, float(HD) ** 0.5, ALU.mult, ALU.mult).then_inc(const_step, 1)
                dve.wait_ge(pow_done, 2)
                dve.tensor_tensor(small[:, 2, :], rstd[:, :], rstd[:, :], ALU.mult).then_inc(var_ready, 1)
                dve.wait_ge(var_ready, 3)
                dve.tensor_tensor(small[:, 2, :], small[:, 2, :], small[:, 3, :], ALU.mult).then_inc(var_ready, 1)
                dve.wait_ge(var_ready, 4)
                dve.tensor_scalar(small[:, 2, :], small[:, 2, :], LN_EPS, None, ALU.add).then_inc(var_ready, 1)
                dve.wait_ge(pow_done, 3)
                dve.tensor_tensor(rstd[:, :], rstd[:, :], small[:, 1, :], ALU.mult).then_inc(scale_done, 1)

        ln_x = sb("ln_x", [P, D])
        ln_c = sb("ln_c", [P, D])
        kvT = sb("kvT", [P, K])
        qk = sb("qk", [P, 3, INNER])
        sq = sb("sq", [P, 3, INNER])
        qkn = sb("qkn", [P, 3, INNER])
        ss = sb("ss", [P, 3 * H])
        ssm = sb("ssm", [P, 3 * H])
        r_norm = sb("r_norm", [P, 3 * H])
        QZ = [sb(f"QZ{i}", [P, H, P]) for i in range(2)]
        KT = [sb(f"KT{i}", [P, 4, K]) for i in range(2)]
        VC = [sb(f"VC{i}", [P, INNER]) for i in range(2)]
        VL = [sb(f"VL{i}", [P, INNER]) for i in range(2)]
        y = sb("y", [P, D])
        y_stat = sb("y_stat", [P, 6])
        y_sums = sb("y_sums", [P, 2])
        y_diff = sb("y_diff", [P, 1])
        y_mean = sb("y_mean", [P, 1])
        y_within = sb("y_within", [P, 1])
        y_between = sb("y_between", [P, 1])
        y_var = sb("y_var", [P, 1])
        y_rstd = sb("y_rstd", [P, 1])
        y_norm = sb("y_norm", [P, D])
        y_w = sb("y_w", [P, D])
        y_wb = sb("y_wb", [P, D])

        names = ("ln_made ln_turned kvT_made q_proj q_copied kc_proj kc_copied kl_proj kl_copied vc_proj vc_copied "
                 "vl_proj vl_copied ss_summed ss_ready norm_inverted normed qT_turned qT_copied kcT_turned kcT_copied "
                 "klT_turned klT_copied y_stats y_aggr y_parts y_var_ready y_inverted y_normed y_weighted y_biased x_added "
                 "x_stats buffers_zeroed").split()
        s = {name: sem(name) for name in names}
        cell = {}

        def score(pe, n, u):
            par = cell["par"]
            wait(pe, s["qT_copied"], n + 1)
            wait(pe, s["kcT_copied"], n + 1)
            wait(pe, s["klT_copied"], n + 1)
            for c in range(2):
                pe.matmul(psum[:, 2 * u + c, 0:2 * K], first_row[:, :], keep_row[:, entries(n), :].broadcast_to([P, 2, K]),
                          start=True, stop=False, skip_group_check=True)
                for j in range(2):
                    h = 4 * u + 2 * c + j
                    mm = pe.matmul(psum[:, 2 * u + c, j * K:(j + 1) * K], QZ[par][:, h, :], KT[par][:, h // 2, :],
                                   start=False, stop=True, skip_group_check=True)
            return mm

        pt_plan = ([(j, 0, C) for j in range(4)], [(j, C, P) for j in range(4)])
        pv_plan = [(j, HD * (j % 2), j // 2, [(0, j, C), (1, j, P)]) for j in range(4)]
        t = softmax_units(nc, st, sem, psum, 4, K, HD, pt_plan, pv_plan, score, E, ident, ident_bf, ones, "l0")

        with nc.Block() as block:
            @block.tensor
            def _(pe):
                def prepare_a(m):
                    wait(pe, s["ln_made"], m + 1)
                    wait(pe, s["klT_copied"], m)
                    pe.transpose(psum[:, 6, 0:C], ln_c[0:C, :], ident[0:C, 0:C])
                    pe.transpose(psum[:, 6, P:2 * P], ln_x[:, :], ident[:, :]).then_inc(s["ln_turned"], 1)
                    wait(pe, s["kvT_made"], m + 1)
                    wait(pe, s["kcT_copied"], m)
                    pe.matmul(psum[:, 7, :], kvT[:, C:K], wq[:, :], start=True, stop=True).then_inc(s["q_proj"], 1)
                    pe.matmul(psum[0:C, 6, :], kvT[:, 0:C], wkv[:, 0:INNER], start=True, stop=True).then_inc(s["kc_proj"], 1)
                    wait(pe, s["q_copied"], m + 1)
                    pe.matmul(psum[:, 7, :], kvT[:, C:K], wkv[:, 0:INNER], start=True, stop=True).then_inc(s["kl_proj"], 1)
                    wait(pe, s["kc_copied"], m + 1)
                    pe.matmul(psum[0:C, 6, :], kvT[:, 0:C], wkv[:, INNER:], start=True, stop=True).then_inc(s["vc_proj"], 1)
                    wait(pe, s["kl_copied"], m + 1)
                    pe.matmul(psum[:, 7, :], kvT[:, C:K], wkv[:, INNER:], start=True, stop=True).then_inc(s["vl_proj"], 1)

                def prepare_b(m):
                    wait(pe, s["normed"], m + 1)
                    wait(pe, s["vc_copied"], m + 1)
                    for c in range(4):
                        tr = pe.transpose(psum[:, 6, c * P:(c + 1) * P], qkn[:, 0, c * P:(c + 1) * P], ident[:, :])
                    tr.then_inc(s["qT_turned"], 1)
                    wait(pe, s["vl_copied"], m + 1)
                    for c in range(4):
                        tr = pe.transpose(psum[:, 7, c * C:(c + 1) * C], qkn[0:C, 1, c * P:(c + 1) * P], ident[0:C, 0:C])
                    tr.then_inc(s["kcT_turned"], 1)
                    wait(pe, s["qT_copied"], m + 1)
                    for c in range(4):
                        tr = pe.transpose(psum[:, 6, c * P:(c + 1) * P], qkn[:, 2, c * P:(c + 1) * P], ident[:, :])
                    tr.then_inc(s["klT_turned"], 1)

                def pv(n, u, par):
                    t["pe_pv"](pe, n, u, lambda h, i: (VC[par][0:C, h * HD:(h + 1) * HD], VL[par][:, h * HD:(h + 1) * HD])[i])

                def body(n, par, final=False, first=False):
                    cell["par"] = par
                    t["pe_scores"](pe, n, 1)
                    t["pe_turn_max"](pe, n, 0)
                    if not first:
                        pv(n - 1, 1, 1 - par)
                    t["pe_subtract_max"](pe, n, 0)
                    if not final:
                        prepare_a(n + 1)
                    if not first:
                        t["pe_project"](pe, n - 1, wo)
                    t["pe_turn_probs"](pe, n, 0)
                    t["pe_turn_max"](pe, n, 1)
                    pv(n, 0, par)
                    t["pe_subtract_max"](pe, n, 1)
                    if not final:
                        prepare_b(n + 1)
                    t["pe_turn_probs"](pe, n, 1)
                    if not final:
                        cell["par"] = 1 - par
                        t["pe_scores"](pe, n + 1, 0)

                prepare_a(0)
                wait(pe, s["buffers_zeroed"], 2)
                prepare_b(0)
                cell["par"] = 0
                t["pe_scores"](pe, 0, 0)
                body(0, 0, first=True)
                with pe.Fori(0, B // 2 - 1) as i:
                    body(2 * i + 1, 1)
                    body(2 * i + 2, 0)
                body(B - 1, 1, final=True)
                pv(B - 1, 1, 1)
                t["pe_project"](pe, B - 1, wo)

            @block.scalar
            def _(act):
                def prepare_a(m, par):
                    wait(act, s["ln_turned"], m + 1)
                    wait(act, s["vl_proj"], m)
                    act.activation(kvT[:, 0:C], psum[:, 6, 0:C], ACT.Identity, bias=LNX_B, scale=LNX_W)
                    act.activation(kvT[:, C:K], psum[:, 6, P:2 * P], ACT.Identity, bias=LNL_B,
                                   scale=LNL_W).then_inc(s["kvT_made"], 1)
                    wait(act, s["normed"], m)
                    wait(act, s["ss_summed"], m)
                    for i, (proj, copied, bank, rows) in enumerate((("q_proj", "q_copied", 7, P), ("kc_proj", "kc_copied", 6, C),
                                                                    ("kl_proj", "kl_copied", 7, P))):
                        wait(act, s[proj], m + 1)
                        act.copy(qk[0:rows, i, :], psum[0:rows, bank, :])
                        act.activation(sq[0:rows, i, :], psum[0:rows, bank, :], ACT.Square).then_inc(s[copied], 1)
                    wait(act, s["vc_proj"], m + 1)
                    wait(act, t["pv_done"][1], m - 1)
                    act.copy(VC[par][0:C, :], psum[0:C, 6, :]).then_inc(s["vc_copied"], 1)
                    wait(act, s["vl_proj"], m + 1)
                    act.copy(VL[par][:, :], psum[:, 7, :]).then_inc(s["vl_copied"], 1)

                def prepare_b(m, par):
                    wait(act, s["qT_turned"], m + 1)
                    wait(act, t["scored"][1], m - 1)
                    for half in range(2):
                        r = slice(64 * half, 64 * half + 64)
                        a = act.activation(QZ[par][r, half:H:2, :], psum[r, 6, :].rearrange("p (c q) -> p c q", c=4),
                                           ACT.Copy, scale=qk_scale[r, :])
                    a.then_inc(s["qT_copied"], 1)

                def take_projection(n):
                    wait(act, t["projected"], n + 1)
                    wait(act, s["y_normed"], n)
                    act.copy(y[:, :], psum[:, 5, 0:D]).then_inc(t["projection_taken"], 1)

                def body(n, par, final=False, first=False):
                    t["act_copy_max"](act, n, 0)
                    t["act_exp"](act, n, 0)
                    if not final:
                        prepare_a(n + 1, 1 - par)
                    if not first:
                        take_projection(n - 1)
                    t["act_copy_pt0"](act, n, 0)
                    t["act_copy_max"](act, n, 1)
                    t["act_exp"](act, n, 1)
                    if not final:
                        prepare_b(n + 1, 1 - par)
                    t["act_copy_pt0"](act, n, 1)

                wait(act, s["buffers_zeroed"], 2)
                prepare_a(0, 0)
                prepare_b(0, 0)
                body(0, 0, first=True)
                with act.Fori(0, B // 2 - 1) as i:
                    body(2 * i + 1, 1)
                    body(2 * i + 2, 0)
                body(B - 1, 1, final=True)
                take_projection(B - 1)

            @block.vector
            def _(dve):
                def norm_inputs(m):
                    wait(dve, s["ln_turned"], m)
                    dve.tensor_scalar(ln_x[:, :], X[:, entries(m), :].rearrange("p a d -> p (a d)"), mean[:, entries(m)], rstd[:, entries(m)],
                                      ALU.subtract, ALU.mult)
                    dve.tensor_scalar(ln_c[0:C, :], CT[0:C, entries(m), :].rearrange("p a d -> p (a d)"), mean_c[0:C, entries(m)],
                                      rstd_c[0:C, entries(m)], ALU.subtract, ALU.mult).then_inc(s["ln_made"], 1)

                def sum_squares(m):
                    wait(dve, s["kl_copied"], m + 1)
                    dve.tensor_reduce(ss[:, :], sq[:, :, :].rearrange("p a (h d) -> p (a h) d", d=HD), AX.X,
                                      ALU.add).then_inc(s["ss_summed"], 1)
                    wait(dve, s["ss_summed"], m + 1)
                    wait(dve, s["norm_inverted"], m)
                    dve.tensor_scalar(ssm[:, :], ss[:, :], 1e-24, None, ALU.max).then_inc(s["ss_ready"], 1)

                def copy_k(m, par):
                    wait(dve, s["kcT_turned"], m + 1)
                    wait(dve, t["scored"][1], m - 1)
                    dve.tensor_copy(KT[par][:, :, 0:C], psum[:, 7, 0:4 * C].rearrange("p (c k) -> p c k", c=4)).then_inc(s["kcT_copied"], 1)
                    wait(dve, s["klT_turned"], m + 1)
                    dve.tensor_copy(KT[par][:, :, C:K], psum[:, 6, :].rearrange("p (c k) -> p c k", c=4)).then_inc(s["klT_copied"], 1)

                def y_moments(n):
                    wait(dve, t["projection_taken"], n + 1)
                    dve.bn_stats(y_stat[:, :], y[:, :]).then_inc(s["y_stats"], 1)
                    wait(dve, s["y_stats"], n + 1)
                    dve.tensor_tensor(y_sums[:, :], y_stat[:, 1:3], y_stat[:, 4:6], ALU.add)
                    dve.tensor_tensor(y_diff[:, :], y_stat[:, 1:2], y_stat[:, 4:5], ALU.subtract).then_inc(s["y_aggr"], 1)
                    wait(dve, s["y_aggr"], n + 1)
                    dve.tensor_scalar(y_mean[:, :], y_sums[:, 0:1], 0.5, None, ALU.mult)
                    dve.tensor_scalar(y_within[:, :], y_sums[:, 1:2], 1.0 / D, LN_EPS, ALU.mult, ALU.add)
                    dve.scalar_tensor_tensor(y_between[:, :], y_diff[:, :], 0.25, y_diff[:, :], ALU.mult,
                                             ALU.mult).then_inc(s["y_parts"], 1)
                    wait(dve, s["y_parts"], n + 1)
                    wait(dve, s["y_inverted"], n)
                    dve.tensor_tensor(y_var[:, :], y_within[:, :], y_between[:, :], ALU.add).then_inc(s["y_var_ready"], 1)

                def y_normalize(n):
                    wait(dve, s["y_inverted"], n + 1)
                    wait(dve, s["y_weighted"], n)
                    dve.tensor_scalar(y_norm[:, :], y[:, :], y_mean[:, :], y_rstd[:, :], ALU.subtract,
                                      ALU.mult).then_inc(s["y_normed"], 1)

                def x_moments(n):
                    wait_apart(dve, s["x_added"], n + 1, s["buffers_zeroed"])
                    dve.bn_stats(stats6[:, entries(n), :].rearrange("p a d -> p (a d)"),
                                 X[:, entries(n), :].rearrange("p a d -> p (a d)")).then_inc(s["x_stats"], 1)

                def body(n, par, final=False, first=False, second=False):
                    t["dve_max"](dve, n, 0)
                    if not first:
                        t["dve_scale"](dve, n - 1, 1)
                    if not final:
                        norm_inputs(n + 1)
                        sum_squares(n + 1)
                    if not first:
                        y_moments(n - 1)
                    t["dve_copy_pt1"](dve, n, 0)
                    t["dve_max"](dve, n, 1)
                    t["dve_scale"](dve, n, 0)
                    if not first:
                        y_normalize(n - 1)
                    if not final:
                        copy_k(n + 1, 1 - par)
                    t["dve_copy_pt1"](dve, n, 1)
                    if not first:
                        x_moments(n - 1)

                for q in range(2):
                    dve.memset(QZ[q][:, :, :], 0.0).then_inc(s["buffers_zeroed"], 1)
                dve.memset(sq[:, :, :], 1.0).then_inc(s["buffers_zeroed"], 1)
                dve.memset(qk[:, :, :], 1.0).then_inc(s["buffers_zeroed"], 1)
                norm_inputs(0)
                sum_squares(0)
                copy_k(0, 0)
                body(0, 0, first=True)
                with dve.Fori(0, B // 2 - 1) as i:
                    body(2 * i + 1, 1)
                    body(2 * i + 2, 0)
                body(B - 1, 1, final=True)
                t["dve_scale"](dve, B - 1, 1)
                y_moments(B - 1)
                y_normalize(B - 1)
                x_moments(B - 1)

            @block.gpsimd
            def _(pool):
                def norm_qk(m):
                    wait(pool, s["ss_ready"], m + 1)
                    pool.tensor_tensor(r_norm[:, :], ssm[:, :], mhalf[:, 0:3 * H], ALU.pow).then_inc(s["norm_inverted"], 1)
                    wait(pool, s["norm_inverted"], m + 1)
                    wait(pool, s["klT_turned"], m)
                    pool.tensor_tensor(qkn[:, :, :].rearrange("p a (h d) -> p (a h) d", d=HD),
                                       qk[:, :, :].rearrange("p a (h d) -> p (a h) d", d=HD),
                                       r_norm[:, :].unsqueeze(2).broadcast_to([P, 3 * H, HD]), ALU.mult).then_inc(s["normed"], 1)

                def finish(n):
                    wait(pool, s["y_var_ready"], n + 1)
                    pool.tensor_tensor(y_rstd[:, :], y_var[:, :], mhalf[:, 0:1], ALU.pow).then_inc(s["y_inverted"], 1)

                def add(n):
                    wait(pool, s["y_normed"], n + 1)
                    pool.tensor_tensor(y_w[:, :], y_norm[:, :], lnow[:, :], ALU.mult).then_inc(s["y_weighted"], 1)
                    wait(pool, s["y_weighted"], n + 1)
                    pool.tensor_tensor(y_wb[:, :], y_w[:, :], lnob[:, :], ALU.add).then_inc(s["y_biased"], 1)
                    wait(pool, s["y_biased"], n + 1)
                    xs = X[:, entries(n), :].rearrange("p a d -> p (a d)")
                    pool.tensor_tensor(xs, xs, y_wb[:, :], ALU.add).then_inc(s["x_added"], 1)

                def body(n, final=False, first=False):
                    if not final:
                        norm_qk(n + 1)
                    if not first:
                        finish(n - 1)
                        add(n - 1)

                wait(pool, s["buffers_zeroed"], 4)
                norm_qk(0)
                body(0, first=True)
                with pool.Fori(0, B // 2 - 1) as i:
                    body(2 * i + 1)
                    body(2 * i + 2)
                body(B - 1, final=True)
                finish(B - 1)
                add(B - 1)


def l0_ffn(nc, psum, X, X2, XN, stats6, mean, rstd, mhalf, small, ident, ones, wm_in, wp_in, wc1_in, wc2_in):
    with ExitStack() as sems, ExitStack() as st:
        def sb(name, shape, dt=F32):
            return st.enter_context(nc.sbuf_tensor(name, shape, dt))

        wm = sb("wm", [D, F_FULL])
        wp = sb("wp", [P, F_FULL // P, D])
        wc1 = sb("wc1", [D, 32])
        wc2 = sb("wc2", [32, F_FULL])
        pooledT = sb("pooledT", [D, B])
        same_entry = sb("same_entry", [P, P])
        earlier = sb("earlier", [P, P])
        history = sb("history", [P, Q4])
        maskT = sb("maskT", [P, 3, P])
        done = sb("done", [P, 1], I32)
        bufs = dict(
            zn=sb("zn", [P, GB, D]), zT=sb("zT", [D, GB * P]), hT=[sb(f"hT{i}", [P, GB * P]) for i in range(4)],
            yT=sb("yT", [D, GB * P]), pool4=sb("pool4", [D, GB]))

        with signals(nc, "ffn") as sem:
            var_ready, weights, router_consts = sem("var_ready"), sem("weights"), sem("router_consts")
            powed, moments_step = sem("powed"), sem("moments_step")
            with nc.Block() as block:
                @block.sync
                def _(sp):
                    sp.dma_start(wm[:, :], wm_in).then_inc(weights, 16)
                    sp.dma_start(wp[:, :, :], wp_in.rearrange("(c p) d -> p c d", p=P)).then_inc(weights, 16)
                    sp.dma_start(wc1[:, :], wc1_in).then_inc(weights, 16)
                    sp.dma_start(wc2[:, :], wc2_in).then_inc(weights, 16)
                    sp.wait_ge(weights, 64)

                @block.vector
                def _(dve):
                    moments(dve, stats6, mean, small, moments_step)
                    dve.tensor_scalar(small[:, 0, :], small[:, 3, :], LN_EPS, None, ALU.add).then_inc(var_ready, 1)
                    dve.memset(done[:, :], 0)
                    dve.memset(history[:, :], 0.0).then_inc(moments_step, 1)
                    dve.wait_ge(moments_step, 7)
                    dve.memset(history[0:32, :], 1.0)
                    dve.memset(history[32:64, 0:F_ITER - Q4], 1.0)

                @block.gpsimd
                def _(pool):
                    pool.memset(same_entry[:, :], 0.0).then_inc(router_consts, 1)
                    pool.memset(earlier[:, :], 0.0).then_inc(router_consts, 1)
                    pool.wait_ge(var_ready, 1)
                    pool.tensor_tensor(rstd[:, :], small[:, 0, :], mhalf[:, :], ALU.pow).then_inc(powed, 1)
                    n = 2
                    for q in range(4):
                        pool.wait_ge(router_consts, n)
                        v = same_entry[:, :].rearrange("p (a c) -> p a c", a=4)
                        pool.affine_select(out=v, in_=v, compare_op=ALU.not_equal, fill=1.0, base=-32 * q,
                                           pattern=[[0, 4], [-1, 32]], channel_multiplier=1).then_inc(router_consts, 1)
                        n += 1
                        if q < 3:
                            v = earlier[:, 32 * (q + 1):].rearrange("p (a c) -> p a c", a=3 - q)
                            pool.affine_select(out=v, in_=v, compare_op=ALU.not_equal, fill=1.0, base=-32 * q,
                                               pattern=[[0, 3 - q], [-1, 32]], channel_multiplier=1).then_inc(router_consts, 1)
                            n += 1
                    pool.wait_ge(router_consts, n)

        ffn_step(nc, psum, bufs, X, X, X2, XN, stats6, mean, rstd, wm, wp, None, pooledT, ident, None, 1)
        route(nc, psum, pooledT, wc1, wc2, same_entry, earlier, history, maskT, done, ident, ones, None, 1)
        for step in (2, 3):
            ffn_step(nc, psum, bufs, XN, X, X2, XN, stats6, None, None, wm, wp, maskT, pooledT, ident, done, step)
            if step == 2:
                route(nc, psum, pooledT, wc1, wc2, same_entry, earlier, history, maskT, done, ident, ones, done, step)


def moments(dve, stats6, mean, small, step):
    m_even, v_even, m_odd, v_odd = (stats6[:, :, i] for i in (1, 2, 4, 5))
    dve.tensor_tensor(small[:, 0, :], m_even, m_odd, ALU.add)
    dve.tensor_tensor(small[:, 1, :], m_even, m_odd, ALU.subtract)
    dve.tensor_tensor(small[:, 2, :], v_even, v_odd, ALU.add).then_inc(step, 3)
    dve.wait_ge(step, 3)
    dve.tensor_scalar(mean[:, :], small[:, 0, :], 0.5, None, ALU.mult).then_inc(step, 1)
    dve.scalar_tensor_tensor(small[:, 3, :], small[:, 1, :], 0.25, small[:, 1, :], ALU.mult, ALU.mult).then_inc(step, 1)
    dve.wait_ge(step, 5)
    dve.scalar_tensor_tensor(small[:, 3, :], small[:, 2, :], 1.0 / D, small[:, 3, :], ALU.mult, ALU.add).then_inc(step, 1)
    dve.wait_ge(step, 6)


def entries(n, count=1):
    return slice(n, n + count) if isinstance(n, int) else bass.ds(n, count)


@contextmanager
def where_not_done(eng, done):
    if done is None:
        yield
    else:
        flag = eng.value_load(done[0:1, 0:1], min_val=0, max_val=1)
        with eng.If(flag == 0):
            yield


def ffn_step(nc, psum, bufs, SRC, X, X2, XN, stats6, mean, rstd, wm, wp, maskT, pooledT, ident, done, step):
    chunks = 4 if maskT is None else F_FULL // P
    zn, zT, hT, yT, pool4 = (bufs[k] for k in ("zn", "zT", "hT", "yT", "pool4"))
    ring = 3
    with ExitStack() as sems, ExitStack() as st:
        sem = sems.enter_context(signals(nc, f"ffn_step{step}"))
        in_ready = sem("in_ready")
        in_turned = sem("in_turned")
        in_copied = sem("in_copied")
        hidden = [sem(f"hidden{f}") for f in range(chunks)]
        activated = [sem(f"activated{f}") for f in range(chunks)]
        multiplied = [sem(f"multiplied{f}") for f in range(chunks)]
        out_copied = sem("out_copied")
        out_summed = sem("out_summed")
        out_pooled = sem("out_pooled")
        out_turned = sem("out_turned")
        xn_written = sem("xn_written")
        x_added = sem("ffn_x_added")
        x_stats = sem("ffn_x_stats")

        def last_in_ring(f, size):
            return (f - size, 0) if f >= size else (max(c for c in range(chunks) if c % size == f % size), 1)

        block = st.enter_context(nc.Block())

        @block.tensor
        def _(pe):
            def turn_back(g):
                wait(pe, out_copied, g + 1)
                wait(pe, x_added, g)
                for b in range(GB):
                    tr = pe.transpose(psum[:, 7, b * P:(b + 1) * P], yT[:, b * P:(b + 1) * P], ident[:, :])
                tr.then_inc(out_turned, 1)

            def up(g, f):
                before, back = last_in_ring(f, ring)
                wait(pe, activated[before], g + 1 - back)
                pe.matmul(psum[:, f % ring, :], wm[:, f * P:(f + 1) * P], zT[:, :], start=True, stop=True).then_inc(hidden[f], 1)

            def down(g, f):
                wait(pe, activated[f], g + 1)
                if f == 0:
                    wait(pe, out_copied, g)
                    wait(pe, out_summed, g)
                pe.matmul(psum[:, 4, :], wp[:, f, :], hT[f % 4][:, :], start=(f == 0), stop=(f == chunks - 1)).then_inc(multiplied[f], 1)

            def body(g, first=False):
                wait(pe, in_ready, g + 1)
                wait(pe, in_copied, g)
                for b in range(GB):
                    tr = pe.transpose(psum[:, 6, b * P:(b + 1) * P], zn[:, b, :], ident[:, :])
                tr.then_inc(in_turned, 1)
                if not first:
                    turn_back(g - 1)
                wait(pe, in_copied, g + 1)
                up(g, 0)
                up(g, 1)
                for f in range(chunks):
                    if f + 2 < chunks:
                        up(g, f + 2)
                    down(g, f)

            with where_not_done(pe, done):
                body(0, first=True)
                with pe.Fori(0, NG - 1) as i:
                    body(i + 1)
                turn_back(NG - 1)

        @block.scalar
        def _(act):
            def body(g):
                wait(act, in_turned, g + 1)
                wait(act, hidden[chunks - 1], g)
                act.copy(zT[:, :], psum[:, 6, :]).then_inc(in_copied, 1)
                if maskT is None:
                    for f in range(0, chunks, 2):
                        wait(act, hidden[f], g + 1)
                        before, back = last_in_ring(f, 4)
                        wait(act, multiplied[before], g + 1 - back)
                        act.activation(hT[f % 4][:, :], psum[:, f % ring, :], ACT.Relu).then_inc(activated[f], 1)
                wait(act, multiplied[chunks - 1], g + 1)
                wait(act, out_turned, g)
                wait(act, out_summed, g)
                act.copy(yT[:, :], psum[:, 4, :]).then_inc(out_copied, 1)

            with where_not_done(act, done):
                body(0)
                with act.Fori(0, NG - 1) as i:
                    body(i + 1)

        @block.vector
        def _(dve):
            def load_in(g):
                wait(dve, in_turned, g)
                for b in range(GB):
                    n = g * GB + b
                    src = SRC[:, entries(n), :].rearrange("p a d -> p (a d)")
                    if mean is None:
                        i = dve.tensor_scalar(zn[:, b, :], src, 1.0, None, ALU.mult)
                    else:
                        i = dve.tensor_scalar(zn[:, b, :], src, mean[:, entries(n)], rstd[:, entries(n)], ALU.subtract, ALU.mult)
                i.then_inc(in_ready, 1)

            def activate(g, f):
                wait(dve, hidden[f], g + 1)
                before, back = last_in_ring(f, 4)
                wait(dve, multiplied[before], g + 1 - back)
                if maskT is None:
                    i = dve.tensor_scalar(hT[f % 4][:, :], psum[:, f % ring, :], 0.0, None, ALU.max)
                else:
                    active = maskT[:, f % 3, entries(g * GB + (f // 3) * B, GB)].unsqueeze(2).broadcast_to([P, GB, P])
                    i = dve.scalar_tensor_tensor(hT[f % 4][:, :].rearrange("p (b t) -> p b t", b=GB),
                                                 psum[:, f % ring, :].rearrange("p (b t) -> p b t", b=GB), 0.0, active,
                                                 ALU.max, ALU.mult)
                i.then_inc(activated[f], 1)

            def pool_out(g):
                wait(dve, out_copied, g + 1)
                wait(dve, out_pooled, g)
                dve.tensor_reduce(pool4[:, :], yT[:, :].rearrange("p (b t) -> p b t", b=GB), AX.X,
                                  ALU.add).then_inc(out_summed, 1)
                wait(dve, out_summed, g + 1)
                dve.tensor_scalar(pooledT[:, entries(g * GB, GB)], pool4[:, :], 1.0 / P, None, ALU.mult).then_inc(out_pooled, 1)

            def write_out(g):
                o = psum[:, 7, :].rearrange("p (b d) -> p b d", b=GB)
                wait(dve, out_turned, g + 1)
                dve.tensor_scalar(XN[:, entries(g * GB, GB), :], o, 1.0, None, ALU.mult).then_inc(xn_written, 1)
                wait(dve, xn_written, g + 1)
                dve.tensor_tensor(X2[:, entries(g * GB, GB), :], o, X[:, entries(g * GB, GB), :], ALU.add).then_inc(x_added, 1)
                wait_apart(dve, x_added, g + 1, in_ready)
                for b in range(GB):
                    n = g * GB + b
                    i = dve.bn_stats(stats6[:, entries(n), :].rearrange("p a d -> p (a d)"),
                                     X2[:, entries(n), :].rearrange("p a d -> p (a d)"))
                i.then_inc(x_stats, 1)

            def body(g, first=False, final=False):
                if not first:
                    write_out(g - 1)
                for f in (range(1, chunks, 2) if maskT is None else range(chunks)):
                    activate(g, f)
                if not final:
                    load_in(g + 1)
                pool_out(g)

            with where_not_done(dve, done):
                load_in(0)
                body(0, first=True)
                with dve.Fori(0, NG - 2) as i:
                    body(i + 1)
                body(NG - 1, final=True)
                write_out(NG - 1)


def wait_apart(eng, sem, value, met):
    eng.wait_ge(met, 1)
    wait(eng, sem, value)


def route(nc, psum, pooledT, wc1, wc2, same_entry, earlier, history, maskT, done, ident, ones, flag, step):
    with ExitStack() as sems, ExitStack() as st:
        def sb(name, shape, dt=F32):
            return st.enter_context(nc.sbuf_tensor(f"{name}_{step}", shape, dt))

        sem = sems.enter_context(signals(nc, f"route{step}"))
        zr = sb("zr", [32, B])
        logits = sb("logits", [P, Q4])
        u = sb("u", [P, Q4])
        hit = sb("hit", [P, Q4])
        equal = sb("equal", [P, Q4])
        rank = sb("rank", [P, Q4])
        chosen = sb("chosen", [P, Q4])
        combined = sb("combined", [P, Q4])
        count = sb("count", [P, 2])
        positive = sb("positive", [P, 1])
        sign = sb("sign", [P, 1])
        wanted = sb("wanted", [P, 1])
        bit = sb("bit", [P, 1], I32)
        found = sb("found", [P, 1], I32)
        trial = sb("trial", [P, 1], I32)
        enough = sb("enough", [P, 1], I32)
        gained = sb("gained", [P, 1], I32)
        threshold = sb("threshold", [P, 1])
        offset = sb("offset", [P, 1])
        need = sb("need", [P, 1])
        novelty = sb("novelty", [P, 1])
        little = sb("little", [P, 1], I32)

        z_done = sem("z_done")
        z_taken = sem("z_taken")
        logits_done = sem("logits_done")
        counted = sem("counted")
        totalled = sem("totalled")
        dve_step = sem("dve_step")
        mask_ready = sem("mask_ready")
        mask_turned = sem("mask_turned")
        BITS = 31
        total = psum[:, 2, 0:1]

        block = st.enter_context(nc.Block())

        @block.tensor
        def _(pe):
            with where_not_done(pe, flag):
                pe.matmul(psum[0:32, 0, 0:B], wc1[:, :], pooledT[:, :], start=True, stop=True).then_inc(z_done, 1)
                pe.wait_ge(z_taken, 1)
                for q in range(4):
                    mm = pe.matmul(psum[32 * q:32 * q + 32, 1, 0:Q4], zr[:, :], wc2[:, q * Q4:(q + 1) * Q4], start=True, stop=True)
                mm.then_inc(logits_done, 1)
                pe.wait_ge(counted, 1)
                pe.matmul(total, same_entry[:, :], count[:, 0:1], start=True, stop=True).then_inc(totalled, 1)
                with pe.Fori(0, BITS) as i:
                    pe.wait_ge(counted, i + 2)
                    pe.matmul(total, same_entry[:, :], count[:, 0:1], start=True, stop=True).then_inc(totalled, 1)
                pe.wait_ge(counted, BITS + 2)
                pe.matmul(total, same_entry[:, :], count[:, 0:1], start=True, stop=True)
                pe.matmul(psum[:, 3, 0:1], earlier[:, :], count[:, 1:2], start=True, stop=True).then_inc(totalled, 1)
                pe.wait_ge(mask_ready, 1)
                for j in range(3):
                    pe.transpose(psum[:, 5, j * P:(j + 1) * P], chosen[:, j * P:(j + 1) * P], ident[:, :])
                pe.matmul(psum[:, 6, 0:1], ones[:, :], count[:, 0:1], start=True, stop=True).then_inc(mask_turned, 1)

        @block.scalar
        def _(act):
            with where_not_done(act, flag):
                act.wait_ge(z_done, 1)
                act.activation(zr[:, :], psum[0:32, 0, 0:B], ACT.Relu).then_inc(z_taken, 1)

        @block.vector
        def _(dve):
            at = [0]

            def then(ins):
                at[0] += 1
                ins.then_inc(dve_step, 1)
                dve.wait_ge(dve_step, at[0])

            with where_not_done(dve, flag):
                dve.wait_ge(logits_done, 1)
                then(dve.tensor_copy(logits[:, :], psum[:, 1, 0:Q4]))
                dve.tensor_scalar(hit[:, :], logits[:, :], 0.0, None, ALU.is_ge, ALU.add, accum_out=count[:, 0:1]).then_inc(counted, 1)
                dve.memset(bit[:, :], 1 << (BITS - 1))
                dve.memset(found[:, :], 0)
                dve.wait_ge(totalled, 1)
                then(dve.tensor_scalar(positive[:, :], total, float(F_ITER), None, ALU.is_ge))
                dve.tensor_scalar(sign[:, :], positive[:, :], 2.0, -1.0, ALU.mult, ALU.add)
                then(dve.tensor_scalar(wanted[:, :], positive[:, :], float(2 * F_ITER - F_FULL - 1), float(F_FULL - F_ITER + 1),
                                       ALU.mult, ALU.add))
                then(dve.tensor_scalar(u[:, :], logits[:, :], sign[:, :], None, ALU.mult))
                done_so_far = at[0]
                per_bit = 4
                with dve.Fori(0, BITS) as i:
                    base = i * per_bit + done_so_far
                    dve.tensor_tensor(trial[:, :], found[:, :], bit[:, :], ALU.bitwise_or).then_inc(dve_step, 1)
                    dve.wait_ge(dve_step, base + 1)
                    dve.tensor_scalar(hit[:, :], u[:, :], trial[:, :].bitcast(F32), None, ALU.is_ge, ALU.add,
                                      accum_out=count[:, 0:1]).then_inc(counted, 1)
                    dve.wait_ge(totalled, i + 2)
                    dve.tensor_tensor(enough[:, :], total, wanted[:, :], ALU.is_ge).then_inc(dve_step, 1)
                    dve.wait_ge(dve_step, base + 2)
                    dve.tensor_tensor(gained[:, :], bit[:, :], enough[:, :], ALU.mult).then_inc(dve_step, 1)
                    dve.wait_ge(dve_step, base + 3)
                    dve.tensor_scalar(bit[:, :], bit[:, :], 1, None, ALU.logical_shift_right)
                    dve.tensor_tensor(found[:, :], found[:, :], gained[:, :], ALU.bitwise_or).then_inc(dve_step, 1)
                    dve.wait_ge(dve_step, base + 4)
                at[0] += BITS * per_bit
                then(dve.tensor_tensor(threshold[:, :], found[:, :].bitcast(F32), sign[:, :], ALU.mult))
                then(dve.tensor_scalar(equal[:, :], logits[:, :], threshold[:, :], None, ALU.is_equal, ALU.add, accum_out=count[:, 1:2]))
                dve.tensor_scalar(hit[:, :], logits[:, :], threshold[:, :], None, ALU.is_gt, ALU.add,
                                  accum_out=count[:, 0:1]).then_inc(counted, 1)
                dve.wait_ge(totalled, BITS + 2)
                dve.tensor_scalar(need[:, :], total, -1.0, float(F_ITER), ALU.mult, ALU.add)
                then(dve.tensor_copy(offset[:, :], psum[:, 3, 0:1]))
                then(dve.memset(u[:, :], 1.0))
                then(dve.tensor_tensor_scan(rank[:, :], u[:, :], equal[:, :], offset[:, :], ALU.mult, ALU.add))
                then(dve.scalar_tensor_tensor(equal[:, :], rank[:, :], need[:, :], equal[:, :], ALU.is_le, ALU.mult))
                then(dve.tensor_tensor(chosen[:, :], hit[:, :], equal[:, :], ALU.add))
                then(dve.tensor_tensor(combined[:, :], history[:, :], chosen[:, :], ALU.max))
                then(dve.tensor_tensor(hit[:, :], combined[:, :], history[:, :], ALU.subtract))
                then(dve.tensor_copy(history[:, :], combined[:, :]))
                dve.tensor_scalar(combined[:, :], hit[:, :], 1.0, None, ALU.mult, ALU.add, accum_out=count[:, 0:1]).then_inc(mask_ready, 1)
                dve.wait_ge(mask_turned, 1)
                dve.tensor_copy(maskT[:, :, :], psum[:, 5, 0:3 * P].rearrange("p (j c) -> p j c", j=3))
                then(dve.tensor_scalar(novelty[:, :], psum[:, 6, 0:1], 1.0 / (B * F_ITER), None, ALU.mult))
                then(dve.tensor_scalar(little[:, :], novelty[:, :], 0.7, None, ALU.is_lt))
                then(dve.tensor_copy(done[:, :], little[:, :]))


def attention16(nc, kind, psum, XI, XO, stats6, mean, rstd, rms, mhalf, small, ident, ident_bf, ones, cols,
                weights_in, ctxT_in, mask_in):
    l1 = kind == "l1"
    H, HD = 16, 8
    K = C if l1 else P
    LAT = 64
    G1 = cols[:, 6:7]
    with ExitStack() as sems, ExitStack() as st:
        def sb(name, shape, dt=F32):
            return st.enter_context(nc.sbuf_tensor(f"{kind}_{name}", shape, dt))

        sem = sems.enter_context(signals(nc, kind))
        wq = sb("wq1", [D, D])
        wk = sb("wk1", [D if l1 else LAT, D])
        wv = sb("wv1", [D if l1 else LAT, D])
        wdkv = sb("wdkv", [D, LAT])
        wo = sb("wo1", [P, 4, D])
        mask32 = sb("mask32", [P, C], I32)
        bias = sb("bias", [P, K], BF16)
        own_rows = sb("own_rows", [P, H])
        E = sb("E16", [16, 8, K], BF16)
        scale = sb("scale", [P, B])
        loaded = sem("loaded")
        mask_loaded = sem("mask_loaded")
        step = sem("moments_step")
        var_ready = sem("var_ready")
        pow_done = sem("pow_done")
        made = sem("made")
        with nc.Block() as block:
            @block.sync
            def _(sp):
                if l1:
                    sp.dma_start(mask32[:, :], mask_in).then_inc(mask_loaded, 16)
                    tiles = ((wq, weights_in[0]), (wk, weights_in[1]), (wv, weights_in[2]))
                else:
                    tiles = ((wq, weights_in[0]), (wdkv, weights_in[1]), (wk, weights_in[2]), (wv, weights_in[3]))
                for tile, src in tiles:
                    sp.dma_start(tile[:, :], src).then_inc(loaded, 16)
                sp.dma_start(wo[:, :, :], weights_in[-1].rearrange("(c p) d -> p c d", p=P)).then_inc(loaded, 16)
                sp.wait_ge(loaded, 16 * (len(tiles) + 1))

            @block.vector
            def _(dve):
                moments(dve, stats6, mean, small, step)
                dve.tensor_scalar(small[:, 0, :], small[:, 3, :], LN_EPS, None, ALU.add).then_inc(var_ready, 1)
                if l1:
                    dve.wait_ge(mask_loaded, 16)
                    dve.tensor_scalar(bias[:, :], mask32[:, :], 0.0, -2e9, ALU.is_equal, ALU.mult)
                    return
                dve.wait_ge(pow_done, 1)
                dve.tensor_tensor(small[:, 1, :], rstd[:, :], rstd[:, :], ALU.mult).then_inc(var_ready, 1)
                dve.wait_ge(var_ready, 2)
                dve.tensor_tensor(small[:, 2, :], small[:, 1, :], small[:, 3, :], ALU.mult).then_inc(var_ready, 1)
                dve.wait_ge(var_ready, 3)
                dve.tensor_scalar(small[:, 1, :], small[:, 2, :], RMS_EPS, None, ALU.add).then_inc(var_ready, 1)
                dve.wait_ge(pow_done, 2)
                dve.tensor_tensor(scale[:, :], rstd[:, :], rms[:, :], ALU.mult)

            @block.gpsimd
            def _(pool):
                pool.wait_ge(var_ready, 1)
                pool.tensor_tensor(rstd[:, :], small[:, 0, :], mhalf[:, :], ALU.pow).then_inc(pow_done, 1)
                if not l1:
                    pool.wait_ge(var_ready, 4)
                    pool.tensor_tensor(rms[:, :], small[:, 1, :], mhalf[:, :], ALU.pow).then_inc(pow_done, 1)
                    pool.memset(bias[:, :], 0.0).then_inc(made, 1)
                pool.memset(E[:, :, :], 0.0).then_inc(made, 1)
                pool.memset(own_rows[:, :], 1.0).then_inc(made, 1)
                n = 2 if l1 else 3
                pool.wait_ge(made, n)
                if not l1:
                    pool.affine_select(out=bias[:, :], in_=bias[:, :], compare_op=ALU.is_ge, fill=-1e9, base=0,
                                       pattern=[[-1, K]], channel_multiplier=1)
                pool.affine_select(out=own_rows[:, :], in_=own_rows[:, :], compare_op=ALU.is_ge, fill=0.0, base=0,
                                   pattern=[[-HD, H]], channel_multiplier=1)
                pool.affine_select(out=E[:, :, :], in_=E[:, :, :], compare_op=ALU.not_equal, fill=1.0, base=0,
                                   pattern=[[-1, 8], [0, K]], channel_multiplier=1).then_inc(made, 1)
                pool.wait_ge(made, n + 1)
                pool.affine_select(out=own_rows[:, :], in_=own_rows[:, :], compare_op=ALU.is_ge, fill=0.0, base=HD - 1,
                                   pattern=[[HD, H]], channel_multiplier=-1)
                pool.affine_select(out=E[:, :, :], in_=E[:, :, :], compare_op=ALU.not_equal, fill=1.0, base=-8,
                                   pattern=[[-1, 8], [0, K]], channel_multiplier=1)

        zn = sb("zn16", [P, D])
        zT = sb("zT16", [D, P])
        cT = [sb(f"cT{i}", [D, C]) for i in range(2)]
        latT = sb("latT", [LAT, P])
        kT = sb("kT", [P, K])
        QT = [sb(f"QT{i}", [P, P]) for i in range(2)]
        KX = [sb(f"KX{i}", [P, H, K]) for i in range(2)]
        V = [sb(f"V{i}", [P, H, 32]) for i in range(2)]
        names = ("z_made z_turned z_copied q_proj q_copied lat_copied kv_proj k_copied v_copied k_spread x_added x_stats "
                 "v_zeroed").split()
        s = {name: sem(name) for name in names}
        c_loaded = [sem(f"c_loaded{i}") for i in range(2)]
        cell = {}

        def score(pe, n, u):
            par = cell["par"]
            wait(pe, s["q_copied"], n + 1)
            wait(pe, s["k_spread"], n + 1)
            for c in range(2):
                pe.matmul(psum[:, 2 * u + c, 0:4 * K], ident_bf[:, :], bias[:, :].unsqueeze(1).broadcast_to([P, 4, K]),
                          start=True, stop=False, skip_group_check=True)
                h = 8 * u + 4 * c
                mm = pe.matmul(psum[:, 2 * u + c, 0:4 * K], QT[par][:, :], KX[par][:, h:h + 4, :].rearrange("p h k -> p (h k)"),
                               start=False, stop=True, skip_group_check=True)
            return mm

        pt_plan = ([(j, 0, K) for j in range(4)], [(4 + j, 0, K) for j in range(4)])
        pv_plan = [(j, 32 * (j % 4), j // 4, [(j // 4, j % 4, K)]) for j in range(8)]
        t = softmax_units(nc, st, sem, psum, 8, K, 32, pt_plan, pv_plan, score, E, ident, ident_bf, ones, kind)

        with nc.Block() as block:
            @block.tensor
            def _(pe):
                def prepare_a(m):
                    wait(pe, s["z_made"], m + 1)
                    wait(pe, s["v_copied"], m)
                    pe.transpose(psum[:, 6, 0:P], zn[:, :], ident[:, :]).then_inc(s["z_turned"], 1)

                def prepare_b(m, par):
                    wait(pe, s["z_copied"], m + 1)
                    if l1:
                        pe.matmul(psum[:, 7, 0:P], wq[:, :], zT[:, :], start=True, stop=True).then_inc(s["q_proj"], 1)
                        wait(pe, c_loaded[par], half(m) * 16 + 16)
                        pe.matmul(psum[:, 6, 0:C], wk[:, :], cT[par][:, :], start=True, stop=True)
                        pe.matmul(psum[0:C, 6, P:2 * P], cT[par][:, :], wv[:, :], start=True, stop=True).then_inc(s["kv_proj"], 1)
                    else:
                        pe.matmul(psum[0:LAT, 7, P:2 * P], wdkv[:, :], zT[:, :], start=True, stop=True)
                        pe.matmul(psum[:, 7, 0:P], wq[:, :], zT[:, :], start=True, stop=True).then_inc(s["q_proj"], 1)
                        wait(pe, s["lat_copied"], m + 1)
                        pe.matmul(psum[:, 6, 0:K], wk[:, :], latT[:, :], start=True, stop=True)
                        pe.matmul(psum[:, 6, P:2 * P], latT[:, :], wv[:, :], start=True, stop=True).then_inc(s["kv_proj"], 1)

                def half(m):
                    return m // 2

                def pv(n, u, par):
                    t["pe_pv"](pe, n, u, lambda h, i: V[par][0:K, h, :])

                def body(n, par, final=False, first=False):
                    cell["par"] = par
                    t["pe_scores"](pe, n, 1)
                    t["pe_turn_max"](pe, n, 0)
                    if not first:
                        pv(n - 1, 1, 1 - par)
                    t["pe_subtract_max"](pe, n, 0)
                    if not final:
                        prepare_a(n + 1)
                    if not first:
                        t["pe_project"](pe, n - 1, wo)
                    t["pe_turn_probs"](pe, n, 0)
                    t["pe_turn_max"](pe, n, 1)
                    if not final:
                        prepare_b(n + 1, 1 - par)
                    pv(n, 0, par)
                    t["pe_subtract_max"](pe, n, 1)
                    t["pe_turn_probs"](pe, n, 1)
                    if not final:
                        cell["par"] = 1 - par
                        t["pe_scores"](pe, n + 1, 0)

                prepare_a(0)
                prepare_b(0, 0)
                cell["par"] = 0
                t["pe_scores"](pe, 0, 0)
                body(0, 0, first=True)
                with pe.Fori(0, B // 2 - 1) as i:
                    body(2 * i + 1, 1)
                    body(2 * i + 2, 0)
                body(B - 1, 1, final=True)
                wait(pe, s["v_zeroed"], 2)
                pv(B - 1, 1, 1)
                t["pe_project"](pe, B - 1, wo)

            @block.scalar
            def _(act):
                def prepare_a(m):
                    wait(act, s["z_turned"], m + 1)
                    wait(act, s["q_proj"], m)
                    act.activation(zT[:, :], psum[:, 6, 0:P], ACT.Copy, scale=1.0 if l1 else G1).then_inc(s["z_copied"], 1)

                def prepare_b(m, par):
                    wait(act, s["q_proj"], m + 1)
                    if not l1:
                        wait(act, s["kv_proj"], m)
                        act.copy(latT[:, :], psum[0:LAT, 7, P:2 * P]).then_inc(s["lat_copied"], 1)
                    wait(act, t["scored"][1], m - 1)
                    act.mul(QT[par][:, :], psum[:, 7, 0:P], float(HD) ** -0.5).then_inc(s["q_copied"], 1)
                    wait(act, s["kv_proj"], m + 1)
                    wait(act, s["k_spread"], m)
                    act.copy(kT[:, :], psum[:, 6, 0:K]).then_inc(s["k_copied"], 1)
                    wait(act, s["v_zeroed"], 2)
                    wait(act, t["pv_done"][1], m - 1)
                    act.copy(V[par][0:K, :, 0:HD], psum[0:K, 6, P:2 * P].rearrange("k (h d) -> k h d", d=HD)).then_inc(s["v_copied"], 1)

                def body(n, par, final=False, first=False):
                    t["act_copy_max"](act, n, 0)
                    t["act_exp"](act, n, 0)
                    if not final:
                        prepare_a(n + 1)
                    t["act_copy_pt0"](act, n, 0)
                    t["act_copy_max"](act, n, 1)
                    if not final:
                        prepare_b(n + 1, 1 - par)
                    t["act_exp"](act, n, 1)
                    t["act_copy_pt0"](act, n, 1)

                prepare_a(0)
                prepare_b(0, 0)
                body(0, 0, first=True)
                with act.Fori(0, B // 2 - 1) as i:
                    body(2 * i + 1, 1)
                    body(2 * i + 2, 0)
                body(B - 1, 1, final=True)

            @block.vector
            def _(dve):
                def norm_input(m):
                    src = XI[:, entries(m), :].rearrange("p a d -> p (a d)")
                    wait(dve, s["z_turned"], m)
                    dve.tensor_scalar(zn[:, :], src, mean[:, entries(m)], (rstd if l1 else scale)[:, entries(m)], ALU.subtract,
                                      ALU.mult).then_inc(s["z_made"], 1)
                    if not l1:
                        dve.tensor_scalar(XO[:, entries(m), :].rearrange("p a d -> p (a d)"), src, mean[:, entries(m)],
                                          rstd[:, entries(m)], ALU.subtract, ALU.mult)

                def add_projection(n):
                    wait(dve, t["projected"], n + 1)
                    xs = XO[:, entries(n), :].rearrange("p a d -> p (a d)")
                    dve.tensor_tensor(xs, psum[:, 5, 0:D], xs, ALU.add).then_inc(t["projection_taken"], 1)
                    wait_apart(dve, t["projection_taken"], n + 1, s["z_made"])
                    dve.bn_stats(stats6[:, entries(n), :].rearrange("p a d -> p (a d)"), xs).then_inc(s["x_stats"], 1)

                def body(n, par, final=False, first=False):
                    t["dve_max"](dve, n, 0)
                    if not first:
                        t["dve_scale"](dve, n - 1, 1)
                    if not final:
                        norm_input(n + 1)
                    if not first:
                        add_projection(n - 1)
                    t["dve_copy_pt1"](dve, n, 0)
                    t["dve_max"](dve, n, 1)
                    t["dve_scale"](dve, n, 0)
                    t["dve_copy_pt1"](dve, n, 1)

                for q in range(2):
                    dve.memset(V[q][:, :, :], 0.0).then_inc(s["v_zeroed"], 1)
                norm_input(0)
                body(0, 0, first=True)
                with dve.Fori(0, B // 2 - 1) as i:
                    body(2 * i + 1, 1)
                    body(2 * i + 2, 0)
                body(B - 1, 1, final=True)
                t["dve_scale"](dve, B - 1, 1)
                add_projection(B - 1)

            @block.gpsimd
            def _(pool):
                def spread_k(m, par):
                    wait(pool, s["k_copied"], m + 1)
                    wait(pool, t["scored"][1], m - 1)
                    pool.tensor_tensor(KX[par][:, :, :], kT[:, :].unsqueeze(1).broadcast_to([P, H, K]),
                                       own_rows[:, :].unsqueeze(2).broadcast_to([P, H, K]), ALU.mult).then_inc(s["k_spread"], 1)

                spread_k(0, 0)
                spread_k(1, 1)
                with pool.Fori(0, B // 2 - 1) as i:
                    spread_k(2 * i + 2, 0)
                    spread_k(2 * i + 3, 1)

            if l1:
                @block.sync
                def _(sp):
                    def load(m, par):
                        wait(sp, s["kv_proj"], m - 1)
                        sp.dma_start(cT[par][:, :], ctxT_in[entries(m)].rearrange("a d t -> (a d) t")).then_inc(c_loaded[par], 16)

                    load(0, 0)
                    load(1, 1)
                    with sp.Fori(0, B // 2 - 1) as i:
                        load(2 * i + 2, 0)
                        load(2 * i + 3, 1)


def moe(nc, psum, X2, X3, stats6, mean, rms, mhalf, small, ident, cols, gate_in, w1_in, w2_in, out):
    NE, HID, HALVES = 8, 256, 2
    G2 = cols[:, 7:8]
    N = GB * P
    with ExitStack() as sems, ExitStack() as st:
        def sb(name, shape, dt=F32):
            return st.enter_context(nc.sbuf_tensor(name, shape, dt))

        sem = sems.enter_context(signals(nc, "moe"))
        w1 = sb("w1", [D, NE, HID])
        w2 = sb("w2", [P, NE * HALVES, D])
        gate = sb("gate", [D, NE])
        index = sb("index", [P, NE])
        loaded, step, var_ready, iota_made = sem("loaded"), sem("moments_step"), sem("var_ready"), sem("iota_made")
        index_i = sb("index_i", [P, NE], I32)
        with nc.Block() as block:
            @block.sync
            def _(sp):
                sp.dma_start(w1[:, :, :], w1_in).then_inc(loaded, 16)
                sp.dma_start(w2[:, :, :], w2_in.rearrange("(c p) d -> p c d", p=P)).then_inc(loaded, 16)
                sp.dma_start(gate[:, :], gate_in).then_inc(loaded, 16)
                sp.wait_ge(loaded, 48)

            @block.vector
            def _(dve):
                moments(dve, stats6, mean, small, step)
                dve.tensor_tensor(small[:, 0, :], mean[:, :], mean[:, :], ALU.mult).then_inc(var_ready, 1)
                dve.wait_ge(var_ready, 1)
                dve.tensor_tensor(small[:, 1, :], small[:, 0, :], small[:, 3, :], ALU.add).then_inc(var_ready, 1)
                dve.wait_ge(var_ready, 2)
                dve.tensor_scalar(small[:, 2, :], small[:, 1, :], RMS_EPS, None, ALU.add).then_inc(var_ready, 1)
                dve.wait_ge(iota_made, 1)
                dve.tensor_copy(index[:, :], index_i[:, :])

            @block.gpsimd
            def _(pool):
                pool.iota(index_i[:, :], pattern=[[1, NE]], base=0, channel_multiplier=0).then_inc(iota_made, 1)
                pool.wait_ge(var_ready, 3)
                pool.tensor_tensor(rms[:, :], small[:, 2, :], mhalf[:, :], ALU.pow)

        hn = sb("hn", [P, GB, D])
        hT = [sb(f"moe_hT{i}", [D, N]) for i in range(2)]
        logits = sb("moe_logits", [P, GB, NE])
        best = sb("best", [P, GB, NE])
        best_at = sb("best_at", [P, GB, NE], U32)
        best_at_f = sb("best_at_f", [P, GB, NE])
        margin = sb("margin", [P, GB])
        tanh_half = sb("tanh_half", [P, GB])
        gates = sb("gates", [P, 2, GB])
        first_part = sb("first_part", [P, GB, NE])
        second_part = sb("second_part", [P, GB, NE])
        combine = [sb(f"combine{i}", [P, GB, NE]) for i in range(2)]
        RING = 4
        hid = [sb(f"hid{i}", [P, N]) for i in range(RING)]
        prod = [sb(f"prod{i}", [P, GB, D]) for i in range(2)]
        acc = [sb(f"acc{i}", [P, GB, D]) for i in range(2)]
        names = ("h_made h_turned h_copied gated logits_copied best_done index_done index_copied margin_done tanh_done gates_done "
                 "parts_made combined stored x_summed").split()
        s = {name: sem(name) for name in names}
        NC_ = NE * HALVES
        hidden = [sem(f"hidden{i}") for i in range(NC_)]
        activated = [sem(f"activated{i}") for i in range(NC_)]
        expert = [sem(f"expert{e}") for e in range(NE)]
        weighted = [sem(f"weighted{e}") for e in range(NE)]
        summed = [sem(f"summed{e}") for e in range(NE)]
        BANKS = 3
        stored = [sem("stored0"), sem("stored1")]
        def last_in_ring(i, size, n):
            return (i - size, 0) if i >= size else (max(c for c in range(n) if c % size == i % size), 1)

        with nc.Block() as block:
            @block.tensor
            def _(pe):
                def prepare(g, par):
                    wait(pe, s["h_made"], g + 1)
                    wait(pe, s["h_copied"], g)
                    for b in range(GB):
                        tr = pe.transpose(psum[:, 0, b * P:(b + 1) * P], hn[:, b, :], ident[:, :])
                    tr.then_inc(s["h_turned"], 1)
                    wait(pe, s["h_copied"], g + 1)
                    wait(pe, s["logits_copied"], g)
                    for b in range(GB):
                        mm = pe.matmul(psum[:, 1, b * NE:(b + 1) * NE], hT[par][:, b * P:(b + 1) * P], gate[:, :],
                                       start=True, stop=True)
                    mm.then_inc(s["gated"], 1)

                def up(g, par, i):
                    before, back = last_in_ring(i, BANKS, NC_)
                    wait(pe, activated[before], g + 1 - back)
                    e, half = divmod(i, HALVES)
                    pe.matmul(psum[:, 2 + i % BANKS, :], w1[:, e, half * P:(half + 1) * P], hT[par][:, :],
                              start=True, stop=True).then_inc(hidden[i], 1)

                def down(g, e):
                    before, back = last_in_ring(e, 2, NE)
                    wait(pe, weighted[before], g + 1 - back)
                    wait(pe, activated[2 * e + 1], g + 1)
                    for b in range(GB):
                        for half in range(HALVES):
                            i = 2 * e + half
                            mm = pe.matmul(psum[:, 5 + e % 2, b * D:(b + 1) * D], hid[i % RING][:, b * P:(b + 1) * P], w2[:, i, :],
                                           start=(half == 0), stop=(half == HALVES - 1))
                    mm.then_inc(expert[e], 1)

                def body(g, par, final=False):
                    for i in range(NC_):
                        up(g, par, i)
                        if i % 2 == 1 and i >= 3:
                            down(g, (i - 3) // 2)
                        if i == 9 and not final:
                            prepare(g + 1, 1 - par)
                    down(g, NE - 1)

                prepare(0, 0)
                wait(pe, s["h_copied"], 1)
                body(0, 0)
                with pe.Fori(0, NG // 2 - 1) as i:
                    body(2 * i + 1, 1)
                    body(2 * i + 2, 0)
                body(NG - 1, 1, final=True)

            @block.scalar
            def _(act):
                def copy_h(g, par):
                    wait(act, s["h_turned"], g + 1)
                    wait(act, hidden[NC_ - 1], g - 1)
                    act.activation(hT[par][:, :], psum[:, 0, :], ACT.Copy, scale=G2).then_inc(s["h_copied"], 1)

                def squash(g):
                    wait(act, s["margin_done"], g + 1)
                    wait(act, s["gates_done"], g)
                    act.activation(tanh_half[:, :], margin[:, :], ACT.Tanh, scale=0.5).then_inc(s["tanh_done"], 1)

                def body(g, par, final=False):
                    for i in range(NC_):
                        wait(act, hidden[i], g + 1)
                        if i >= RING:
                            wait(act, expert[(i - RING) // 2], g + 1)
                        else:
                            wait(act, expert[(NC_ - RING + i) // 2], g)
                        act.activation(hid[i % RING][:, :], psum[:, 2 + i % BANKS, :], ACT.Silu).then_inc(activated[i], 1)
                        if i == 9 and not final:
                            copy_h(g + 1, 1 - par)
                        if i == 13 and not final:
                            squash(g + 1)

                copy_h(0, 0)
                squash(0)
                body(0, 0)
                with act.Fori(0, NG // 2 - 1) as i:
                    body(2 * i + 1, 1)
                    body(2 * i + 2, 0)
                body(NG - 1, 1, final=True)

            @block.vector
            def _(dve):
                def norm(g):
                    wait(dve, s["h_turned"], g)
                    for b in range(GB):
                        n = g * GB + b
                        i = dve.tensor_scalar(hn[:, b, :], X3[:, entries(n), :].rearrange("p a d -> p (a d)"), rms[:, entries(n)],
                                              None, ALU.mult)
                    i.then_inc(s["h_made"], 1)

                def choose(g):
                    wait(dve, s["gated"], g + 1)
                    dve.tensor_copy(logits[:, :, :], psum[:, 1, 0:GB * NE].rearrange("p (b e) -> p b e", e=NE)).then_inc(s["logits_copied"], 1)
                    wait_apart(dve, s["logits_copied"], g + 1, s["h_made"])
                    for b in range(GB):
                        i = dve.max(best[:, b, :], logits[:, b, :])
                    i.then_inc(s["best_done"], 1)
                    wait_apart(dve, s["best_done"], g + 1, s["h_made"])
                    for b in range(GB):
                        i = dve.max_index(best_at[:, b, :], best[:, b, :], logits[:, b, :])
                    dve.tensor_tensor(margin[:, :], best[:, :, 0], best[:, :, 1], ALU.subtract).then_inc(s["margin_done"], 1)
                    wait(dve, s["margin_done"], g + 1)
                    dve.tensor_copy(best_at_f[:, :, :], best_at[:, :, :]).then_inc(s["index_copied"], 1)

                def weigh(g, par):
                    wait(dve, s["tanh_done"], g + 1)
                    dve.tensor_scalar(gates[:, 0, :], tanh_half[:, :], 0.5, 0.5, ALU.mult, ALU.add)
                    dve.tensor_scalar(gates[:, 1, :], tanh_half[:, :], -0.5, 0.5, ALU.mult, ALU.add).then_inc(s["gates_done"], 1)
                    wait(dve, s["gates_done"], g + 1)
                    wait(dve, s["index_copied"], g + 1)
                    for b in range(GB):
                        dve.tensor_scalar(first_part[:, b, :], index[:, :], best_at_f[:, b, 0:1], gates[:, 0, b:b + 1],
                                          ALU.is_equal, ALU.mult)
                        i = dve.tensor_scalar(second_part[:, b, :], index[:, :], best_at_f[:, b, 1:2], gates[:, 1, b:b + 1],
                                              ALU.is_equal, ALU.mult)
                    i.then_inc(s["parts_made"], 1)
                    wait(dve, s["parts_made"], g + 1)
                    dve.tensor_tensor(combine[par][:, :, :], first_part[:, :, :], second_part[:, :, :], ALU.add).then_inc(s["combined"], 1)

                def body(g, par, final=False):
                    for e in range(NE):
                        wait(dve, expert[e], g + 1)
                        wait(dve, s["combined"], g + 1)
                        before, back = last_in_ring(e, 2, NE)
                        wait(dve, summed[before], g + 1 - back)
                        dve.tensor_tensor(prod[e % 2][:, :, :], psum[:, 5 + e % 2, :].rearrange("p (b d) -> p b d", b=GB),
                                          combine[par][:, :, e:e + 1].broadcast_to([P, GB, D]), ALU.mult).then_inc(weighted[e], 1)
                        if e == 1 and not final:
                            norm(g + 1)
                        if e == 4 and not final:
                            choose(g + 1)
                        if e == 6 and not final:
                            weigh(g + 1, 1 - par)

                norm(0)
                choose(0)
                weigh(0, 0)
                body(0, 0)
                with dve.Fori(0, NG // 2 - 1) as i:
                    body(2 * i + 1, 1)
                    body(2 * i + 2, 0)
                body(NG - 1, 1, final=True)

            @block.gpsimd
            def _(pool):
                def body(g, par, final=False):
                    a = acc[par]
                    xs = entries(g * GB, GB)
                    wait(pool, stored[par], 16 * GB * (g // 2))
                    pool.tensor_tensor(a[:, :, :], X2[:, xs, :], X3[:, xs, :], ALU.add).then_inc(s["x_summed"], 1)
                    wait(pool, s["x_summed"], g + 1)
                    for e in range(NE):
                        wait(pool, weighted[e], g + 1)
                        if e:
                            wait(pool, summed[e - 1], g + 1)
                        pool.tensor_tensor(a[:, :, :], a[:, :, :], prod[e % 2][:, :, :], ALU.add).then_inc(summed[e], 1)

                body(0, 0)
                with pool.Fori(0, NG // 2 - 1) as i:
                    body(2 * i + 1, 1)
                    body(2 * i + 2, 0)
                body(NG - 1, 1)

            @block.sync
            def _(sp):
                def store(g, par):
                    wait(sp, summed[NE - 1], g + 1)
                    for b in range(GB):
                        sp.dma_start(out[entries(g * GB + b)].rearrange("a t d -> (a t) d"), acc[par][:, b, :]).then_inc(stored[par], 16)

                store(0, 0)
                with sp.Fori(0, NG // 2 - 1) as i:
                    store(2 * i + 1, 1)
                    store(2 * i + 2, 0)
                store(NG - 1, 1)
                sp.wait_ge(stored[0], 16 * GB * (NG // 2))
                sp.wait_ge(stored[1], 16 * GB * (NG // 2))


def lay_out(np, i):
    f = lambda a: np.ascontiguousarray(np.asarray(a))
    def pad_wo(w_inT):
        w = np.zeros((4, 4, 32, D), np.float32)
        w[:, :, 0:8, :] = f(w_inT).reshape(4, 4, 8, D)
        return f(w.reshape(4 * P, D))
    cols = np.stack([f(i[n]) for n in ("L0_xattn_ln_x_w", "L0_xattn_ln_x_b", "L0_xattn_ln_l_w", "L0_xattn_ln_l_b")]
                    + [np.concatenate([f(i[n]), f(i[n])]) for n in ("L0_xattn_q_scale", "L0_xattn_k_scale")]
                    + [f(i["L1_ffn_g1"]), f(i["L1_ffn_g2"])], axis=1)
    T = lambda n: f(np.asarray(i[n]).T)
    return {
        "x_in": f(i["x"]), "ctx_in": f(i["ctx_1024"]), "ctxT_in": f(np.transpose(np.asarray(i["ctx_1024"]), (0, 2, 1))),
        "keep_in": f(i["mask_BxS2_bk0"]).reshape(1, B * C),
        "qk_mask_in": f(i["mask_1x1xSxS2_ik0"]).reshape(P, C), "cols_in": f(cols),
        "lnow_in": f(i["L0_xattn_ln_o_w"]).reshape(1, D), "lnob_in": f(i["L0_xattn_ln_o_b"]).reshape(1, D),
        "wq0_in": f(i["L0_xattn_Wq"]), "wkv0_in": f(i["L0_xattn_Wkv"]), "wo0_in": f(i["L0_xattn_Wo"]),
        "wm_in": T("L0_ffn_Wm"), "wp_in": T("L0_ffn_Wp"), "wc1_in": T("L0_ffn_Wc1"), "wc2_in": T("L0_ffn_Wc2"),
        "wq1_in": T("L1_xattn_w_q"), "wk1_in": T("L1_xattn_w_k"), "wv1_in": T("L1_xattn_w_v"),
        "wo1_in": pad_wo(np.asarray(i["L1_xattn_w_o"]).T),
        "wq2_in": f(i["L1_ffn_Wq"]), "wdkv_in": f(i["L1_ffn_Wdkv"]), "wuk_in": f(i["L1_ffn_Wuk"]),
        "wuv_in": f(i["L1_ffn_Wuv"]), "wo2_in": pad_wo(i["L1_ffn_Wo"]),
        "gate_in": f(i["L1_ffn_gate_w"]), "w1_in": f(np.transpose(np.asarray(i["L1_ffn_w1"]), (1, 0, 2))),
        "w2_in": f(i["L1_ffn_w2"]).reshape(8 * 256, D),
    }


def kernel(**inputs):
    import numpy as _np
    import concourse.bacc as _bacc
    from concourse import mybir as _mybir
    from concourse.bass_utils import run_bass_kernel_spmd as _run

    nc = _bacc.Bacc("TRN2", target_bir_lowering=False, num_devices=1)
    arrays = lay_out(_np, inputs)
    args = [nc.dram_tensor(n, a.shape, _mybir.dt.from_np(a.dtype), kind="ExternalInput").ap() for n, a in arrays.items()]
    out = nc.dram_tensor("out_dram", (B, P, D), _mybir.dt.float32, kind="ExternalOutput").ap()
    mega_kernel(nc, *args, out)
    r = _run(nc, [arrays], core_ids=[0])
    return r.results[0]["out_dram"]
```

```python
from contextlib import ExitStack, contextmanager

import concourse.bass as bass
from concourse import mybir

ALU = mybir.AluOpType
ACT = mybir.ActivationFunctionType
AX = mybir.AxisListType
F32 = mybir.dt.float32
BF16 = mybir.dt.bfloat16
I32 = mybir.dt.int32
U32 = mybir.dt.uint32
U8 = mybir.dt.uint8

P = 128
B = 32
D = 128
C = 120
GB = 4
NG = B // GB
LN_EPS = 1e-5
RMS_EPS = 1e-6
F_ITER = 512
F_FULL = 3 * F_ITER
Q4 = F_FULL // 4
NEG_MAX = -3.0e38


def wait(eng, sem, value):
    if isinstance(value, int) and value <= 0:
        return
    eng.wait_ge(sem, value)


@contextmanager
def signals(nc, phase):
    given = []

    def sem(name):
        given.append(nc.alloc_semaphore(f"{phase}_{name}"))
        return given[-1]

    yield sem
    nc.clear_and_free_semaphores(given)
    nc.all_engine_barrier()


def mega_kernel(nc, x_in, ctx_in, ctxT_in, keep_in, qk_mask_in, cols_in, lnow_in, lnob_in, wq0_in, wkv0_in, wo0_in,
                wm_in, wp_in, wc1_in, wc2_in, wq1_in, wk1_in, wv1_in, wo1_in, wq2_in, wdkv_in, wuk_in, wuv_in,
                wo2_in, gate_in, w1_in, w2_in, out, stop_after=9):
    ctx = ExitStack()
    with ctx:
        def sb(name, shape, dt=F32, stack=ctx):
            return stack.enter_context(nc.sbuf_tensor(name, shape, dt))

        X = sb("X", [P, B, D])
        X2 = sb("X2", [P, B, D])
        X3 = sb("X3", [P, B, D])
        stats6 = sb("stats6", [P, B, 6])
        mean = sb("mean", [P, B])
        rstd = sb("rstd", [P, B])
        rms = sb("rms", [P, B])
        mhalf = sb("mhalf", [P, B])
        small = sb("small", [P, 4, B])
        ident = sb("ident", [P, P])
        ident_bf = sb("ident_bf", [P, P], BF16)
        ones = sb("ones", [P, P])
        ones_bf = sb("ones_bf", [P, P], BF16)
        cols = sb("cols", [P, 8])
        LNX_W, LNX_B, LNL_W, LNL_B, QS, KS, G1, G2 = (cols[:, i:i + 1] for i in range(8))
        psum = ctx.enter_context(nc.psum_tensor("psum", [P, 8, 512], F32))

        load_x_and_constants(nc, sb, X, x_in, cols, cols_in, ident, ident_bf, ones, ones_bf, mhalf, stats6)
        if stop_after >= 1:
            l0_attention(nc, psum, X, stats6, mean, rstd, mhalf, small, ident, ident_bf, ones, ones_bf, cols,
                         ctx_in, keep_in, lnow_in, lnob_in, wq0_in, wkv0_in, wo0_in)
        last = X
        if stop_after >= 2:
            l0_ffn(nc, psum, X, X2, X3, stats6, mean, rstd, mhalf, small, ident, ones, wm_in, wp_in, wc1_in, wc2_in)
            last = X2
        if stop_after >= 3:
            attention16(nc, "l1", psum, X2, X2, stats6, mean, rstd, rms, mhalf, small, ident, ident_bf, ones, cols,
                        (wq1_in, wk1_in, wv1_in, wo1_in), ctxT_in, qk_mask_in)
        if stop_after >= 4:
            attention16(nc, "mla", psum, X2, X3, stats6, mean, rstd, rms, mhalf, small, ident, ident_bf, ones, cols,
                        (wq2_in, wdkv_in, wuk_in, wuv_in, wo2_in), None, None)
            last = X3
        if stop_after >= 5:
            moe(nc, psum, X2, X3, stats6, mean, rms, mhalf, small, ident, cols, gate_in, w1_in, w2_in, out)
        else:
            with nc.semaphore("dump") as dump, nc.Block() as block:
                @block.sync
                def _(sp):
                    sp.dma_start(out.rearrange("b t d -> t b d"), last[:, :, :]).then_inc(dump, 16)
                    sp.wait_ge(dump, 16)


def load_x_and_constants(nc, sb, X, x_in, cols, cols_in, ident, ident_bf, ones, ones_bf, mhalf, stats6):
    with ExitStack() as sems, ExitStack() as st:
        sem = sems.enter_context(signals(nc, "load"))
        x_loaded = [sem(f"x_loaded{g}") for g in range(NG)]
        cols_loaded = sem("cols_loaded")
        zeroed = sem("zeroed")
        identity_made = sem("identity_made")
        block = st.enter_context(nc.Block())
        x_view = x_in.rearrange("b t d -> t b d")

        @block.sync
        def _(sp):
            for g in range(NG):
                sp.dma_start(X[:, g * GB:(g + 1) * GB, :], x_view[:, g * GB:(g + 1) * GB, :]).then_inc(x_loaded[g], 16)
            sp.dma_start(cols[:, :], cols_in).then_inc(cols_loaded, 16)
            sp.wait_ge(cols_loaded, 16)

        @block.gpsimd
        def _(pool):
            pool.memset(ident[:, :], 0.0).then_inc(zeroed, 1)
            pool.memset(ident_bf[:, :], 0.0).then_inc(zeroed, 1)
            pool.memset(ones[:, :], 1.0)
            pool.memset(ones_bf[:, :], 1.0)
            pool.memset(mhalf[:, :], -0.5)
            pool.wait_ge(zeroed, 2)
            for m in (ident, ident_bf):
                pool.affine_select(out=m[:, :], in_=m[:, :], compare_op=ALU.not_equal, fill=1.0, base=0,
                                   pattern=[[-1, P]], channel_multiplier=1).then_inc(identity_made, 1)
            pool.wait_ge(identity_made, 2)

        @block.vector
        def _(dve):
            for g in range(NG):
                dve.wait_ge(x_loaded[g], 16)
                for b in range(g * GB, (g + 1) * GB):
                    dve.bn_stats(stats6[:, b, :], X[:, b, :])



def softmax_units(nc, st, new_sem, psum, H, K, width, pt_plan, pv_plan, score, ident, tag):
    def sem(name):
        return [new_sem(f"{name}{u}") for u in range(2)]

    def sb(name, shape, dt=F32):
        return st.enter_context(nc.sbuf_tensor(f"{tag}_{name}", shape, dt))

    HB = H // 2
    n_max = [sb(f"n_max{u}", [P, H]) for u in range(2)]
    sums = [sb(f"sums{u}", [P, H]) for u in range(2)]
    r_sums = [sb(f"r_sums{u}", [P, H]) for u in range(2)]
    r_wide = [sb(f"r_wide{u}", [P, H, width]) for u in range(2)]
    probs = [sb(f"probs{u}", [P, H, K]) for u in range(2)]
    probsT = [sb(f"probsT{u}", [P, 2, 4, P]) for u in range(2)]
    r_spread = sb("r_spread", [P, 2, P])
    outT = sb("outT", [P, 4, P])

    scored = sem("scored")
    max_taken = sem("max_taken")
    exp_done = sem("exp_done")
    sum_inverted = sem("sum_inverted")
    sum_repeated = sem("sum_repeated")
    pt0_turned = sem("pt0_turned")
    pt1_turned = sem("pt1_turned")
    pt0_copied = sem("pt0_copied")
    pt1_copied = sem("pt1_copied")
    r_turned = sem("r_turned")
    r_copied = sem("r_copied")
    pv_done = sem("pv_done")
    out_scaled = sem("out_scaled")
    projected = new_sem("projected")
    projection_taken = new_sem("projection_taken")
    KN = [pt_plan[0][0][2], pt_plan[1][0][2]]

    def pe_scores(pe, n, u, bank):
        if bank == 0:
            wait(pe, exp_done[u], n)
        s = score(pe, n, u, bank)
        if bank == 1:
            s.then_inc(scored[u], 1)

    def dve_max(dve, n, u):
        wait(dve, scored[u], n + 1)
        wait(dve, exp_done[u], n)
        dve.tensor_reduce(n_max[u][:, :].rearrange("p (c j) -> p c j", c=2),
                          psum[:, 2 * u:2 * u + 2, 0:HB * K].rearrange("p c (j k) -> p c j k", k=K), AX.X, ALU.max,
                          negate=True).then_inc(max_taken[u], 1)

    def act_exp(act, n, u):
        wait(act, max_taken[u], n + 1)
        wait(act, pt1_turned[u], n)
        wait(act, sum_inverted[u], n)
        for h in range(H):
            e = act.activation(probs[u][:, h, :], psum[:, 2 * u + h // HB, (h % HB) * K:(h % HB + 1) * K], ACT.Exp,
                               bias=n_max[u][:, h:h + 1], accum_out=sums[u][:, h:h + 1])
        e.then_inc(exp_done[u], 1)

    def dve_invert(dve, n, u):
        wait(dve, exp_done[u], n + 1)
        dve.reciprocal(r_sums[u][:, :], sums[u][:, :]).then_inc(sum_inverted[u], 1)
        wait(dve, sum_inverted[u], n + 1)
        wait(dve, r_turned[u], n)
        dve.tensor_copy(r_wide[u][:, :, :], r_sums[u][:, :].unsqueeze(2).broadcast_to([P, H, width])).then_inc(sum_repeated[u], 1)

    def pe_turn_probs0(pe, n, u):
        wait(pe, exp_done[u], n + 1)
        wait(pe, r_copied[1 - u], n if u == 0 else n + 1)
        for j, (h, k0, kn) in enumerate(pt_plan[0]):
            t = pe.transpose(psum[0:kn, 4, j * P:(j + 1) * P], probs[u][:, h, k0:k0 + kn], ident[:, :])
        t.then_inc(pt0_turned[u], 1)

    def pe_turn_probs1(pe, n, u):
        if u == 0:
            wait(pe, projection_taken, n)
        else:
            wait(pe, out_scaled[0], n + 1)
        for j, (h, k0, kn) in enumerate(pt_plan[1]):
            t = pe.transpose(psum[0:kn, 5, j * P:(j + 1) * P], probs[u][:, h, k0:k0 + kn], ident[:, :])
        t.then_inc(pt1_turned[u], 1)

    def act_copy_pt0(act, n, u):
        wait(act, pt0_turned[u], n + 1)
        wait(act, pv_done[u], n)
        act.copy(probsT[u][0:KN[0], 0, :, :], psum[0:KN[0], 4, :].rearrange("k (j q) -> k j q", j=4)).then_inc(pt0_copied[u], 1)

    def dve_copy_pt1(dve, n, u):
        wait(dve, pt1_turned[u], n + 1)
        wait(dve, pv_done[u], n)
        dve.tensor_copy(probsT[u][0:KN[1], 1, :, :], psum[0:KN[1], 5, :].rearrange("k (j q) -> k j q", j=4)).then_inc(pt1_copied[u], 1)

    def pe_turn_sums(pe, n, u):
        wait(pe, sum_repeated[u], n + 1)
        wait(pe, pt0_copied[u], n + 1)
        hb = P // width
        for b in range(2):
            t = pe.transpose(psum[:, 4, b * P:(b + 1) * P],
                             r_wide[u][:, b * hb:(b + 1) * hb, :].rearrange("p h w -> p (h w)"), ident[:, :])
        t.then_inc(r_turned[u], 1)

    def act_copy_sums(act, n, u):
        wait(act, r_turned[u], n + 1)
        wait(act, out_scaled[1 - u], n if u == 0 else n + 1)
        act.copy(r_spread[:, :, :], psum[:, 4, 0:2 * P].rearrange("p (b q) -> p b q", b=2)).then_inc(r_copied[u], 1)

    def dve_copy_sums(dve, n, u):
        wait(dve, r_turned[u], n + 1)
        wait(dve, out_scaled[1 - u], n if u == 0 else n + 1)
        dve.tensor_copy(r_spread[:, :, :], psum[:, 4, 0:2 * P].rearrange("p (b q) -> p b q", b=2)).then_inc(r_copied[u], 1)

    def pe_pv(pe, n, u, v_of):
        wait(pe, pt0_copied[u], n + 1)
        wait(pe, pt1_copied[u], n + 1)
        for j, row, blk, parts in pv_plan:
            for i, (c, slot, kn) in enumerate(parts):
                mm = pe.matmul(psum[row:row + width, 5, blk * P:(blk + 1) * P], v_of(u * H + j, i), probsT[u][0:kn, c, slot, :],
                               start=(i == 0), stop=(i == len(parts) - 1), skip_group_check=True)
        mm.then_inc(pv_done[u], 1)

    def dve_scale(dve, n, u):
        wait(dve, pv_done[u], n + 1)
        wait(dve, r_copied[u], n + 1)
        if u == 0:
            wait(dve, projected, n)
        dve.tensor_tensor(outT[:, 2 * u:2 * u + 2, :], psum[:, 5, 0:256].rearrange("p (b q) -> p b q", b=2), r_spread[:, :, :],
                          ALU.mult).then_inc(out_scaled[u], 1)

    def pe_project(pe, n, wo):
        wait(pe, out_scaled[1], n + 1)
        for c in range(4):
            mm = pe.matmul(psum[:, 5, 0:D], outT[:, c, :], wo[:, c, :], start=(c == 0), stop=(c == 3))
        mm.then_inc(projected, 1)

    return dict(locals())


def run_entries(eng, body):
    body(0, 0, first=True)
    with eng.Fori(0, B // 2 - 2) as i:
        body(2 * i + 1, 1)
        body(2 * i + 2, 0)
    body(B - 3, 1)
    body(B - 2, 0, after=False)
    body(B - 1, 1, after=False, next_=False)


def l0_attention(nc, psum, X, stats6, mean, rstd, mhalf, small, ident, ident_bf, ones, ones_bf, cols,
                 ctx_in, keep_in, lnow_in, lnob_in, wq_in, wkv_in, wo_in):
    H, HD = 8, 64
    K = C + P
    INNER = H * HD
    LNX_W, LNX_B, LNL_W, LNL_B, QS, KS = (cols[:, i:i + 1] for i in range(6))
    with ExitStack() as sems, ExitStack() as st:
        def sb(name, shape, dt=F32):
            return st.enter_context(nc.sbuf_tensor(name, shape, dt))

        sem = sems.enter_context(signals(nc, "l0"))
        CT = sb("CT", [P, B, D])
        keep8 = sb("keep8", [1, B * C], U8)
        keep_row = sb("keep_row", [P, B, K], BF16)
        stats6_c = sb("stats6_c", [P, B, 6])
        mean_c = sb("mean_c", [P, B])
        small_c = sb("small_c", [P, 4, B])
        rstd_c = sb("rstd_c", [P, B])
        wq = sb("wq", [D, INNER])
        wkv = sb("wkv", [D, 2 * INNER])
        wo = sb("wo", [P, 4, D])
        lnow = sb("lnow", [P, D])
        lnob = sb("lnob", [P, D])
        qk_scale = sb("qk_scale", [P, 1])
        first_row = sb("first_row", [P, P], BF16)

        loaded = sem("l0_loaded")
        keep_loaded = sem("keep_loaded")
        c_loaded = [sem(f"c_loaded{g}") for g in range(NG)]
        const_step = sem("const_step")
        row_zeroed = sem("row_zeroed")
        c_stats = sem("c_stats")
        x_moments_step = sem("x_moments_step")
        c_moments_step = sem("c_moments_step")
        var_ready = sem("var_ready")
        pow_done = sem("pow_done")
        scale_done = sem("scale_done")
        with nc.Block() as block:
            @block.sync
            def _(sp):
                c_view = ctx_in.rearrange("b t d -> t b d")
                for g in range(NG):
                    sp.dma_start(CT[0:C, g * GB:(g + 1) * GB, :], c_view[:, g * GB:(g + 1) * GB, :]).then_inc(c_loaded[g], 16)
                sp.dma_start(keep8[:, :], keep_in).then_inc(keep_loaded, 16)
                sp.dma_start(wq[:, :], wq_in).then_inc(loaded, 16)
                sp.dma_start(wkv[:, :], wkv_in).then_inc(loaded, 16)
                sp.dma_start(wo[:, :, :], wo_in.rearrange("(c p) d -> p c d", p=P)).then_inc(loaded, 16)
                sp.dma_start(lnow[:, :], lnow_in.broadcast_to([P, D])).then_inc(loaded, 16)
                sp.dma_start(lnob[:, :], lnob_in.broadcast_to([P, D])).then_inc(loaded, 16)
                sp.wait_ge(loaded, 80)

            @block.gpsimd
            def _(pool):
                pool.memset(first_row[:, :], 0.0).then_inc(row_zeroed, 1)
                pool.wait_ge(row_zeroed, 1)
                pool.memset(first_row[0:1, :], 1.0)
                pool.wait_ge(var_ready, 2)
                pool.tensor_tensor(rstd[:, :], small[:, 0, :], mhalf[:, :], ALU.pow).then_inc(pow_done, 1)
                pool.tensor_tensor(rstd_c[0:C, :], small_c[0:C, 0, :], mhalf[0:C, :], ALU.pow).then_inc(pow_done, 1)
                pool.wait_ge(var_ready, 5)
                pool.tensor_tensor(small[:, 1, :], small[:, 2, :], mhalf[:, :], ALU.pow).then_inc(pow_done, 1)

            @block.vector
            def _(dve):
                dve.memset(keep_row[:, :, :].bitcast(U32), 0).then_inc(const_step, 1)
                for g in range(NG):
                    dve.wait_ge(c_loaded[g], 16)
                    for b in range(g * GB, (g + 1) * GB):
                        dve.bn_stats(stats6_c[0:C, b, :], CT[0:C, b, :]).then_inc(c_stats, 1)
                moments(dve, stats6, mean, small, x_moments_step)
                dve.wait_ge(c_stats, B)
                moments(dve, stats6_c[0:C], mean_c[0:C], small_c[0:C], c_moments_step)
                dve.tensor_scalar(small[:, 0, :], small[:, 3, :], LN_EPS, None, ALU.add).then_inc(var_ready, 1)
                dve.tensor_scalar(small_c[0:C, 0, :], small_c[0:C, 3, :], LN_EPS, None, ALU.add).then_inc(var_ready, 1)
                dve.wait_ge(keep_loaded, 16)
                dve.wait_ge(const_step, 1)
                dve.tensor_scalar(keep_row[0:1, :, 0:C], keep8[:, :].rearrange("a (b c) -> a b c", b=B), 1.0, -NEG_MAX,
                                  ALU.subtract, ALU.mult)
                dve.tensor_scalar(qk_scale[:, :], QS, KS, float(HD) ** 0.5, ALU.mult, ALU.mult).then_inc(const_step, 1)
                dve.wait_ge(pow_done, 2)
                dve.tensor_tensor(small[:, 2, :], rstd[:, :], rstd[:, :], ALU.mult).then_inc(var_ready, 1)
                dve.wait_ge(var_ready, 3)
                dve.tensor_tensor(small[:, 2, :], small[:, 2, :], small[:, 3, :], ALU.mult).then_inc(var_ready, 1)
                dve.wait_ge(var_ready, 4)
                dve.tensor_scalar(small[:, 2, :], small[:, 2, :], LN_EPS, None, ALU.add).then_inc(var_ready, 1)
                dve.wait_ge(pow_done, 3)
                dve.tensor_tensor(rstd[:, :], rstd[:, :], small[:, 1, :], ALU.mult).then_inc(scale_done, 1)

        ln_x = sb("ln_x", [P, D])
        ln_c = sb("ln_c", [P, D])
        kvT = sb("kvT", [P, K])
        qk = sb("qk", [P, 3, INNER])
        sq = sb("sq", [P, 3, INNER])
        qkn = sb("qkn", [P, 3, INNER])
        ss = sb("ss", [P, 3 * H])
        ssm = sb("ssm", [P, 3 * H])
        r_norm = sb("r_norm", [P, 3 * H])
        QZ = [sb(f"QZ{i}", [P, H, P]) for i in range(2)]
        KT = [sb(f"KT{i}", [P, 4, K]) for i in range(2)]
        VC = [sb(f"VC{i}", [P, INNER]) for i in range(2)]
        VL = [sb(f"VL{i}", [P, INNER]) for i in range(2)]
        y = sb("y", [P, D])
        y_stat = sb("y_stat", [P, 6])
        y_sums = sb("y_sums", [P, 2])
        y_diff = sb("y_diff", [P, 1])
        y_mean = sb("y_mean", [P, 1])
        y_within = sb("y_within", [P, 1])
        y_between = sb("y_between", [P, 1])
        y_var = sb("y_var", [P, 1])
        y_rstd = sb("y_rstd", [P, 1])
        y_norm = sb("y_norm", [P, D])
        y_w = sb("y_w", [P, D])
        y_wb = sb("y_wb", [P, D])

        names = ("ln_made ln_turned kvT_made squared qT_scaled q_proj q_copied kc_proj kc_copied kl_proj kl_copied vc_proj vc_copied "
                 "vl_proj vl_copied ss_summed ss_ready norm_inverted normed qT_turned qT_copied kcT_turned kcT_copied "
                 "klT_turned klT_copied y_stats y_aggr y_parts y_var_ready y_inverted y_normed y_weighted y_biased x_added "
                 "x_stats buffers_zeroed").split()
        s = {name: sem(name) for name in names}
        cell = {}

        def scale_qT(eng, par, half):
            r = slice(64 * half, 64 * half + 64)
            dst, src = QZ[par][r, half:H:2, :], psum[r, 6, :].rearrange("p (c q) -> p c q", c=4)
            if half == 0:
                return eng.activation(dst, src, ACT.Copy, scale=qk_scale[r, :])
            return eng.tensor_scalar(dst, src, qk_scale[r, :], None, ALU.mult)

        def score(pe, n, u, c):
            par = cell["par"]
            wait(pe, s["qT_copied"], n + 1)
            wait(pe, s["qT_scaled"], n + 1)
            wait(pe, s["kcT_copied"], n + 1)
            wait(pe, s["klT_copied"], n + 1)
            pe.matmul(psum[:, 2 * u + c, 0:2 * K], first_row[:, :], keep_row[:, entries(n), :].broadcast_to([P, 2, K]),
                      start=True, stop=False, skip_group_check=True)
            for j in range(2):
                h = 4 * u + 2 * c + j
                mm = pe.matmul(psum[:, 2 * u + c, j * K:(j + 1) * K], QZ[par][:, h, :], KT[par][:, h // 2, :],
                               start=False, stop=True, skip_group_check=True)
            return mm

        pt_plan = ([(j, 0, C) for j in range(4)], [(j, C, P) for j in range(4)])
        pv_plan = [(j, HD * (j % 2), j // 2, [(0, j, C), (1, j, P)]) for j in range(4)]
        t = softmax_units(nc, st, sem, psum, 4, K, HD, pt_plan, pv_plan, score, ident, "l0")

        with nc.Block() as block:
            @block.tensor
            def _(pe):
                def values_c(m):
                    wait(pe, s["klT_copied"], m)
                    pe.matmul(psum[0:C, 6, :], kvT[:, 0:C], wkv[:, INNER:], start=True, stop=True).then_inc(s["vc_proj"], 1)

                def values_x(m):
                    wait(pe, s["kcT_copied"], m)
                    pe.matmul(psum[:, 7, :], kvT[:, C:K], wkv[:, INNER:], start=True, stop=True).then_inc(s["vl_proj"], 1)

                def turn_inputs(m):
                    wait(pe, s["ln_made"], m + 1)
                    wait(pe, s["vc_copied"], m)
                    pe.transpose(psum[:, 6, 0:C], ln_c[0:C, :], ident[0:C, 0:C])
                    pe.transpose(psum[:, 6, P:2 * P], ln_x[:, :], ident[:, :]).then_inc(s["ln_turned"], 1)

                def project_q_kc(m):
                    wait(pe, s["kvT_made"], m + 1)
                    wait(pe, s["vl_copied"], m)
                    pe.matmul(psum[:, 7, :], kvT[:, C:K], wq[:, :], start=True, stop=True).then_inc(s["q_proj"], 1)
                    pe.matmul(psum[0:C, 6, :], kvT[:, 0:C], wkv[:, 0:INNER], start=True, stop=True).then_inc(s["kc_proj"], 1)

                def project_kl(m):
                    wait(pe, s["q_copied"], m + 1)
                    pe.matmul(psum[:, 7, :], kvT[:, C:K], wkv[:, 0:INNER], start=True, stop=True).then_inc(s["kl_proj"], 1)

                def turn_q_kc(m, others):
                    wait(pe, s["normed"], m + 1)
                    wait(pe, s["kc_copied"], m + 1 + others)
                    for c in range(4):
                        tr = pe.transpose(psum[:, 6, c * P:(c + 1) * P], qkn[:, 0, c * P:(c + 1) * P], ident[:, :])
                    tr.then_inc(s["qT_turned"], 1)
                    wait(pe, s["kl_copied"], m + 1 + others)
                    for c in range(4):
                        tr = pe.transpose(psum[:, 7, c * C:(c + 1) * C], qkn[0:C, 1, c * P:(c + 1) * P], ident[0:C, 0:C])
                    tr.then_inc(s["kcT_turned"], 1)

                def turn_kl(m):
                    wait(pe, s["qT_copied"], m + 1)
                    wait(pe, s["qT_scaled"], m + 1)
                    for c in range(4):
                        tr = pe.transpose(psum[:, 6, c * P:(c + 1) * P], qkn[:, 2, c * P:(c + 1) * P], ident[:, :])
                    tr.then_inc(s["klT_turned"], 1)

                def pv(n, u, par):
                    t["pe_pv"](pe, n, u, lambda h, i: (VC[par][0:C, h * HD:(h + 1) * HD], VL[par][:, h * HD:(h + 1) * HD])[i])

                def scores(n, u, par, banks=(0, 1)):
                    cell["par"] = par
                    for bank in banks:
                        t["pe_scores"](pe, n, u, bank)

                def body(n, par, first=False, next_=True, after=True):
                    if not first:
                        t["pe_project"](pe, n - 1, wo)
                    if next_:
                        values_c(n + 1)
                    t["pe_turn_probs0"](pe, n, 0)
                    t["pe_turn_probs1"](pe, n, 0)
                    if next_:
                        values_x(n + 1)
                    if after:
                        turn_inputs(n + 2)
                    t["pe_turn_sums"](pe, n, 0)
                    pv(n, 0, par)
                    if after:
                        project_q_kc(n + 2)
                    t["pe_turn_probs0"](pe, n, 1)
                    if after:
                        project_kl(n + 2)
                    t["pe_turn_probs1"](pe, n, 1)
                    if next_:
                        turn_q_kc(n + 1, others=after)
                    t["pe_turn_sums"](pe, n, 1)
                    if next_:
                        turn_kl(n + 1)
                    pv(n, 1, par)
                    if next_:
                        scores(n + 1, 0, 1 - par)
                        scores(n + 1, 1, 1 - par)

                wait(pe, s["buffers_zeroed"], 2)
                turn_inputs(0)
                project_q_kc(0)
                project_kl(0)
                turn_q_kc(0, others=False)
                turn_kl(0)
                wait(pe, s["klT_copied"], 1)
                wait(pe, s["kcT_copied"], 1)
                values_c(0)
                values_x(0)
                scores(0, 0, 0)
                scores(0, 1, 0)
                turn_inputs(1)
                project_q_kc(1)
                project_kl(1)
                wait(pe, s["kc_copied"], 2)
                wait(pe, s["kl_copied"], 2)
                run_entries(pe, body)
                t["pe_project"](pe, B - 1, wo)

            @block.scalar
            def _(act):
                def copy_values_c(m, par):
                    wait(act, s["vc_proj"], m + 1)
                    wait(act, t["pv_done"][1], m - 1)
                    act.copy(VC[par][0:C, :], psum[0:C, 6, :]).then_inc(s["vc_copied"], 1)

                def copy_values_x(m, par):
                    wait(act, s["vl_proj"], m + 1)
                    act.copy(VL[par][:, :], psum[:, 7, :]).then_inc(s["vl_copied"], 1)

                def make_kvT(m):
                    wait(act, s["ln_turned"], m + 1)
                    wait(act, s["vl_proj"], m)
                    act.activation(kvT[:, 0:C], psum[:, 6, 0:C], ACT.Identity, bias=LNX_B, scale=LNX_W)
                    act.activation(kvT[:, C:K], psum[:, 6, P:2 * P], ACT.Identity, bias=LNL_B,
                                   scale=LNL_W).then_inc(s["kvT_made"], 1)

                def copy_qk(m):
                    wait(act, s["normed"], m)
                    for i, (proj, copied, bank, rows) in enumerate((("q_proj", "q_copied", 7, P), ("kc_proj", "kc_copied", 6, C),
                                                                    ("kl_proj", "kl_copied", 7, P))):
                        wait(act, s[proj], m + 1)
                        act.copy(qk[0:rows, i, :], psum[0:rows, bank, :]).then_inc(s[copied], 1)

                def square_qk(m):
                    wait(act, s["kl_copied"], m + 1)
                    wait(act, s["ss_summed"], m)
                    act.activation(sq[:, :, :], qk[:, :, :], ACT.Square).then_inc(s["squared"], 1)

                def copy_qT(m, par):
                    wait(act, s["qT_turned"], m + 1)
                    wait(act, t["scored"][1], m - 1)
                    scale_qT(act, par, 0).then_inc(s["qT_copied"], 1)

                def take_projection(n):
                    wait(act, t["projected"], n + 1)
                    wait(act, s["y_normed"], n)
                    act.copy(y[:, :], psum[:, 5, 0:D]).then_inc(t["projection_taken"], 1)

                def body(n, par, first=False, next_=True, after=True):
                    if not first:
                        take_projection(n - 1)
                    if next_:
                        copy_values_c(n + 1, 1 - par)
                    t["act_copy_pt0"](act, n, 0)
                    if next_:
                        copy_values_x(n + 1, 1 - par)
                    if after:
                        make_kvT(n + 2)
                    t["act_copy_sums"](act, n, 0)
                    t["act_exp"](act, n, 1)
                    if after:
                        copy_qk(n + 2)
                    t["act_copy_pt0"](act, n, 1)
                    if next_:
                        copy_qT(n + 1, 1 - par)
                    t["act_copy_sums"](act, n, 1)
                    if after:
                        square_qk(n + 2)
                    if next_:
                        t["act_exp"](act, n + 1, 0)

                wait(act, s["buffers_zeroed"], 4)
                make_kvT(0)
                copy_qk(0)
                square_qk(0)
                copy_qT(0, 0)
                copy_values_c(0, 0)
                copy_values_x(0, 0)
                t["act_exp"](act, 0, 0)
                make_kvT(1)
                copy_qk(1)
                square_qk(1)
                run_entries(act, body)
                take_projection(B - 1)

            @block.vector
            def _(dve):
                def norm_inputs(m):
                    wait(dve, s["ln_turned"], m)
                    dve.tensor_scalar(ln_x[:, :], X[:, entries(m), :].rearrange("p a d -> p (a d)"), mean[:, entries(m)], rstd[:, entries(m)],
                                      ALU.subtract, ALU.mult)
                    dve.tensor_scalar(ln_c[0:C, :], CT[0:C, entries(m), :].rearrange("p a d -> p (a d)"), mean_c[0:C, entries(m)],
                                      rstd_c[0:C, entries(m)], ALU.subtract, ALU.mult).then_inc(s["ln_made"], 1)

                def sum_squares(m):
                    wait(dve, s["squared"], m + 1)
                    dve.tensor_reduce(ss[:, :], sq[:, :, :].rearrange("p a (h d) -> p (a h) d", d=HD), AX.X,
                                      ALU.add).then_inc(s["ss_summed"], 1)
                    wait(dve, s["ss_summed"], m + 1)
                    wait(dve, s["norm_inverted"], m)
                    dve.tensor_scalar(ssm[:, :], ss[:, :], 1e-24, None, ALU.max).then_inc(s["ss_ready"], 1)

                def copy_qT(m, par):
                    wait(dve, s["qT_turned"], m + 1)
                    wait(dve, t["scored"][1], m - 1)
                    scale_qT(dve, par, 1).then_inc(s["qT_scaled"], 1)

                def copy_kc(m, par):
                    wait(dve, s["kcT_turned"], m + 1)
                    wait(dve, t["scored"][1], m - 1)
                    dve.tensor_copy(KT[par][:, :, 0:C], psum[:, 7, 0:4 * C].rearrange("p (c k) -> p c k", c=4)).then_inc(s["kcT_copied"], 1)

                def copy_kl(m, par):
                    wait(dve, s["klT_turned"], m + 1)
                    dve.tensor_copy(KT[par][:, :, C:K], psum[:, 6, :].rearrange("p (c k) -> p c k", c=4)).then_inc(s["klT_copied"], 1)

                def y_moments(n):
                    wait(dve, t["projection_taken"], n + 1)
                    dve.bn_stats(y_stat[:, :], y[:, :]).then_inc(s["y_stats"], 1)
                    wait(dve, s["y_stats"], n + 1)
                    dve.tensor_tensor(y_sums[:, :], y_stat[:, 1:3], y_stat[:, 4:6], ALU.add)
                    dve.tensor_tensor(y_diff[:, :], y_stat[:, 1:2], y_stat[:, 4:5], ALU.subtract).then_inc(s["y_aggr"], 1)
                    wait(dve, s["y_aggr"], n + 1)
                    dve.tensor_scalar(y_mean[:, :], y_sums[:, 0:1], 0.5, None, ALU.mult)
                    dve.tensor_scalar(y_within[:, :], y_sums[:, 1:2], 1.0 / D, LN_EPS, ALU.mult, ALU.add)
                    dve.scalar_tensor_tensor(y_between[:, :], y_diff[:, :], 0.25, y_diff[:, :], ALU.mult,
                                             ALU.mult).then_inc(s["y_parts"], 1)
                    wait(dve, s["y_parts"], n + 1)
                    wait(dve, s["y_inverted"], n)
                    dve.tensor_tensor(y_var[:, :], y_within[:, :], y_between[:, :], ALU.add).then_inc(s["y_var_ready"], 1)

                def y_normalize(n):
                    wait(dve, s["y_inverted"], n + 1)
                    wait(dve, s["y_weighted"], n)
                    dve.tensor_scalar(y_norm[:, :], y[:, :], y_mean[:, :], y_rstd[:, :], ALU.subtract,
                                      ALU.mult).then_inc(s["y_normed"], 1)

                def x_moments(n):
                    wait_apart(dve, s["x_added"], n + 1, s["buffers_zeroed"])
                    dve.bn_stats(stats6[:, entries(n), :].rearrange("p a d -> p (a d)"),
                                 X[:, entries(n), :].rearrange("p a d -> p (a d)")).then_inc(s["x_stats"], 1)

                def body(n, par, first=False, next_=True, after=True):
                    if not first:
                        t["dve_scale"](dve, n - 1, 1)
                    if after:
                        norm_inputs(n + 2)
                    t["dve_invert"](dve, n, 0)
                    t["dve_max"](dve, n, 1)
                    t["dve_copy_pt1"](dve, n, 0)
                    if not first:
                        y_moments(n - 1)
                    t["dve_scale"](dve, n, 0)
                    t["dve_invert"](dve, n, 1)
                    if not first:
                        y_normalize(n - 1)
                    t["dve_copy_pt1"](dve, n, 1)
                    if next_:
                        copy_qT(n + 1, 1 - par)
                        copy_kc(n + 1, 1 - par)
                        copy_kl(n + 1, 1 - par)
                    if not first:
                        x_moments(n - 1)
                    if after:
                        sum_squares(n + 2)
                    if next_:
                        t["dve_max"](dve, n + 1, 0)

                for q in range(2):
                    dve.memset(QZ[q][:, :, :], 0.0).then_inc(s["buffers_zeroed"], 1)
                dve.memset(sq[:, :, :], 1.0).then_inc(s["buffers_zeroed"], 1)
                dve.memset(qk[:, :, :], 1.0).then_inc(s["buffers_zeroed"], 1)
                norm_inputs(0)
                sum_squares(0)
                copy_qT(0, 0)
                copy_kc(0, 0)
                copy_kl(0, 0)
                t["dve_max"](dve, 0, 0)
                norm_inputs(1)
                sum_squares(1)
                run_entries(dve, body)
                t["dve_scale"](dve, B - 1, 1)
                y_moments(B - 1)
                y_normalize(B - 1)
                x_moments(B - 1)

            @block.gpsimd
            def _(pool):
                def norm_qk(m):
                    wait(pool, s["ss_ready"], m + 1)
                    pool.tensor_tensor(r_norm[:, :], ssm[:, :], mhalf[:, 0:3 * H], ALU.pow).then_inc(s["norm_inverted"], 1)
                    wait(pool, s["norm_inverted"], m + 1)
                    wait(pool, s["klT_turned"], m)
                    pool.tensor_tensor(qkn[:, :, :].rearrange("p a (h d) -> p (a h) d", d=HD),
                                       qk[:, :, :].rearrange("p a (h d) -> p (a h) d", d=HD),
                                       r_norm[:, :].unsqueeze(2).broadcast_to([P, 3 * H, HD]), ALU.mult).then_inc(s["normed"], 1)

                def finish(n):
                    wait(pool, s["y_var_ready"], n + 1)
                    pool.tensor_tensor(y_rstd[:, :], y_var[:, :], mhalf[:, 0:1], ALU.pow).then_inc(s["y_inverted"], 1)

                def add(n):
                    wait(pool, s["y_normed"], n + 1)
                    pool.tensor_tensor(y_w[:, :], y_norm[:, :], lnow[:, :], ALU.mult).then_inc(s["y_weighted"], 1)
                    wait(pool, s["y_weighted"], n + 1)
                    pool.tensor_tensor(y_wb[:, :], y_w[:, :], lnob[:, :], ALU.add).then_inc(s["y_biased"], 1)
                    wait(pool, s["y_biased"], n + 1)
                    xs = X[:, entries(n), :].rearrange("p a d -> p (a d)")
                    pool.tensor_tensor(xs, xs, y_wb[:, :], ALU.add).then_inc(s["x_added"], 1)

                def body(n, par, first=False, next_=True, after=True):
                    if not first:
                        finish(n - 1)
                        add(n - 1)
                    if after:
                        norm_qk(n + 2)

                wait(pool, s["buffers_zeroed"], 4)
                norm_qk(0)
                norm_qk(1)
                run_entries(pool, body)
                finish(B - 1)
                add(B - 1)


def l0_ffn(nc, psum, X, X2, XN, stats6, mean, rstd, mhalf, small, ident, ones, wm_in, wp_in, wc1_in, wc2_in):
    with ExitStack() as sems, ExitStack() as st:
        def sb(name, shape, dt=F32):
            return st.enter_context(nc.sbuf_tensor(name, shape, dt))

        wm = sb("wm", [D, F_FULL])
        wp = sb("wp", [P, F_FULL // P, D])
        wc1 = sb("wc1", [D, 32])
        wc2 = sb("wc2", [32, F_FULL])
        pooledT = sb("pooledT", [D, B])
        same_entry = sb("same_entry", [P, P])
        earlier = sb("earlier", [P, P])
        history = sb("history", [P, Q4])
        maskT = sb("maskT", [P, 3, P])
        done = sb("done", [P, 1], I32)
        bufs = dict(
            zn=sb("zn", [P, GB, D]), zT=sb("zT", [D, GB * P]), hT=[sb(f"hT{i}", [P, GB * P]) for i in range(4)],
            yT=sb("yT", [D, GB * P]), pool4=sb("pool4", [D, GB]))

        with signals(nc, "ffn") as sem:
            var_ready, weights, router_consts = sem("var_ready"), sem("weights"), sem("router_consts")
            powed, moments_step = sem("powed"), sem("moments_step")
            with nc.Block() as block:
                @block.sync
                def _(sp):
                    sp.dma_start(wm[:, :], wm_in).then_inc(weights, 16)
                    sp.dma_start(wp[:, :, :], wp_in.rearrange("(c p) d -> p c d", p=P)).then_inc(weights, 16)
                    sp.dma_start(wc1[:, :], wc1_in).then_inc(weights, 16)
                    sp.dma_start(wc2[:, :], wc2_in).then_inc(weights, 16)
                    sp.wait_ge(weights, 64)

                @block.vector
                def _(dve):
                    moments(dve, stats6, mean, small, moments_step)
                    dve.tensor_scalar(small[:, 0, :], small[:, 3, :], LN_EPS, None, ALU.add).then_inc(var_ready, 1)
                    dve.memset(done[:, :], 0)
                    dve.memset(history[:, :], 0.0).then_inc(moments_step, 1)
                    dve.wait_ge(moments_step, 7)
                    dve.memset(history[0:32, :], 1.0)
                    dve.memset(history[32:64, 0:F_ITER - Q4], 1.0)

                @block.gpsimd
                def _(pool):
                    pool.memset(same_entry[:, :], 0.0).then_inc(router_consts, 1)
                    pool.memset(earlier[:, :], 0.0).then_inc(router_consts, 1)
                    pool.wait_ge(var_ready, 1)
                    pool.tensor_tensor(rstd[:, :], small[:, 0, :], mhalf[:, :], ALU.pow).then_inc(powed, 1)
                    n = 2
                    for q in range(4):
                        pool.wait_ge(router_consts, n)
                        v = same_entry[:, :].rearrange("p (a c) -> p a c", a=4)
                        pool.affine_select(out=v, in_=v, compare_op=ALU.not_equal, fill=1.0, base=-32 * q,
                                           pattern=[[0, 4], [-1, 32]], channel_multiplier=1).then_inc(router_consts, 1)
                        n += 1
                        if q < 3:
                            v = earlier[:, 32 * (q + 1):].rearrange("p (a c) -> p a c", a=3 - q)
                            pool.affine_select(out=v, in_=v, compare_op=ALU.not_equal, fill=1.0, base=-32 * q,
                                               pattern=[[0, 3 - q], [-1, 32]], channel_multiplier=1).then_inc(router_consts, 1)
                            n += 1
                    pool.wait_ge(router_consts, n)

        ffn_step(nc, psum, bufs, X, X, X2, XN, stats6, mean, rstd, wm, wp, None, pooledT, ident, None, 1)
        route(nc, psum, pooledT, wc1, wc2, same_entry, earlier, history, maskT, done, ident, ones, None, 1)
        for step in (2, 3):
            ffn_step(nc, psum, bufs, XN, X, X2, XN, stats6, None, None, wm, wp, maskT, pooledT, ident, done, step)
            if step == 2:
                route(nc, psum, pooledT, wc1, wc2, same_entry, earlier, history, maskT, done, ident, ones, done, step)


def moments(dve, stats6, mean, small, step):
    m_even, v_even, m_odd, v_odd = (stats6[:, :, i] for i in (1, 2, 4, 5))
    dve.tensor_tensor(small[:, 0, :], m_even, m_odd, ALU.add)
    dve.tensor_tensor(small[:, 1, :], m_even, m_odd, ALU.subtract)
    dve.tensor_tensor(small[:, 2, :], v_even, v_odd, ALU.add).then_inc(step, 3)
    dve.wait_ge(step, 3)
    dve.tensor_scalar(mean[:, :], small[:, 0, :], 0.5, None, ALU.mult).then_inc(step, 1)
    dve.scalar_tensor_tensor(small[:, 3, :], small[:, 1, :], 0.25, small[:, 1, :], ALU.mult, ALU.mult).then_inc(step, 1)
    dve.wait_ge(step, 5)
    dve.scalar_tensor_tensor(small[:, 3, :], small[:, 2, :], 1.0 / D, small[:, 3, :], ALU.mult, ALU.add).then_inc(step, 1)
    dve.wait_ge(step, 6)


def entries(n, count=1):
    return slice(n, n + count) if isinstance(n, int) else bass.ds(n, count)


@contextmanager
def where_not_done(eng, done):
    if done is None:
        yield
    else:
        flag = eng.value_load(done[0:1, 0:1], min_val=0, max_val=1)
        with eng.If(flag == 0):
            yield


def ffn_step(nc, psum, bufs, SRC, X, X2, XN, stats6, mean, rstd, wm, wp, maskT, pooledT, ident, done, step):
    chunks = 4 if maskT is None else F_FULL // P
    zn, zT, hT, yT, pool4 = (bufs[k] for k in ("zn", "zT", "hT", "yT", "pool4"))
    ring = 3
    with ExitStack() as sems, ExitStack() as st:
        sem = sems.enter_context(signals(nc, f"ffn_step{step}"))
        in_ready = sem("in_ready")
        in_turned = sem("in_turned")
        in_copied = sem("in_copied")
        hidden = [sem(f"hidden{f}") for f in range(chunks)]
        activated = [sem(f"activated{f}") for f in range(chunks)]
        multiplied = [sem(f"multiplied{f}") for f in range(chunks)]
        out_copied = sem("out_copied")
        out_summed = sem("out_summed")
        out_pooled = sem("out_pooled")
        out_turned = sem("out_turned")
        xn_written = sem("xn_written")
        x_added = sem("ffn_x_added")
        x_stats = sem("ffn_x_stats")

        def last_in_ring(f, size):
            return (f - size, 0) if f >= size else (max(c for c in range(chunks) if c % size == f % size), 1)

        block = st.enter_context(nc.Block())

        @block.tensor
        def _(pe):
            def turn_back(g):
                wait(pe, out_copied, g + 1)
                wait(pe, x_added, g)
                for b in range(GB):
                    tr = pe.transpose(psum[:, 7, b * P:(b + 1) * P], yT[:, b * P:(b + 1) * P], ident[:, :])
                tr.then_inc(out_turned, 1)

            def up(g, f):
                before, back = last_in_ring(f, ring)
                wait(pe, activated[before], g + 1 - back)
                pe.matmul(psum[:, f % ring, :], wm[:, f * P:(f + 1) * P], zT[:, :], start=True, stop=True).then_inc(hidden[f], 1)

            def down(g, f):
                wait(pe, activated[f], g + 1)
                if f == 0:
                    wait(pe, out_copied, g)
                    wait(pe, out_summed, g)
                pe.matmul(psum[:, 4, :], wp[:, f, :], hT[f % 4][:, :], start=(f == 0), stop=(f == chunks - 1)).then_inc(multiplied[f], 1)

            def body(g, first=False):
                wait(pe, in_ready, g + 1)
                wait(pe, in_copied, g)
                for b in range(GB):
                    tr = pe.transpose(psum[:, 6, b * P:(b + 1) * P], zn[:, b, :], ident[:, :])
                tr.then_inc(in_turned, 1)
                if not first:
                    turn_back(g - 1)
                wait(pe, in_copied, g + 1)
                up(g, 0)
                up(g, 1)
                for f in range(chunks):
                    if f + 2 < chunks:
                        up(g, f + 2)
                    down(g, f)

            with where_not_done(pe, done):
                body(0, first=True)
                with pe.Fori(0, NG - 1) as i:
                    body(i + 1)
                turn_back(NG - 1)

        @block.scalar
        def _(act):
            def body(g):
                wait(act, in_turned, g + 1)
                wait(act, hidden[chunks - 1], g)
                act.copy(zT[:, :], psum[:, 6, :]).then_inc(in_copied, 1)
                if maskT is None:
                    for f in range(0, chunks, 2):
                        wait(act, hidden[f], g + 1)
                        before, back = last_in_ring(f, 4)
                        wait(act, multiplied[before], g + 1 - back)
                        act.activation(hT[f % 4][:, :], psum[:, f % ring, :], ACT.Relu).then_inc(activated[f], 1)
                wait(act, multiplied[chunks - 1], g + 1)
                wait(act, out_turned, g)
                wait(act, out_summed, g)
                act.copy(yT[:, :], psum[:, 4, :]).then_inc(out_copied, 1)

            with where_not_done(act, done):
                body(0)
                with act.Fori(0, NG - 1) as i:
                    body(i + 1)

        @block.vector
        def _(dve):
            def load_in(g):
                wait(dve, in_turned, g)
                for b in range(GB):
                    n = g * GB + b
                    src = SRC[:, entries(n), :].rearrange("p a d -> p (a d)")
                    if mean is None:
                        i = dve.tensor_scalar(zn[:, b, :], src, 1.0, None, ALU.mult)
                    else:
                        i = dve.tensor_scalar(zn[:, b, :], src, mean[:, entries(n)], rstd[:, entries(n)], ALU.subtract, ALU.mult)
                i.then_inc(in_ready, 1)

            def activate(g, f):
                wait(dve, hidden[f], g + 1)
                before, back = last_in_ring(f, 4)
                wait(dve, multiplied[before], g + 1 - back)
                if maskT is None:
                    i = dve.tensor_scalar(hT[f % 4][:, :], psum[:, f % ring, :], 0.0, None, ALU.max)
                else:
                    active = maskT[:, f % 3, entries(g * GB + (f // 3) * B, GB)].unsqueeze(2).broadcast_to([P, GB, P])
                    i = dve.scalar_tensor_tensor(hT[f % 4][:, :].rearrange("p (b t) -> p b t", b=GB),
                                                 psum[:, f % ring, :].rearrange("p (b t) -> p b t", b=GB), 0.0, active,
                                                 ALU.max, ALU.mult)
                i.then_inc(activated[f], 1)

            def pool_out(g):
                wait(dve, out_copied, g + 1)
                wait(dve, out_pooled, g)
                dve.tensor_reduce(pool4[:, :], yT[:, :].rearrange("p (b t) -> p b t", b=GB), AX.X,
                                  ALU.add).then_inc(out_summed, 1)
                wait(dve, out_summed, g + 1)
                dve.tensor_scalar(pooledT[:, entries(g * GB, GB)], pool4[:, :], 1.0 / P, None, ALU.mult).then_inc(out_pooled, 1)

            def write_out(g):
                o = psum[:, 7, :].rearrange("p (b d) -> p b d", b=GB)
                wait(dve, out_turned, g + 1)
                dve.tensor_scalar(XN[:, entries(g * GB, GB), :], o, 1.0, None, ALU.mult).then_inc(xn_written, 1)
                wait(dve, xn_written, g + 1)
                dve.tensor_tensor(X2[:, entries(g * GB, GB), :], o, X[:, entries(g * GB, GB), :], ALU.add).then_inc(x_added, 1)
                wait_apart(dve, x_added, g + 1, in_ready)
                for b in range(GB):
                    n = g * GB + b
                    i = dve.bn_stats(stats6[:, entries(n), :].rearrange("p a d -> p (a d)"),
                                     X2[:, entries(n), :].rearrange("p a d -> p (a d)"))
                i.then_inc(x_stats, 1)

            def body(g, first=False, final=False):
                if not first:
                    write_out(g - 1)
                for f in (range(1, chunks, 2) if maskT is None else range(chunks)):
                    activate(g, f)
                if not final:
                    load_in(g + 1)
                pool_out(g)

            with where_not_done(dve, done):
                load_in(0)
                body(0, first=True)
                with dve.Fori(0, NG - 2) as i:
                    body(i + 1)
                body(NG - 1, final=True)
                write_out(NG - 1)


def wait_apart(eng, sem, value, met):
    eng.wait_ge(met, 1)
    wait(eng, sem, value)


def route(nc, psum, pooledT, wc1, wc2, same_entry, earlier, history, maskT, done, ident, ones, flag, step):
    with ExitStack() as sems, ExitStack() as st:
        def sb(name, shape, dt=F32):
            return st.enter_context(nc.sbuf_tensor(f"{name}_{step}", shape, dt))

        sem = sems.enter_context(signals(nc, f"route{step}"))
        zr = sb("zr", [32, B])
        logits = sb("logits", [P, Q4])
        u = sb("u", [P, Q4])
        hit = sb("hit", [P, Q4])
        equal = sb("equal", [P, Q4])
        rank = sb("rank", [P, Q4])
        chosen = sb("chosen", [P, Q4])
        combined = sb("combined", [P, Q4])
        count = sb("count", [P, 2])
        positive = sb("positive", [P, 1])
        sign = sb("sign", [P, 1])
        wanted = sb("wanted", [P, 1])
        bit = sb("bit", [P, 1], I32)
        found = sb("found", [P, 1], I32)
        trial = sb("trial", [P, 1], I32)
        enough = sb("enough", [P, 1], I32)
        gained = sb("gained", [P, 1], I32)
        threshold = sb("threshold", [P, 1])
        offset = sb("offset", [P, 1])
        need = sb("need", [P, 1])
        novelty = sb("novelty", [P, 1])
        little = sb("little", [P, 1], I32)

        z_done = sem("z_done")
        z_taken = sem("z_taken")
        logits_done = sem("logits_done")
        counted = sem("counted")
        totalled = sem("totalled")
        dve_step = sem("dve_step")
        mask_ready = sem("mask_ready")
        mask_turned = sem("mask_turned")
        BITS = 31
        total = psum[:, 2, 0:1]

        block = st.enter_context(nc.Block())

        @block.tensor
        def _(pe):
            with where_not_done(pe, flag):
                pe.matmul(psum[0:32, 0, 0:B], wc1[:, :], pooledT[:, :], start=True, stop=True).then_inc(z_done, 1)
                pe.wait_ge(z_taken, 1)
                for q in range(4):
                    mm = pe.matmul(psum[32 * q:32 * q + 32, 1, 0:Q4], zr[:, :], wc2[:, q * Q4:(q + 1) * Q4], start=True, stop=True)
                mm.then_inc(logits_done, 1)
                pe.wait_ge(counted, 1)
                pe.matmul(total, same_entry[:, :], count[:, 0:1], start=True, stop=True).then_inc(totalled, 1)
                with pe.Fori(0, BITS) as i:
                    pe.wait_ge(counted, i + 2)
                    pe.matmul(total, same_entry[:, :], count[:, 0:1], start=True, stop=True).then_inc(totalled, 1)
                pe.wait_ge(counted, BITS + 2)
                pe.matmul(total, same_entry[:, :], count[:, 0:1], start=True, stop=True)
                pe.matmul(psum[:, 3, 0:1], earlier[:, :], count[:, 1:2], start=True, stop=True).then_inc(totalled, 1)
                pe.wait_ge(mask_ready, 1)
                for j in range(3):
                    pe.transpose(psum[:, 5, j * P:(j + 1) * P], chosen[:, j * P:(j + 1) * P], ident[:, :])
                pe.matmul(psum[:, 6, 0:1], ones[:, :], count[:, 0:1], start=True, stop=True).then_inc(mask_turned, 1)

        @block.scalar
        def _(act):
            with where_not_done(act, flag):
                act.wait_ge(z_done, 1)
                act.activation(zr[:, :], psum[0:32, 0, 0:B], ACT.Relu).then_inc(z_taken, 1)

        @block.vector
        def _(dve):
            at = [0]

            def then(ins):
                at[0] += 1
                ins.then_inc(dve_step, 1)
                dve.wait_ge(dve_step, at[0])

            with where_not_done(dve, flag):
                dve.wait_ge(logits_done, 1)
                then(dve.tensor_copy(logits[:, :], psum[:, 1, 0:Q4]))
                dve.tensor_scalar(hit[:, :], logits[:, :], 0.0, None, ALU.is_ge, ALU.add, accum_out=count[:, 0:1]).then_inc(counted, 1)
                dve.memset(bit[:, :], 1 << (BITS - 1))
                dve.memset(found[:, :], 0)
                dve.wait_ge(totalled, 1)
                then(dve.tensor_scalar(positive[:, :], total, float(F_ITER), None, ALU.is_ge))
                dve.tensor_scalar(sign[:, :], positive[:, :], 2.0, -1.0, ALU.mult, ALU.add)
                then(dve.tensor_scalar(wanted[:, :], positive[:, :], float(2 * F_ITER - F_FULL - 1), float(F_FULL - F_ITER + 1),
                                       ALU.mult, ALU.add))
                then(dve.tensor_scalar(u[:, :], logits[:, :], sign[:, :], None, ALU.mult))
                done_so_far = at[0]
                per_bit = 4
                with dve.Fori(0, BITS) as i:
                    base = i * per_bit + done_so_far
                    dve.tensor_tensor(trial[:, :], found[:, :], bit[:, :], ALU.bitwise_or).then_inc(dve_step, 1)
                    dve.wait_ge(dve_step, base + 1)
                    dve.tensor_scalar(hit[:, :], u[:, :], trial[:, :].bitcast(F32), None, ALU.is_ge, ALU.add,
                                      accum_out=count[:, 0:1]).then_inc(counted, 1)
                    dve.wait_ge(totalled, i + 2)
                    dve.tensor_tensor(enough[:, :], total, wanted[:, :], ALU.is_ge).then_inc(dve_step, 1)
                    dve.wait_ge(dve_step, base + 2)
                    dve.tensor_tensor(gained[:, :], bit[:, :], enough[:, :], ALU.mult).then_inc(dve_step, 1)
                    dve.wait_ge(dve_step, base + 3)
                    dve.tensor_scalar(bit[:, :], bit[:, :], 1, None, ALU.logical_shift_right)
                    dve.tensor_tensor(found[:, :], found[:, :], gained[:, :], ALU.bitwise_or).then_inc(dve_step, 1)
                    dve.wait_ge(dve_step, base + 4)
                at[0] += BITS * per_bit
                then(dve.tensor_tensor(threshold[:, :], found[:, :].bitcast(F32), sign[:, :], ALU.mult))
                then(dve.tensor_scalar(equal[:, :], logits[:, :], threshold[:, :], None, ALU.is_equal, ALU.add, accum_out=count[:, 1:2]))
                dve.tensor_scalar(hit[:, :], logits[:, :], threshold[:, :], None, ALU.is_gt, ALU.add,
                                  accum_out=count[:, 0:1]).then_inc(counted, 1)
                dve.wait_ge(totalled, BITS + 2)
                dve.tensor_scalar(need[:, :], total, -1.0, float(F_ITER), ALU.mult, ALU.add)
                then(dve.tensor_copy(offset[:, :], psum[:, 3, 0:1]))
                then(dve.memset(u[:, :], 1.0))
                then(dve.tensor_tensor_scan(rank[:, :], u[:, :], equal[:, :], offset[:, :], ALU.mult, ALU.add))
                then(dve.scalar_tensor_tensor(equal[:, :], rank[:, :], need[:, :], equal[:, :], ALU.is_le, ALU.mult))
                then(dve.tensor_tensor(chosen[:, :], hit[:, :], equal[:, :], ALU.add))
                then(dve.tensor_tensor(combined[:, :], history[:, :], chosen[:, :], ALU.max))
                then(dve.tensor_tensor(hit[:, :], combined[:, :], history[:, :], ALU.subtract))
                then(dve.tensor_copy(history[:, :], combined[:, :]))
                dve.tensor_scalar(combined[:, :], hit[:, :], 1.0, None, ALU.mult, ALU.add, accum_out=count[:, 0:1]).then_inc(mask_ready, 1)
                dve.wait_ge(mask_turned, 1)
                dve.tensor_copy(maskT[:, :, :], psum[:, 5, 0:3 * P].rearrange("p (j c) -> p j c", j=3))
                then(dve.tensor_scalar(novelty[:, :], psum[:, 6, 0:1], 1.0 / (B * F_ITER), None, ALU.mult))
                then(dve.tensor_scalar(little[:, :], novelty[:, :], 0.7, None, ALU.is_lt))
                then(dve.tensor_copy(done[:, :], little[:, :]))


def attention16(nc, kind, psum, XI, XO, stats6, mean, rstd, rms, mhalf, small, ident, ident_bf, ones, cols,
                weights_in, ctxT_in, mask_in):
    l1 = kind == "l1"
    H, HD = 16, 8
    K = C if l1 else P
    LAT = 64
    G1 = cols[:, 6:7]
    with ExitStack() as sems, ExitStack() as st:
        def sb(name, shape, dt=F32):
            return st.enter_context(nc.sbuf_tensor(f"{kind}_{name}", shape, dt))

        sem = sems.enter_context(signals(nc, kind))
        wq = sb("wq1", [D, D])
        wk = sb("wk1", [D if l1 else LAT, D])
        wv = sb("wv1", [D if l1 else LAT, D])
        wdkv = sb("wdkv", [D, LAT])
        wo = sb("wo1", [P, 4, D])
        mask32 = sb("mask32", [P, C], I32)
        bias = sb("bias", [P, K], BF16)
        own_rows = sb("own_rows", [P, H])
        scale = sb("scale", [P, B])
        loaded = sem("loaded")
        mask_loaded = sem("mask_loaded")
        step = sem("moments_step")
        var_ready = sem("var_ready")
        pow_done = sem("pow_done")
        made = sem("made")
        with nc.Block() as block:
            @block.sync
            def _(sp):
                if l1:
                    sp.dma_start(mask32[:, :], mask_in).then_inc(mask_loaded, 16)
                    tiles = ((wq, weights_in[0]), (wk, weights_in[1]), (wv, weights_in[2]))
                else:
                    tiles = ((wq, weights_in[0]), (wdkv, weights_in[1]), (wk, weights_in[2]), (wv, weights_in[3]))
                for tile, src in tiles:
                    sp.dma_start(tile[:, :], src).then_inc(loaded, 16)
                sp.dma_start(wo[:, :, :], weights_in[-1].rearrange("(c p) d -> p c d", p=P)).then_inc(loaded, 16)
                sp.wait_ge(loaded, 16 * (len(tiles) + 1))

            @block.vector
            def _(dve):
                moments(dve, stats6, mean, small, step)
                dve.tensor_scalar(small[:, 0, :], small[:, 3, :], LN_EPS, None, ALU.add).then_inc(var_ready, 1)
                if l1:
                    dve.wait_ge(mask_loaded, 16)
                    dve.tensor_scalar(bias[:, :], mask32[:, :], 0.0, -2e9, ALU.is_equal, ALU.mult)
                    return
                dve.wait_ge(pow_done, 1)
                dve.tensor_tensor(small[:, 1, :], rstd[:, :], rstd[:, :], ALU.mult).then_inc(var_ready, 1)
                dve.wait_ge(var_ready, 2)
                dve.tensor_tensor(small[:, 2, :], small[:, 1, :], small[:, 3, :], ALU.mult).then_inc(var_ready, 1)
                dve.wait_ge(var_ready, 3)
                dve.tensor_scalar(small[:, 1, :], small[:, 2, :], RMS_EPS, None, ALU.add).then_inc(var_ready, 1)
                dve.wait_ge(pow_done, 2)
                dve.tensor_tensor(scale[:, :], rstd[:, :], rms[:, :], ALU.mult)

            @block.gpsimd
            def _(pool):
                pool.wait_ge(var_ready, 1)
                pool.tensor_tensor(rstd[:, :], small[:, 0, :], mhalf[:, :], ALU.pow).then_inc(pow_done, 1)
                if not l1:
                    pool.wait_ge(var_ready, 4)
                    pool.tensor_tensor(rms[:, :], small[:, 1, :], mhalf[:, :], ALU.pow).then_inc(pow_done, 1)
                    pool.memset(bias[:, :], 0.0).then_inc(made, 1)
                pool.memset(own_rows[:, :], 1.0).then_inc(made, 1)
                n = 1 if l1 else 2
                pool.wait_ge(made, n)
                if not l1:
                    pool.affine_select(out=bias[:, :], in_=bias[:, :], compare_op=ALU.is_ge, fill=-1e9, base=0,
                                       pattern=[[-1, K]], channel_multiplier=1)
                pool.affine_select(out=own_rows[:, :], in_=own_rows[:, :], compare_op=ALU.is_ge, fill=0.0, base=0,
                                   pattern=[[-HD, H]], channel_multiplier=1).then_inc(made, 1)
                pool.wait_ge(made, n + 1)
                pool.affine_select(out=own_rows[:, :], in_=own_rows[:, :], compare_op=ALU.is_ge, fill=0.0, base=HD - 1,
                                   pattern=[[HD, H]], channel_multiplier=-1)

        zn = sb("zn16", [P, D])
        zT = sb("zT16", [D, P])
        cT = [sb(f"cT{i}", [D, C]) for i in range(2)]
        latT = sb("latT", [LAT, P])
        kT = sb("kT", [P, K])
        QT = [sb(f"QT{i}", [P, P]) for i in range(2)]
        KX = [sb(f"KX{i}", [P, H, K]) for i in range(2)]
        V = [sb(f"V{i}", [P, H, 32]) for i in range(2)]
        names = ("z_made z_turned z_copied q_proj q_copied lat_copied k_proj v_proj k_copied v_copied k_spread x_added x_stats "
                 "v_zeroed").split()
        s = {name: sem(name) for name in names}
        c_loaded = [sem(f"c_loaded{i}") for i in range(2)]
        cell = {}

        def score(pe, n, u, c):
            par = cell["par"]
            wait(pe, s["q_copied"], n + 1)
            wait(pe, s["k_spread"], n + 1)
            pe.matmul(psum[:, 2 * u + c, 0:4 * K], ident_bf[:, :], bias[:, :].unsqueeze(1).broadcast_to([P, 4, K]),
                      start=True, stop=False, skip_group_check=True)
            h = 8 * u + 4 * c
            return pe.matmul(psum[:, 2 * u + c, 0:4 * K], QT[par][:, :], KX[par][:, h:h + 4, :].rearrange("p h k -> p (h k)"),
                             start=False, stop=True, skip_group_check=True)

        pt_plan = ([(j, 0, K) for j in range(4)], [(4 + j, 0, K) for j in range(4)])
        pv_plan = [(j, 32 * (j % 4), j // 4, [(j // 4, j % 4, K)]) for j in range(8)]
        t = softmax_units(nc, st, sem, psum, 8, K, 32, pt_plan, pv_plan, score, ident, kind)

        with nc.Block() as block:
            @block.tensor
            def _(pe):
                def turn_input(m):
                    wait(pe, s["z_made"], m + 1)
                    wait(pe, s["k_copied"], m)
                    pe.transpose(psum[:, 6, 0:P], zn[:, :], ident[:, :]).then_inc(s["z_turned"], 1)

                def project_q(m):
                    wait(pe, s["z_copied"], m + 1)
                    wait(pe, s["v_copied"], m)
                    if not l1:
                        pe.matmul(psum[0:LAT, 7, P:2 * P], wdkv[:, :], zT[:, :], start=True, stop=True)
                    pe.matmul(psum[:, 7, 0:P], wq[:, :], zT[:, :], start=True, stop=True).then_inc(s["q_proj"], 1)

                def project_k(m, par):
                    if l1:
                        wait(pe, c_loaded[par], m // 2 * 16 + 16)
                        pe.matmul(psum[:, 6, 0:K], wk[:, :], cT[par][:, :], start=True, stop=True).then_inc(s["k_proj"], 1)
                    else:
                        wait(pe, s["lat_copied"], m + 1)
                        pe.matmul(psum[:, 6, 0:K], wk[:, :], latT[:, :], start=True, stop=True).then_inc(s["k_proj"], 1)

                def values(m, par):
                    wait(pe, s["q_copied"], m + 1)
                    pe.matmul(psum[0:K, 7, 0:P], cT[par][:, :] if l1 else latT[:, :], wv[:, :], start=True,
                              stop=True).then_inc(s["v_proj"], 1)

                def pv(n, u, par):
                    t["pe_pv"](pe, n, u, lambda h, i: V[par][0:K, h, :])

                def scores(n, u, par, banks=(0, 1)):
                    cell["par"] = par
                    for bank in banks:
                        t["pe_scores"](pe, n, u, bank)

                def body(n, par, first=False, next_=True, after=True):
                    if after:
                        turn_input(n + 2)
                    if next_:
                        values(n + 1, 1 - par)
                    t["pe_turn_probs0"](pe, n, 0)
                    if not first:
                        t["pe_project"](pe, n - 1, wo)
                    if next_:
                        scores(n + 1, 0, 1 - par, (0,))
                    t["pe_turn_probs1"](pe, n, 0)
                    if next_:
                        scores(n + 1, 0, 1 - par, (1,))
                    if after:
                        project_q(n + 2)
                    t["pe_turn_sums"](pe, n, 0)
                    pv(n, 0, par)
                    t["pe_turn_probs0"](pe, n, 1)
                    if after:
                        project_k(n + 2, par)
                    if next_:
                        scores(n + 1, 1, 1 - par, (0,))
                    t["pe_turn_probs1"](pe, n, 1)
                    if next_:
                        scores(n + 1, 1, 1 - par, (1,))
                    t["pe_turn_sums"](pe, n, 1)
                    pv(n, 1, par)

                def prepare(m):
                    turn_input(m)
                    project_q(m)
                    project_k(m, m)

                prepare(0)
                values(0, 0)
                scores(0, 0, 0)
                scores(0, 1, 0)
                prepare(1)
                wait(pe, s["k_copied"], 2)
                run_entries(pe, body)
                t["pe_project"](pe, B - 1, wo)

            @block.scalar
            def _(act):
                def copy_input(m):
                    wait(act, s["z_turned"], m + 1)
                    wait(act, s["q_proj"], m)
                    act.activation(zT[:, :], psum[:, 6, 0:P], ACT.Copy, scale=1.0 if l1 else G1).then_inc(s["z_copied"], 1)

                def copy_q(m, par):
                    wait(act, s["q_proj"], m + 1)
                    if not l1:
                        wait(act, s["v_proj"], m)
                        act.copy(latT[:, :], psum[0:LAT, 7, P:2 * P]).then_inc(s["lat_copied"], 1)
                    wait(act, t["scored"][1], m - 1)
                    act.mul(QT[par][:, :], psum[:, 7, 0:P], float(HD) ** -0.5).then_inc(s["q_copied"], 1)

                def copy_k(m):
                    wait(act, s["k_proj"], m + 1)
                    wait(act, s["k_spread"], m)
                    act.copy(kT[:, :], psum[:, 6, 0:K]).then_inc(s["k_copied"], 1)

                def copy_values(m, par):
                    wait(act, s["v_proj"], m + 1)
                    wait(act, t["pv_done"][1], m - 1)
                    act.copy(V[par][0:K, :, 0:HD], psum[0:K, 7, 0:P].rearrange("k (h d) -> k h d", d=HD)).then_inc(s["v_copied"], 1)

                def body(n, par, first=False, next_=True, after=True):
                    if after:
                        copy_input(n + 2)
                    if next_:
                        copy_values(n + 1, 1 - par)
                    t["act_copy_pt0"](act, n, 0)
                    t["act_exp"](act, n, 1)
                    if after:
                        copy_q(n + 2, par)
                    if after:
                        copy_k(n + 2)
                    t["act_copy_pt0"](act, n, 1)
                    if next_:
                        t["act_exp"](act, n + 1, 0)

                def prepare(m):
                    copy_input(m)
                    copy_q(m, m)
                    copy_k(m)

                wait(act, s["v_zeroed"], 2)
                prepare(0)
                copy_values(0, 0)
                t["act_exp"](act, 0, 0)
                prepare(1)
                run_entries(act, body)

            @block.vector
            def _(dve):
                def norm_input(m):
                    src = XI[:, entries(m), :].rearrange("p a d -> p (a d)")
                    wait(dve, s["z_turned"], m)
                    dve.tensor_scalar(zn[:, :], src, mean[:, entries(m)], (rstd if l1 else scale)[:, entries(m)], ALU.subtract,
                                      ALU.mult).then_inc(s["z_made"], 1)
                    if not l1:
                        dve.tensor_scalar(XO[:, entries(m), :].rearrange("p a d -> p (a d)"), src, mean[:, entries(m)],
                                          rstd[:, entries(m)], ALU.subtract, ALU.mult)

                def add_projection(n):
                    wait(dve, t["projected"], n + 1)
                    xs = XO[:, entries(n), :].rearrange("p a d -> p (a d)")
                    dve.tensor_tensor(xs, psum[:, 5, 0:D], xs, ALU.add).then_inc(t["projection_taken"], 1)
                    wait_apart(dve, t["projection_taken"], n + 1, s["z_made"])
                    dve.bn_stats(stats6[:, entries(n), :].rearrange("p a d -> p (a d)"), xs).then_inc(s["x_stats"], 1)

                def body(n, par, first=False, next_=True, after=True):
                    if after:
                        norm_input(n + 2)
                    if not first:
                        t["dve_copy_sums"](dve, n - 1, 1)
                        t["dve_scale"](dve, n - 1, 1)
                    t["dve_max"](dve, n, 1)
                    if not first:
                        add_projection(n - 1)
                    t["dve_invert"](dve, n, 0)
                    t["dve_copy_pt1"](dve, n, 0)
                    t["dve_copy_sums"](dve, n, 0)
                    t["dve_scale"](dve, n, 0)
                    if next_:
                        t["dve_max"](dve, n + 1, 0)
                    t["dve_invert"](dve, n, 1)
                    t["dve_copy_pt1"](dve, n, 1)

                for q in range(2):
                    dve.memset(V[q][:, :, :], 0.0).then_inc(s["v_zeroed"], 1)
                norm_input(0)
                t["dve_max"](dve, 0, 0)
                norm_input(1)
                run_entries(dve, body)
                t["dve_copy_sums"](dve, B - 1, 1)
                t["dve_scale"](dve, B - 1, 1)
                add_projection(B - 1)

            @block.gpsimd
            def _(pool):
                def spread_k(m, par):
                    wait(pool, s["k_copied"], m + 1)
                    wait(pool, t["scored"][1], m - 1)
                    pool.tensor_tensor(KX[par][:, :, :], kT[:, :].unsqueeze(1).broadcast_to([P, H, K]),
                                       own_rows[:, :].unsqueeze(2).broadcast_to([P, H, K]), ALU.mult).then_inc(s["k_spread"], 1)

                spread_k(0, 0)
                spread_k(1, 1)
                with pool.Fori(0, B // 2 - 1) as i:
                    spread_k(2 * i + 2, 0)
                    spread_k(2 * i + 3, 1)

            if l1:
                @block.sync
                def _(sp):
                    def load(m, par):
                        wait(sp, s["v_proj"], m - 1)
                        sp.dma_start(cT[par][:, :], ctxT_in[entries(m)].rearrange("a d t -> (a d) t")).then_inc(c_loaded[par], 16)

                    load(0, 0)
                    load(1, 1)
                    with sp.Fori(0, B // 2 - 1) as i:
                        load(2 * i + 2, 0)
                        load(2 * i + 3, 1)


def moe(nc, psum, X2, X3, stats6, mean, rms, mhalf, small, ident, cols, gate_in, w1_in, w2_in, out):
    NE, HID, HALVES = 8, 256, 2
    G2 = cols[:, 7:8]
    N = GB * P
    with ExitStack() as sems, ExitStack() as st:
        def sb(name, shape, dt=F32):
            return st.enter_context(nc.sbuf_tensor(name, shape, dt))

        sem = sems.enter_context(signals(nc, "moe"))
        w1 = sb("w1", [D, NE, HID])
        w2 = sb("w2", [P, NE * HALVES, D])
        gate = sb("gate", [D, NE])
        index = sb("index", [P, NE])
        loaded, step, var_ready, iota_made = sem("loaded"), sem("moments_step"), sem("var_ready"), sem("iota_made")
        index_i = sb("index_i", [P, NE], I32)
        with nc.Block() as block:
            @block.sync
            def _(sp):
                sp.dma_start(w1[:, :, :], w1_in).then_inc(loaded, 16)
                sp.dma_start(w2[:, :, :], w2_in.rearrange("(c p) d -> p c d", p=P)).then_inc(loaded, 16)
                sp.dma_start(gate[:, :], gate_in).then_inc(loaded, 16)
                sp.wait_ge(loaded, 48)

            @block.vector
            def _(dve):
                moments(dve, stats6, mean, small, step)
                dve.tensor_tensor(small[:, 0, :], mean[:, :], mean[:, :], ALU.mult).then_inc(var_ready, 1)
                dve.wait_ge(var_ready, 1)
                dve.tensor_tensor(small[:, 1, :], small[:, 0, :], small[:, 3, :], ALU.add).then_inc(var_ready, 1)
                dve.wait_ge(var_ready, 2)
                dve.tensor_scalar(small[:, 2, :], small[:, 1, :], RMS_EPS, None, ALU.add).then_inc(var_ready, 1)
                dve.wait_ge(iota_made, 1)
                dve.tensor_copy(index[:, :], index_i[:, :])

            @block.gpsimd
            def _(pool):
                pool.iota(index_i[:, :], pattern=[[1, NE]], base=0, channel_multiplier=0).then_inc(iota_made, 1)
                pool.wait_ge(var_ready, 3)
                pool.tensor_tensor(rms[:, :], small[:, 2, :], mhalf[:, :], ALU.pow)

        hn = sb("hn", [P, GB, D])
        hT = [sb(f"moe_hT{i}", [D, N]) for i in range(2)]
        logits = sb("moe_logits", [P, GB, NE])
        best = sb("best", [P, GB, NE])
        best_at = sb("best_at", [P, GB, NE], U32)
        best_at_f = sb("best_at_f", [P, GB, NE])
        margin = sb("margin", [P, GB])
        tanh_half = sb("tanh_half", [P, GB])
        gates = sb("gates", [P, 2, GB])
        first_part = sb("first_part", [P, GB, NE])
        second_part = sb("second_part", [P, GB, NE])
        combine = [sb(f"combine{i}", [P, GB, NE]) for i in range(2)]
        RING = 4
        hid = [sb(f"hid{i}", [P, N]) for i in range(RING)]
        prod = [sb(f"prod{i}", [P, GB, D]) for i in range(2)]
        acc = [sb(f"acc{i}", [P, GB, D]) for i in range(2)]
        names = ("h_made h_turned h_copied gated logits_copied best_done index_done index_copied margin_done tanh_done gates_done "
                 "parts_made combined stored x_summed").split()
        s = {name: sem(name) for name in names}
        NC_ = NE * HALVES
        hidden = [sem(f"hidden{i}") for i in range(NC_)]
        activated = [sem(f"activated{i}") for i in range(NC_)]
        expert = [sem(f"expert{e}") for e in range(NE)]
        weighted = [sem(f"weighted{e}") for e in range(NE)]
        summed = [sem(f"summed{e}") for e in range(NE)]
        BANKS = 3
        stored = [sem("stored0"), sem("stored1")]
        def last_in_ring(i, size, n):
            return (i - size, 0) if i >= size else (max(c for c in range(n) if c % size == i % size), 1)

        with nc.Block() as block:
            @block.tensor
            def _(pe):
                def prepare(g, par):
                    wait(pe, s["h_made"], g + 1)
                    wait(pe, s["h_copied"], g)
                    for b in range(GB):
                        tr = pe.transpose(psum[:, 0, b * P:(b + 1) * P], hn[:, b, :], ident[:, :])
                    tr.then_inc(s["h_turned"], 1)
                    wait(pe, s["h_copied"], g + 1)
                    wait(pe, s["logits_copied"], g)
                    for b in range(GB):
                        mm = pe.matmul(psum[:, 1, b * NE:(b + 1) * NE], hT[par][:, b * P:(b + 1) * P], gate[:, :],
                                       start=True, stop=True)
                    mm.then_inc(s["gated"], 1)

                def up(g, par, i):
                    before, back = last_in_ring(i, BANKS, NC_)
                    wait(pe, activated[before], g + 1 - back)
                    e, half = divmod(i, HALVES)
                    pe.matmul(psum[:, 2 + i % BANKS, :], w1[:, e, half * P:(half + 1) * P], hT[par][:, :],
                              start=True, stop=True).then_inc(hidden[i], 1)

                def down(g, e):
                    before, back = last_in_ring(e, 2, NE)
                    wait(pe, weighted[before], g + 1 - back)
                    wait(pe, activated[2 * e + 1], g + 1)
                    for b in range(GB):
                        for half in range(HALVES):
                            i = 2 * e + half
                            mm = pe.matmul(psum[:, 5 + e % 2, b * D:(b + 1) * D], hid[i % RING][:, b * P:(b + 1) * P], w2[:, i, :],
                                           start=(half == 0), stop=(half == HALVES - 1))
                    mm.then_inc(expert[e], 1)

                def body(g, par, final=False):
                    for i in range(NC_):
                        up(g, par, i)
                        if i % 2 == 1 and i >= 3:
                            down(g, (i - 3) // 2)
                        if i == 9 and not final:
                            prepare(g + 1, 1 - par)
                    down(g, NE - 1)

                prepare(0, 0)
                wait(pe, s["h_copied"], 1)
                body(0, 0)
                with pe.Fori(0, NG // 2 - 1) as i:
                    body(2 * i + 1, 1)
                    body(2 * i + 2, 0)
                body(NG - 1, 1, final=True)

            @block.scalar
            def _(act):
                def copy_h(g, par):
                    wait(act, s["h_turned"], g + 1)
                    wait(act, hidden[NC_ - 1], g - 1)
                    act.activation(hT[par][:, :], psum[:, 0, :], ACT.Copy, scale=G2).then_inc(s["h_copied"], 1)

                def squash(g):
                    wait(act, s["margin_done"], g + 1)
                    wait(act, s["gates_done"], g)
                    act.activation(tanh_half[:, :], margin[:, :], ACT.Tanh, scale=0.5).then_inc(s["tanh_done"], 1)

                def body(g, par, final=False):
                    for i in range(NC_):
                        wait(act, hidden[i], g + 1)
                        if i >= RING:
                            wait(act, expert[(i - RING) // 2], g + 1)
                        else:
                            wait(act, expert[(NC_ - RING + i) // 2], g)
                        act.activation(hid[i % RING][:, :], psum[:, 2 + i % BANKS, :], ACT.Silu).then_inc(activated[i], 1)
                        if i == 9 and not final:
                            copy_h(g + 1, 1 - par)
                        if i == 13 and not final:
                            squash(g + 1)

                copy_h(0, 0)
                squash(0)
                body(0, 0)
                with act.Fori(0, NG // 2 - 1) as i:
                    body(2 * i + 1, 1)
                    body(2 * i + 2, 0)
                body(NG - 1, 1, final=True)

            @block.vector
            def _(dve):
                def norm(g):
                    wait(dve, s["h_turned"], g)
                    for b in range(GB):
                        n = g * GB + b
                        i = dve.tensor_scalar(hn[:, b, :], X3[:, entries(n), :].rearrange("p a d -> p (a d)"), rms[:, entries(n)],
                                              None, ALU.mult)
                    i.then_inc(s["h_made"], 1)

                def choose(g):
                    wait(dve, s["gated"], g + 1)
                    dve.tensor_copy(logits[:, :, :], psum[:, 1, 0:GB * NE].rearrange("p (b e) -> p b e", e=NE)).then_inc(s["logits_copied"], 1)
                    wait_apart(dve, s["logits_copied"], g + 1, s["h_made"])
                    for b in range(GB):
                        i = dve.max(best[:, b, :], logits[:, b, :])
                    i.then_inc(s["best_done"], 1)
                    wait_apart(dve, s["best_done"], g + 1, s["h_made"])
                    for b in range(GB):
                        i = dve.max_index(best_at[:, b, :], best[:, b, :], logits[:, b, :])
                    dve.tensor_tensor(margin[:, :], best[:, :, 0], best[:, :, 1], ALU.subtract).then_inc(s["margin_done"], 1)
                    wait(dve, s["margin_done"], g + 1)
                    dve.tensor_copy(best_at_f[:, :, :], best_at[:, :, :]).then_inc(s["index_copied"], 1)

                def weigh(g, par):
                    wait(dve, s["tanh_done"], g + 1)
                    dve.tensor_scalar(gates[:, 0, :], tanh_half[:, :], 0.5, 0.5, ALU.mult, ALU.add)
                    dve.tensor_scalar(gates[:, 1, :], tanh_half[:, :], -0.5, 0.5, ALU.mult, ALU.add).then_inc(s["gates_done"], 1)
                    wait(dve, s["gates_done"], g + 1)
                    wait(dve, s["index_copied"], g + 1)
                    for b in range(GB):
                        dve.tensor_scalar(first_part[:, b, :], index[:, :], best_at_f[:, b, 0:1], gates[:, 0, b:b + 1],
                                          ALU.is_equal, ALU.mult)
                        i = dve.tensor_scalar(second_part[:, b, :], index[:, :], best_at_f[:, b, 1:2], gates[:, 1, b:b + 1],
                                              ALU.is_equal, ALU.mult)
                    i.then_inc(s["parts_made"], 1)
                    wait(dve, s["parts_made"], g + 1)
                    dve.tensor_tensor(combine[par][:, :, :], first_part[:, :, :], second_part[:, :, :], ALU.add).then_inc(s["combined"], 1)

                def body(g, par, final=False):
                    for e in range(NE):
                        wait(dve, expert[e], g + 1)
                        wait(dve, s["combined"], g + 1)
                        before, back = last_in_ring(e, 2, NE)
                        wait(dve, summed[before], g + 1 - back)
                        dve.tensor_tensor(prod[e % 2][:, :, :], psum[:, 5 + e % 2, :].rearrange("p (b d) -> p b d", b=GB),
                                          combine[par][:, :, e:e + 1].broadcast_to([P, GB, D]), ALU.mult).then_inc(weighted[e], 1)
                        if e == 1 and not final:
                            norm(g + 1)
                        if e == 4 and not final:
                            choose(g + 1)
                        if e == 6 and not final:
                            weigh(g + 1, 1 - par)

                norm(0)
                choose(0)
                weigh(0, 0)
                body(0, 0)
                with dve.Fori(0, NG // 2 - 1) as i:
                    body(2 * i + 1, 1)
                    body(2 * i + 2, 0)
                body(NG - 1, 1, final=True)

            @block.gpsimd
            def _(pool):
                def body(g, par, final=False):
                    a = acc[par]
                    xs = entries(g * GB, GB)
                    wait(pool, stored[par], 8 * GB * (g - par))
                    pool.tensor_tensor(a[:, :, :], X2[:, xs, :], X3[:, xs, :], ALU.add).then_inc(s["x_summed"], 1)
                    wait(pool, s["x_summed"], g + 1)
                    for e in range(NE):
                        wait(pool, weighted[e], g + 1)
                        if e:
                            wait(pool, summed[e - 1], g + 1)
                        pool.tensor_tensor(a[:, :, :], a[:, :, :], prod[e % 2][:, :, :], ALU.add).then_inc(summed[e], 1)

                body(0, 0)
                body(1, 1)
                with pool.Fori(0, NG // 2 - 1) as i:
                    body(2 * i + 2, 0)
                    body(2 * i + 3, 1)

            @block.sync
            def _(sp):
                def store(g, par):
                    wait(sp, summed[NE - 1], g + 1)
                    for b in range(GB):
                        sp.dma_start(out[entries(g * GB + b)].rearrange("a t d -> (a t) d"), acc[par][:, b, :]).then_inc(stored[par], 16)

                store(0, 0)
                with sp.Fori(0, NG // 2 - 1) as i:
                    store(2 * i + 1, 1)
                    store(2 * i + 2, 0)
                store(NG - 1, 1)
                sp.wait_ge(stored[0], 16 * GB * (NG // 2))
                sp.wait_ge(stored[1], 16 * GB * (NG // 2))


def lay_out(np, i):
    f = lambda a: np.ascontiguousarray(np.asarray(a))
    def pad_wo(w_inT):
        w = np.zeros((4, 4, 32, D), np.float32)
        w[:, :, 0:8, :] = f(w_inT).reshape(4, 4, 8, D)
        return f(w.reshape(4 * P, D))
    cols = np.stack([f(i[n]) for n in ("L0_xattn_ln_x_w", "L0_xattn_ln_x_b", "L0_xattn_ln_l_w", "L0_xattn_ln_l_b")]
                    + [np.concatenate([f(i[n]), f(i[n])]) for n in ("L0_xattn_q_scale", "L0_xattn_k_scale")]
                    + [f(i["L1_ffn_g1"]), f(i["L1_ffn_g2"])], axis=1)
    T = lambda n: f(np.asarray(i[n]).T)
    return {
        "x_in": f(i["x"]), "ctx_in": f(i["ctx_1024"]), "ctxT_in": f(np.transpose(np.asarray(i["ctx_1024"]), (0, 2, 1))),
        "keep_in": f(i["mask_BxS2_bk0"]).reshape(1, B * C),
        "qk_mask_in": f(i["mask_1x1xSxS2_ik0"]).reshape(P, C), "cols_in": f(cols),
        "lnow_in": f(i["L0_xattn_ln_o_w"]).reshape(1, D), "lnob_in": f(i["L0_xattn_ln_o_b"]).reshape(1, D),
        "wq0_in": f(i["L0_xattn_Wq"]), "wkv0_in": f(i["L0_xattn_Wkv"]), "wo0_in": f(i["L0_xattn_Wo"]),
        "wm_in": T("L0_ffn_Wm"), "wp_in": T("L0_ffn_Wp"), "wc1_in": T("L0_ffn_Wc1"), "wc2_in": T("L0_ffn_Wc2"),
        "wq1_in": T("L1_xattn_w_q"), "wk1_in": T("L1_xattn_w_k"), "wv1_in": T("L1_xattn_w_v"),
        "wo1_in": pad_wo(np.asarray(i["L1_xattn_w_o"]).T),
        "wq2_in": f(i["L1_ffn_Wq"]), "wdkv_in": f(i["L1_ffn_Wdkv"]), "wuk_in": f(i["L1_ffn_Wuk"]),
        "wuv_in": f(i["L1_ffn_Wuv"]), "wo2_in": pad_wo(i["L1_ffn_Wo"]),
        "gate_in": f(i["L1_ffn_gate_w"]), "w1_in": f(np.transpose(np.asarray(i["L1_ffn_w1"]), (1, 0, 2))),
        "w2_in": f(i["L1_ffn_w2"]).reshape(8 * 256, D),
    }


def kernel(**inputs):
    import numpy as _np
    import concourse.bacc as _bacc
    from concourse import mybir as _mybir
    from concourse.bass_utils import run_bass_kernel_spmd as _run

    nc = _bacc.Bacc("TRN2", target_bir_lowering=False, num_devices=1)
    arrays = lay_out(_np, inputs)
    args = [nc.dram_tensor(n, a.shape, _mybir.dt.from_np(a.dtype), kind="ExternalInput").ap() for n, a in arrays.items()]
    out = nc.dram_tensor("out_dram", (B, P, D), _mybir.dt.float32, kind="ExternalOutput").ap()
    mega_kernel(nc, *args, out)
    r = _run(nc, [arrays], core_ids=[0])
    return r.results[0]["out_dram"]
```

```python
from contextlib import ExitStack, contextmanager

import concourse.bass as bass
from concourse import mybir

ALU = mybir.AluOpType
ACT = mybir.ActivationFunctionType
AX = mybir.AxisListType
F32 = mybir.dt.float32
BF16 = mybir.dt.bfloat16
I32 = mybir.dt.int32
U32 = mybir.dt.uint32
U8 = mybir.dt.uint8

P = 128
B = 32
D = 128
C = 120
GB = 4
NG = B // GB
LN_EPS = 1e-5
RMS_EPS = 1e-6
LAT = 64
F_ITER = 512
F_FULL = 3 * F_ITER
Q4 = F_FULL // 4
NEG_MAX = -3.0e38
FIRST = 4


def wait(eng, sem, value):
    if isinstance(value, int) and value <= 0:
        return
    eng.wait_ge(sem, value)


@contextmanager
def signals(nc, phase):
    given = []

    def sem(name):
        given.append(nc.alloc_semaphore(f"{phase}_{name}"))
        return given[-1]

    yield sem
    nc.clear_and_free_semaphores(given)
    nc.all_engine_barrier()


def mega_kernel(nc, x_in, ctx_in, ctxT_in, keep_in, qk_mask_in, cols_in, lnow_in, lnob_in, wq0_in, wkv0_in, wo0_in,
                wm_in, wp_in, wc1_in, wc2_in, wq1_in, wk1_in, wv1_in, wo1_in, wq2_in, wdkv_in, wuk_in, wuv_in,
                wo2_in, gate_in, w1_in, w2_in, out, stop_after=9):
    ctx = ExitStack()
    with ctx:
        def sb(name, shape, dt=F32, stack=ctx):
            return stack.enter_context(nc.sbuf_tensor(name, shape, dt))

        X = sb("X", [P, B, D])
        X2 = sb("X2", [P, B, D])
        X3 = sb("X3", [P, B, D])
        stats6 = sb("stats6", [P, B, 6])
        mean = sb("mean", [P, B])
        rstd = sb("rstd", [P, B])
        rms = sb("rms", [P, B])
        mhalf = sb("mhalf", [P, B])
        small = sb("small", [P, 4, B])
        ident = sb("ident", [P, P])
        ident_bf = sb("ident_bf", [P, P], BF16)
        ones = sb("ones", [P, P])
        cols = sb("cols", [P, 8])
        LNX_W, LNX_B, LNL_W, LNL_B, QS, KS, G1, G2 = (cols[:, i:i + 1] for i in range(8))
        ffn_weights = dict(wm=sb("wm", [D, F_FULL]), wp=sb("wp", [P, F_FULL // P, D]), wc1=sb("wc1", [D, 32]),
                           wc2=sb("wc2", [32, F_FULL]))
        l1_weights = dict(wq=sb("l1_wq", [D, D]), wk=sb("l1_wk", [D, D]), wv=sb("l1_wv", [D, D]), wo=sb("l1_wo", [P, D]),
                          mask=sb("l1_mask", [P, C], I32))
        mla_weights = dict(wq=sb("mla_wq", [D, D]), wdkv=sb("mla_wdkv", [D, LAT]), wk=sb("mla_wk", [LAT, D]),
                           wv=sb("mla_wv", [LAT, D]), wo=sb("mla_wo", [P, D]))
        later_weights = [(ffn_weights["wm"], wm_in), (ffn_weights["wp"], wp_in.rearrange("(c p) d -> p c d", p=P)),
                         (ffn_weights["wc1"], wc1_in), (ffn_weights["wc2"], wc2_in)]
        later_weights += [(l1_weights[k], a) for k, a in (("wq", wq1_in), ("wk", wk1_in), ("wv", wv1_in), ("wo", wo1_in),
                                                          ("mask", qk_mask_in))]
        later_weights += [(mla_weights[k], a) for k, a in (("wq", wq2_in), ("wdkv", wdkv_in), ("wk", wuk_in), ("wv", wuv_in),
                                                           ("wo", wo2_in))]
        psum = ctx.enter_context(nc.psum_tensor("psum", [P, 8, 512], F32))

        if stop_after >= 1:
            l0_attention(nc, psum, X, stats6, mean, rstd, mhalf, small, ident, ident_bf, ones, cols,
                         later_weights, x_in, cols_in, ctx_in, keep_in, lnow_in, lnob_in, wq0_in, wkv0_in, wo0_in)
        last = X
        if stop_after >= 2:
            l0_ffn(nc, psum, X, X2, X3, stats6, mean, rstd, mhalf, small, ident, ones, ffn_weights)
            last = X2
        if stop_after >= 3:
            attention16(nc, "l1", psum, X2, X2, stats6, mean, rstd, mhalf, small, ident, ident_bf, ones, cols,
                        l1_weights, ctxT_in, None)
        if stop_after >= 4:
            moe_weights = dict(w1=sb("w1", [D, 8, 256]), w2=sb("w2", [P, 16, D]), gate=sb("gate", [D, 8]))
            attention16(nc, "mla", psum, X2, X3, stats6, mean, rstd, mhalf, small, ident, ident_bf, ones, cols,
                        mla_weights, None, [(moe_weights["w1"], w1_in), (moe_weights["w2"], w2_in.rearrange("(c p) d -> p c d", p=P)),
                                            (moe_weights["gate"], gate_in)])
            last = X3
        if stop_after >= 5:
            moe(nc, psum, X2, X3, stats6, mean, rms, mhalf, small, ident, cols, moe_weights, out)
        else:
            with nc.semaphore("dump") as dump, nc.Block() as block:
                @block.sync
                def _(sp):
                    sp.dma_start(out.rearrange("b t d -> t b d"), last[:, :, :]).then_inc(dump, 16)
                    sp.wait_ge(dump, 16)


def inverse_roots(pool, out, of, mhalf, some):
    return pool.tensor_tensor(out[:, some], of[:, some], mhalf[0:of.shape[0], some], ALU.pow)


def softmax_units(nc, st, new_sem, psum, H, K, pt_plan, score, bank4_free, bank5_free, ident, tag):
    def sem(name):
        return [new_sem(f"{name}{u}") for u in range(2)]

    def sb(name, shape, dt=F32):
        return st.enter_context(nc.sbuf_tensor(f"{tag}_{name}", shape, dt))

    HB = H // 2
    n_max = [sb(f"n_max{u}", [P, H]) for u in range(2)]
    sums = [sb(f"sums{u}", [P, H]) for u in range(2)]
    r_sums = [sb(f"r_sums{u}", [P, H]) for u in range(2)]
    probs = [sb(f"probs{u}", [P, H, K]) for u in range(2)]
    probsT = [sb(f"probsT{u}", [P, 2, 4, P]) for u in range(2)]

    scored = sem("scored")
    max_taken = sem("max_taken")
    exp_done = sem("exp_done")
    sum_inverted = sem("sum_inverted")
    pt0_turned = sem("pt0_turned")
    pt1_turned = sem("pt1_turned")
    pt0_copied = sem("pt0_copied")
    pt1_copied = sem("pt1_copied")
    pv_done = sem("pv_done")
    KN = [pt_plan[0][0][2], pt_plan[1][0][2]]

    def pe_scores(pe, n, u, bank):
        if bank == 0:
            wait(pe, exp_done[u], n)
        s = score(pe, n, u, bank)
        if bank == 1:
            s.then_inc(scored[u], 1)

    def dve_max(dve, n, u):
        wait(dve, scored[u], n + 1)
        wait(dve, exp_done[u], n)
        dve.tensor_reduce(n_max[u][:, :].rearrange("p (c j) -> p c j", c=2),
                          psum[:, 2 * u:2 * u + 2, 0:HB * K].rearrange("p c (j k) -> p c j k", k=K), AX.X, ALU.max,
                          negate=True).then_inc(max_taken[u], 1)

    def act_exp(act, n, u):
        wait(act, max_taken[u], n + 1)
        wait(act, pt1_turned[u], n)
        wait(act, sum_inverted[u], n)
        for h in range(H):
            e = act.activation(probs[u][:, h, :], psum[:, 2 * u + h // HB, (h % HB) * K:(h % HB + 1) * K], ACT.Exp,
                               bias=n_max[u][:, h:h + 1], accum_out=sums[u][:, h:h + 1])
        e.then_inc(exp_done[u], 1)

    def dve_invert(dve, n, u):
        wait(dve, exp_done[u], n + 1)
        dve.reciprocal(r_sums[u][:, :], sums[u][:, :]).then_inc(sum_inverted[u], 1)
        wait(dve, sum_inverted[u], n + 1)

    def pe_turn_probs0(pe, n, u):
        wait(pe, exp_done[u], n + 1)
        bank4_free(pe, n, u)
        for j, (h, k0, kn) in enumerate(pt_plan[0]):
            t = pe.transpose(psum[0:kn, 4, j * P:(j + 1) * P], probs[u][:, h, k0:k0 + kn], ident[:, :])
        t.then_inc(pt0_turned[u], 1)

    def pe_turn_probs1(pe, n, u):
        bank5_free(pe, n, u)
        for j, (h, k0, kn) in enumerate(pt_plan[1]):
            t = pe.transpose(psum[0:kn, 5, j * P:(j + 1) * P], probs[u][:, h, k0:k0 + kn], ident[:, :])
        t.then_inc(pt1_turned[u], 1)

    def act_copy_pt0(act, n, u):
        wait(act, pt0_turned[u], n + 1)
        wait(act, pv_done[u], n)
        act.copy(probsT[u][0:KN[0], 0, :, :], psum[0:KN[0], 4, :].rearrange("k (j q) -> k j q", j=4)).then_inc(pt0_copied[u], 1)

    def dve_copy_pt1(dve, n, u):
        wait(dve, pt1_turned[u], n + 1)
        wait(dve, pv_done[u], n)
        dve.tensor_copy(probsT[u][0:KN[1], 1, :, :], psum[0:KN[1], 5, :].rearrange("k (j q) -> k j q", j=4)).then_inc(pt1_copied[u], 1)

    return dict(locals())


def run_entries(eng, body, before_loop=None):
    body(0, 0, first=True)
    if before_loop:
        before_loop()
    with eng.Fori(0, B // 2 - 2) as i:
        body(2 * i + 1, 1)
        body(2 * i + 2, 0)
    body(B - 3, 1)
    body(B - 2, 0, after=False)
    body(B - 1, 1, after=False, next_=False)


def l0_attention(nc, psum, X, stats6, mean, rstd, mhalf, small, ident, ident_bf, ones, cols,
                 later_weights, x_in, cols_in, ctx_in, keep_in, lnow_in, lnob_in, wq_in, wkv_in, wo_in):
    H, HD = 8, 64
    K = C + P
    INNER = H * HD
    LNX_W, LNX_B, LNL_W, LNL_B, QS, KS = (cols[:, i:i + 1] for i in range(6))
    with ExitStack() as sems, ExitStack() as st:
        def sb(name, shape, dt=F32):
            return st.enter_context(nc.sbuf_tensor(name, shape, dt))

        sem = sems.enter_context(signals(nc, "l0"))
        CT = sb("CT", [P, B, D])
        keep8 = sb("keep8", [1, B * C], U8)
        keep_row = sb("keep_row", [P, B, K], BF16)
        stats6_c = sb("stats6_c", [P, B, 6])
        mean_c = sb("mean_c", [P, B])
        small_c = sb("small_c", [P, 4, B])
        rstd_c = sb("rstd_c", [P, B])
        wq = sb("wq", [D, INNER])
        wkv = sb("wkv", [D, 2 * INNER])
        wo = sb("wo", [P, 4, D])
        lnow = sb("lnow", [P, D])
        lnob = sb("lnob", [P, D])
        qk_scale = sb("qk_scale", [P, 1])
        first_row = sb("first_row", [P, P], BF16)
        qk = sb("qk", [P, 3, INNER])
        sq = sb("sq", [P, 3, INNER])
        QZ = [sb(f"QZ{i}", [P, H, P]) for i in range(2)]

        x_loaded = [sem(f"x_loaded{g}") for g in range(NG)]
        c_loaded = [sem(f"c_loaded{g}") for g in range(NG)]
        cols_loaded = sem("cols_loaded")
        keep_loaded = sem("keep_loaded")
        weights_loaded = sem("weights_loaded")
        zeroed = sem("zeroed")
        identity_made = sem("identity_made")
        row_zeroed = sem("row_zeroed")
        keep_zeroed = sem("keep_zeroed")
        x_stats_taken = sem("x_stats_taken")
        c_stats_taken = sem("c_stats_taken")
        x_moments_step = sem("x_moments_step")
        c_moments_step = sem("c_moments_step")
        var_ready = sem("var_ready")
        scales_made = sem("scales_made")
        later_weights_loaded = sem("later_weights_loaded")
        with nc.Block() as block:
            @block.sync
            def _(sp):
                x_view = x_in.rearrange("b t d -> t b d")
                c_view = ctx_in.rearrange("b t d -> t b d")
                for g in range(NG):
                    sp.dma_start(X[:, g * GB:(g + 1) * GB, :], x_view[:, g * GB:(g + 1) * GB, :]).then_inc(x_loaded[g], 16)
                for g in range(NG):
                    sp.dma_start(CT[0:C, g * GB:(g + 1) * GB, :], c_view[:, g * GB:(g + 1) * GB, :]).then_inc(c_loaded[g], 16)
                sp.dma_start(wq[:, :], wq_in).then_inc(weights_loaded, 16)
                sp.dma_start(wkv[:, :], wkv_in).then_inc(weights_loaded, 16)
                sp.dma_start(wo[:, :, :], wo_in.rearrange("(c p) d -> p c d", p=P)).then_inc(weights_loaded, 16)
                sp.dma_start(lnow[:, :], lnow_in.broadcast_to([P, D])).then_inc(weights_loaded, 16)
                sp.dma_start(lnob[:, :], lnob_in.broadcast_to([P, D])).then_inc(weights_loaded, 16)
                sp.wait_ge(weights_loaded, 80)

            @block.scalar
            def _(act):
                act.dma_start(keep8[:, :], keep_in).then_inc(keep_loaded, 16)
                act.dma_start(cols[:, :], cols_in).then_inc(cols_loaded, 16)

            @block.gpsimd
            def _(pool):
                pool.memset(mhalf[:, :], -0.5)
                pool.memset(ident[:, :], 0.0).then_inc(zeroed, 1)
                pool.memset(ident_bf[:, :], 0.0).then_inc(zeroed, 1)
                pool.memset(ones[:, :], 1.0)
                pool.memset(first_row[:, :], 0.0).then_inc(row_zeroed, 1)
                pool.memset(keep_row[:, :, :].bitcast(U32), 0).then_inc(keep_zeroed, 1)
                pool.wait_ge(zeroed, 2)
                for m in (ident, ident_bf):
                    pool.affine_select(out=m[:, :], in_=m[:, :], compare_op=ALU.not_equal, fill=1.0, base=0,
                                       pattern=[[-1, P]], channel_multiplier=1).then_inc(identity_made, 1)
                pool.wait_ge(row_zeroed, 1)
                pool.memset(first_row[0:1, :], 1.0)
                for q in range(2):
                    pool.memset(QZ[q][:, :, :], 0.0)
                pool.memset(sq[:, :, :], 1.0)
                pool.memset(qk[:, :, :], 1.0)
                pool.wait_ge(var_ready, 2)
                inverse_roots(pool, rstd, small[:, 0, :], mhalf, slice(0, FIRST)).then_inc(scales_made, 1)
                inverse_roots(pool, rstd_c[0:C], small_c[0:C, 0, :], mhalf, slice(0, FIRST)).then_inc(scales_made, 1)
                pool.wait_ge(scales_made, 2)

            @block.vector
            def _(dve):
                for g in range(NG):
                    dve.wait_ge(x_loaded[g], 16)
                    for b in range(g * GB, (g + 1) * GB):
                        dve.bn_stats(stats6[:, b, :], X[:, b, :]).then_inc(x_stats_taken, 1)
                dve.wait_ge(x_stats_taken, B)
                moments(dve, stats6, mean, small, x_moments_step)
                dve.tensor_scalar(small[:, 0, :], small[:, 3, :], 1.0 + LN_EPS, LN_EPS * LN_EPS, ALU.mult, ALU.add).then_inc(var_ready, 1)
                for g in range(NG):
                    dve.wait_ge(c_loaded[g], 16)
                    for b in range(g * GB, (g + 1) * GB):
                        dve.bn_stats(stats6_c[0:C, b, :], CT[0:C, b, :]).then_inc(c_stats_taken, 1)
                dve.wait_ge(c_stats_taken, B)
                moments(dve, stats6_c[0:C], mean_c[0:C], small_c[0:C], c_moments_step)
                dve.tensor_scalar(small_c[0:C, 0, :], small_c[0:C, 3, :], LN_EPS, None, ALU.add).then_inc(var_ready, 1)
                dve.wait_ge(keep_loaded, 16)
                dve.wait_ge(keep_zeroed, 1)
                dve.tensor_scalar(keep_row[0:1, :, 0:C], keep8[:, :].rearrange("a (b c) -> a b c", b=B), 1.0, -NEG_MAX,
                                  ALU.subtract, ALU.mult)
                dve.wait_ge(cols_loaded, 16)
                dve.tensor_scalar(qk_scale[:, :], QS, KS, float(HD) ** 0.5, ALU.mult, ALU.mult)

        ln_x = sb("ln_x", [P, D])
        ln_c = sb("ln_c", [P, D])
        kvT = sb("kvT", [P, K])
        qkn = sb("qkn", [P, 3, INNER])
        ss = sb("ss", [P, 3 * H])
        ssm = sb("ssm", [P, 3 * H])
        r_norm = sb("r_norm", [P, 3 * H])
        KT = [sb(f"KT{i}", [P, 4, K]) for i in range(2)]
        VC = [sb(f"VC{i}", [P, INNER]) for i in range(2)]
        VL = [sb(f"VL{i}", [P, INNER]) for i in range(2)]
        y = sb("y", [P, D])
        y_stat = sb("y_stat", [P, 6])
        y_sums = sb("y_sums", [P, 2])
        y_diff = sb("y_diff", [P, 1])
        y_mean = sb("y_mean", [P, 1])
        y_within = sb("y_within", [P, 1])
        y_between = sb("y_between", [P, 1])
        y_var = sb("y_var", [P, 1])
        y_rstd = sb("y_rstd", [P, 1])
        y_norm = sb("y_norm", [P, D])
        y_w = sb("y_w", [P, D])
        y_wb = sb("y_wb", [P, D])

        names = ("ln_made ln_turned kvT_made squared qT_scaled q_proj q_copied kc_proj kc_copied kl_proj kl_copied vc_proj vc_copied "
                 "vl_proj vl_copied ss_summed ss_ready norm_inverted normed qT_turned qT_copied kcT_turned kcT_copied "
                 "klT_turned klT_copied y_stats y_aggr y_parts y_var_ready y_inverted y_normed y_weighted y_biased x_added "
                 "x_stats all_scales").split()
        s = {name: sem(name) for name in names}
        cell = {}

        def scale_qT(eng, par, half):
            r = slice(64 * half, 64 * half + 64)
            dst, src = QZ[par][r, half:H:2, :], psum[r, 7, :].rearrange("p (c q) -> p c q", c=4)
            if half == 0:
                return eng.activation(dst, src, ACT.Copy, scale=qk_scale[r, :])
            return eng.tensor_scalar(dst, src, qk_scale[r, :], None, ALU.mult)

        def score(pe, n, u, c):
            par = cell["par"]
            wait(pe, s["qT_copied"], n + 1)
            wait(pe, s["qT_scaled"], n + 1)
            wait(pe, s["kcT_copied"], n + 1)
            wait(pe, s["klT_copied"], n + 1)
            pe.matmul(psum[:, 2 * u + c, 0:2 * K], first_row[:, :], keep_row[:, entries(n), :].broadcast_to([P, 2, K]),
                      start=True, stop=False, skip_group_check=True)
            for j in range(2):
                h = 4 * u + 2 * c + j
                mm = pe.matmul(psum[:, 2 * u + c, j * K:(j + 1) * K], QZ[par][:, h, :], KT[par][:, h // 2, :],
                               start=False, stop=True, skip_group_check=True)
            return mm

        pt_plan = ([(j, 0, C) for j in range(4)], [(j, C, P) for j in range(4)])
        r_wide = [sb(f"r_wide{u}", [P, 4, HD]) for u in range(2)]
        r_spread = sb("r_spread", [P, 2, P])
        outT = sb("outT", [P, 4, P])
        sum_repeated = [sem(f"sum_repeated{u}") for u in range(2)]
        r_turned = [sem(f"r_turned{u}") for u in range(2)]
        r_copied = [sem(f"r_copied{u}") for u in range(2)]
        out_scaled = [sem(f"out_scaled{u}") for u in range(2)]
        projected = sem("projected")
        projection_taken = sem("projection_taken")

        def bank4_free(pe, n, u):
            wait(pe, r_copied[1 - u], n if u == 0 else n + 1)

        def bank5_free(pe, n, u):
            if u == 0:
                wait(pe, projection_taken, n)
            else:
                wait(pe, out_scaled[0], n + 1)

        t = softmax_units(nc, st, sem, psum, 4, K, pt_plan, score, bank4_free, bank5_free, ident, "l0")
        pv_done, probsT = t["pv_done"], t["probsT"]

        def invert_sums(dve, n, u):
            t["dve_invert"](dve, n, u)
            wait(dve, r_turned[u], n)
            dve.tensor_copy(r_wide[u][:, :, :], t["r_sums"][u][:, :].unsqueeze(2).broadcast_to([P, 4, HD])).then_inc(sum_repeated[u], 1)

        def turn_sums(pe, n, u):
            wait(pe, sum_repeated[u], n + 1)
            wait(pe, t["pt0_copied"][u], n + 1)
            for b in range(2):
                tr = pe.transpose(psum[:, 4, b * P:(b + 1) * P],
                                  r_wide[u][:, 2 * b:2 * b + 2, :].rearrange("p h w -> p (h w)"), ident[:, :])
            tr.then_inc(r_turned[u], 1)

        def copy_sums(act, n, u):
            wait(act, r_turned[u], n + 1)
            wait(act, out_scaled[1 - u], n if u == 0 else n + 1)
            act.copy(r_spread[:, :, :], psum[:, 4, 0:2 * P].rearrange("p (b q) -> p b q", b=2)).then_inc(r_copied[u], 1)

        def multiply_v(pe, n, u, par):
            wait(pe, t["pt0_copied"][u], n + 1)
            wait(pe, t["pt1_copied"][u], n + 1)
            for j in range(4):
                h = 4 * u + j
                o = psum[HD * (j % 2):HD * (j % 2) + HD, 5, (j // 2) * P:(j // 2 + 1) * P]
                pe.matmul(o, VC[par][0:C, h * HD:(h + 1) * HD], probsT[u][0:C, 0, j, :], start=True, stop=False,
                          skip_group_check=True)
                mm = pe.matmul(o, VL[par][:, h * HD:(h + 1) * HD], probsT[u][:, 1, j, :], start=False, stop=True,
                               skip_group_check=True)
            mm.then_inc(pv_done[u], 1)

        def scale_out(dve, n, u):
            wait(dve, pv_done[u], n + 1)
            wait(dve, r_copied[u], n + 1)
            if u == 0:
                wait(dve, projected, n)
            dve.tensor_tensor(outT[:, 2 * u:2 * u + 2, :], psum[:, 5, 0:256].rearrange("p (b q) -> p b q", b=2),
                              r_spread[:, :, :], ALU.mult).then_inc(out_scaled[u], 1)

        def project(pe, n):
            wait(pe, out_scaled[1], n + 1)
            for c in range(4):
                mm = pe.matmul(psum[:, 5, 0:D], outT[:, c, :], wo[:, c, :], start=(c == 0), stop=(c == 3))
            mm.then_inc(projected, 1)

        with nc.Block() as block:
            @block.tensor
            def _(pe):
                def values_c(m):
                    wait(pe, s["klT_copied"], m)
                    pe.matmul(psum[0:C, 6, :], kvT[:, 0:C], wkv[:, INNER:], start=True, stop=True).then_inc(s["vc_proj"], 1)

                def values_x(m):
                    wait(pe, s["qT_copied"], m)
                    wait(pe, s["qT_scaled"], m)
                    pe.matmul(psum[:, 7, :], kvT[:, C:K], wkv[:, INNER:], start=True, stop=True).then_inc(s["vl_proj"], 1)

                def turn_inputs(m):
                    wait(pe, s["ln_made"], m + 1)
                    wait(pe, s["vc_copied"], m)
                    pe.transpose(psum[:, 6, 0:C], ln_c[0:C, :], ident[0:C, 0:C])
                    pe.transpose(psum[:, 6, P:2 * P], ln_x[:, :], ident[:, :]).then_inc(s["ln_turned"], 1)

                def project_q_kc(m):
                    wait(pe, s["kvT_made"], m + 1)
                    wait(pe, s["vl_copied"], m)
                    pe.matmul(psum[:, 7, :], kvT[:, C:K], wq[:, :], start=True, stop=True).then_inc(s["q_proj"], 1)
                    pe.matmul(psum[0:C, 6, :], kvT[:, 0:C], wkv[:, 0:INNER], start=True, stop=True).then_inc(s["kc_proj"], 1)

                def project_kl(m):
                    wait(pe, s["q_copied"], m + 1)
                    pe.matmul(psum[:, 7, :], kvT[:, C:K], wkv[:, 0:INNER], start=True, stop=True).then_inc(s["kl_proj"], 1)

                def turn_q_kc(m, others):
                    wait(pe, s["normed"], m + 1)
                    wait(pe, s["kc_copied"], m + 1 + others)
                    for c in range(4):
                        tr = pe.transpose(psum[:, 6, c * C:(c + 1) * C], qkn[0:C, 1, c * P:(c + 1) * P], ident[0:C, 0:C])
                    tr.then_inc(s["kcT_turned"], 1)
                    wait(pe, s["kl_copied"], m + 1 + others)
                    for c in range(4):
                        tr = pe.transpose(psum[:, 7, c * P:(c + 1) * P], qkn[:, 0, c * P:(c + 1) * P], ident[:, :])
                    tr.then_inc(s["qT_turned"], 1)

                def turn_kl(m):
                    wait(pe, s["kcT_copied"], m + 1)
                    for c in range(4):
                        tr = pe.transpose(psum[:, 6, c * P:(c + 1) * P], qkn[:, 2, c * P:(c + 1) * P], ident[:, :])
                    tr.then_inc(s["klT_turned"], 1)

                def scores(n, u, par, banks=(0, 1)):
                    cell["par"] = par
                    for bank in banks:
                        t["pe_scores"](pe, n, u, bank)

                def body(n, par, first=False, next_=True, after=True):
                    if not first:
                        project(pe, n - 1)
                    if next_:
                        values_c(n + 1)
                    t["pe_turn_probs0"](pe, n, 0)
                    t["pe_turn_probs1"](pe, n, 0)
                    if next_:
                        values_x(n + 1)
                    if after:
                        turn_inputs(n + 2)
                    turn_sums(pe, n, 0)
                    multiply_v(pe, n, 0, par)
                    if after:
                        project_q_kc(n + 2)
                    t["pe_turn_probs0"](pe, n, 1)
                    if after:
                        project_kl(n + 2)
                    t["pe_turn_probs1"](pe, n, 1)
                    if next_:
                        turn_q_kc(n + 1, others=after)
                    turn_sums(pe, n, 1)
                    if next_:
                        turn_kl(n + 1)
                    multiply_v(pe, n, 1, par)
                    if next_:
                        scores(n + 1, 0, 1 - par)
                        scores(n + 1, 1, 1 - par)

                turn_inputs(0)
                project_q_kc(0)
                project_kl(0)
                turn_q_kc(0, others=False)
                turn_kl(0)
                wait(pe, s["klT_copied"], 1)
                wait(pe, s["qT_copied"], 1)
                wait(pe, s["qT_scaled"], 1)
                values_c(0)
                values_x(0)
                scores(0, 0, 0)
                scores(0, 1, 0)
                turn_inputs(1)
                project_q_kc(1)
                project_kl(1)
                wait(pe, s["kc_copied"], 2)
                wait(pe, s["kl_copied"], 2)
                run_entries(pe, body)
                project(pe, B - 1)

            @block.scalar
            def _(act):
                def copy_values_c(m, par):
                    wait(act, s["vc_proj"], m + 1)
                    wait(act, t["pv_done"][1], m - 1)
                    act.copy(VC[par][0:C, :], psum[0:C, 6, :]).then_inc(s["vc_copied"], 1)

                def copy_values_x(m, par):
                    wait(act, s["vl_proj"], m + 1)
                    act.copy(VL[par][:, :], psum[:, 7, :]).then_inc(s["vl_copied"], 1)

                def make_kvT(m):
                    wait(act, s["ln_turned"], m + 1)
                    wait(act, s["vl_proj"], m)
                    act.activation(kvT[:, 0:C], psum[:, 6, 0:C], ACT.Identity, bias=LNX_B, scale=LNX_W)
                    act.activation(kvT[:, C:K], psum[:, 6, P:2 * P], ACT.Identity, bias=LNL_B,
                                   scale=LNL_W).then_inc(s["kvT_made"], 1)

                def copy_qk(m):
                    wait(act, s["normed"], m)
                    for i, (proj, copied, bank, rows) in enumerate((("q_proj", "q_copied", 7, P), ("kc_proj", "kc_copied", 6, C),
                                                                    ("kl_proj", "kl_copied", 7, P))):
                        wait(act, s[proj], m + 1)
                        act.copy(qk[0:rows, i, :], psum[0:rows, bank, :]).then_inc(s[copied], 1)

                def square_qk(m):
                    wait(act, s["kl_copied"], m + 1)
                    wait(act, s["ss_summed"], m)
                    act.activation(sq[:, :, :], qk[:, :, :], ACT.Square).then_inc(s["squared"], 1)

                def copy_kcT(m, par):
                    wait(act, s["kcT_turned"], m + 1)
                    wait(act, t["scored"][1], m - 1)
                    act.copy(KT[par][:, :, 0:C], psum[:, 6, 0:4 * C].rearrange("p (c k) -> p c k", c=4)).then_inc(s["kcT_copied"], 1)

                def copy_qT(m, par):
                    wait(act, s["qT_turned"], m + 1)
                    wait(act, t["scored"][1], m - 1)
                    scale_qT(act, par, 0).then_inc(s["qT_copied"], 1)

                def take_projection(n):
                    wait(act, projected, n + 1)
                    wait(act, s["y_normed"], n)
                    act.copy(y[:, :], psum[:, 5, 0:D]).then_inc(projection_taken, 1)

                def body(n, par, first=False, next_=True, after=True):
                    if not first:
                        take_projection(n - 1)
                    if next_:
                        copy_values_c(n + 1, 1 - par)
                    t["act_copy_pt0"](act, n, 0)
                    if next_:
                        copy_values_x(n + 1, 1 - par)
                    if after:
                        make_kvT(n + 2)
                    copy_sums(act, n, 0)
                    t["act_exp"](act, n, 1)
                    if after:
                        copy_qk(n + 2)
                    t["act_copy_pt0"](act, n, 1)
                    if next_:
                        copy_kcT(n + 1, 1 - par)
                        copy_qT(n + 1, 1 - par)
                    copy_sums(act, n, 1)
                    if after:
                        square_qk(n + 2)
                    if next_:
                        t["act_exp"](act, n + 1, 0)

                make_kvT(0)
                copy_qk(0)
                square_qk(0)
                copy_kcT(0, 0)
                copy_qT(0, 0)
                copy_values_c(0, 0)
                copy_values_x(0, 0)
                t["act_exp"](act, 0, 0)
                make_kvT(1)
                copy_qk(1)
                square_qk(1)
                run_entries(act, body)
                take_projection(B - 1)

            @block.vector
            def _(dve):
                def norm_inputs(m):
                    wait(dve, s["ln_turned"], m)
                    dve.tensor_scalar(ln_x[:, :], X[:, entries(m), :].rearrange("p a d -> p (a d)"), mean[:, entries(m)], rstd[:, entries(m)],
                                      ALU.subtract, ALU.mult)
                    dve.tensor_scalar(ln_c[0:C, :], CT[0:C, entries(m), :].rearrange("p a d -> p (a d)"), mean_c[0:C, entries(m)],
                                      rstd_c[0:C, entries(m)], ALU.subtract, ALU.mult).then_inc(s["ln_made"], 1)

                def sum_squares(m):
                    wait(dve, s["squared"], m + 1)
                    dve.tensor_reduce(ss[:, :], sq[:, :, :].rearrange("p a (h d) -> p (a h) d", d=HD), AX.X,
                                      ALU.add).then_inc(s["ss_summed"], 1)
                    wait(dve, s["ss_summed"], m + 1)
                    wait(dve, s["norm_inverted"], m)
                    dve.tensor_scalar(ssm[:, :], ss[:, :], 1e-24, None, ALU.max).then_inc(s["ss_ready"], 1)

                def copy_qT(m, par):
                    wait(dve, s["qT_turned"], m + 1)
                    wait(dve, t["scored"][1], m - 1)
                    scale_qT(dve, par, 1).then_inc(s["qT_scaled"], 1)

                def copy_kl(m, par):
                    wait(dve, s["klT_turned"], m + 1)
                    dve.tensor_copy(KT[par][:, :, C:K], psum[:, 6, :].rearrange("p (c k) -> p c k", c=4)).then_inc(s["klT_copied"], 1)

                def y_moments(n):
                    wait(dve, projection_taken, n + 1)
                    dve.bn_stats(y_stat[:, :], y[:, :]).then_inc(s["y_stats"], 1)
                    wait(dve, s["y_stats"], n + 1)
                    dve.tensor_tensor(y_sums[:, :], y_stat[:, 1:3], y_stat[:, 4:6], ALU.add)
                    dve.tensor_tensor(y_diff[:, :], y_stat[:, 1:2], y_stat[:, 4:5], ALU.subtract).then_inc(s["y_aggr"], 1)
                    wait(dve, s["y_aggr"], n + 1)
                    dve.tensor_scalar(y_mean[:, :], y_sums[:, 0:1], 0.5, None, ALU.mult)
                    dve.tensor_scalar(y_within[:, :], y_sums[:, 1:2], 1.0 / D, LN_EPS, ALU.mult, ALU.add)
                    dve.scalar_tensor_tensor(y_between[:, :], y_diff[:, :], 0.25, y_diff[:, :], ALU.mult,
                                             ALU.mult).then_inc(s["y_parts"], 1)
                    wait(dve, s["y_parts"], n + 1)
                    wait(dve, s["y_inverted"], n)
                    dve.tensor_tensor(y_var[:, :], y_within[:, :], y_between[:, :], ALU.add).then_inc(s["y_var_ready"], 1)

                def y_normalize(n):
                    wait(dve, s["y_inverted"], n + 1)
                    wait(dve, s["y_weighted"], n)
                    dve.tensor_scalar(y_norm[:, :], y[:, :], y_mean[:, :], y_rstd[:, :], ALU.subtract,
                                      ALU.mult).then_inc(s["y_normed"], 1)

                def x_moments(n):
                    wait_apart(dve, s["x_added"], n + 1, s["all_scales"])
                    dve.bn_stats(stats6[:, entries(n), :].rearrange("p a d -> p (a d)"),
                                 X[:, entries(n), :].rearrange("p a d -> p (a d)")).then_inc(s["x_stats"], 1)

                def body(n, par, first=False, next_=True, after=True):
                    if not first:
                        scale_out(dve, n - 1, 1)
                    if after:
                        norm_inputs(n + 2)
                    invert_sums(dve, n, 0)
                    t["dve_max"](dve, n, 1)
                    t["dve_copy_pt1"](dve, n, 0)
                    if not first:
                        y_moments(n - 1)
                    scale_out(dve, n, 0)
                    invert_sums(dve, n, 1)
                    if not first:
                        y_normalize(n - 1)
                    t["dve_copy_pt1"](dve, n, 1)
                    if next_:
                        copy_qT(n + 1, 1 - par)
                        copy_kl(n + 1, 1 - par)
                    if not first:
                        x_moments(n - 1)
                    if after:
                        sum_squares(n + 2)
                    if next_:
                        t["dve_max"](dve, n + 1, 0)

                norm_inputs(0)
                sum_squares(0)
                copy_qT(0, 0)
                copy_kl(0, 0)
                t["dve_max"](dve, 0, 0)
                norm_inputs(1)
                sum_squares(1)
                run_entries(dve, body, before_loop=lambda: wait(dve, s["all_scales"], 2))
                scale_out(dve, B - 1, 1)
                y_moments(B - 1)
                y_normalize(B - 1)
                x_moments(B - 1)

            @block.gpsimd
            def _(pool):
                def norm_qk(m):
                    wait(pool, s["ss_ready"], m + 1)
                    pool.tensor_tensor(r_norm[:, :], ssm[:, :], mhalf[:, 0:3 * H], ALU.pow).then_inc(s["norm_inverted"], 1)
                    wait(pool, s["norm_inverted"], m + 1)
                    wait(pool, s["klT_turned"], m)
                    pool.tensor_tensor(qkn[:, :, :].rearrange("p a (h d) -> p (a h) d", d=HD),
                                       qk[:, :, :].rearrange("p a (h d) -> p (a h) d", d=HD),
                                       r_norm[:, :].unsqueeze(2).broadcast_to([P, 3 * H, HD]), ALU.mult).then_inc(s["normed"], 1)

                def finish(n):
                    wait(pool, s["y_var_ready"], n + 1)
                    pool.tensor_tensor(y_rstd[:, :], y_var[:, :], mhalf[:, 0:1], ALU.pow).then_inc(s["y_inverted"], 1)

                def add(n):
                    wait(pool, s["y_normed"], n + 1)
                    pool.tensor_tensor(y_w[:, :], y_norm[:, :], lnow[:, :], ALU.mult).then_inc(s["y_weighted"], 1)
                    wait(pool, s["y_weighted"], n + 1)
                    pool.tensor_tensor(y_wb[:, :], y_w[:, :], lnob[:, :], ALU.add).then_inc(s["y_biased"], 1)
                    wait(pool, s["y_biased"], n + 1)
                    xs = X[:, entries(n), :].rearrange("p a d -> p (a d)")
                    pool.tensor_tensor(xs, xs, y_wb[:, :], ALU.add).then_inc(s["x_added"], 1)

                def body(n, par, first=False, next_=True, after=True):
                    if not first:
                        finish(n - 1)
                        add(n - 1)
                    if after:
                        norm_qk(n + 2)

                norm_qk(0)
                inverse_roots(pool, rstd, small[:, 0, :], mhalf, slice(FIRST, B)).then_inc(s["all_scales"], 1)
                inverse_roots(pool, rstd_c[0:C], small_c[0:C, 0, :], mhalf, slice(FIRST, B)).then_inc(s["all_scales"], 1)
                norm_qk(1)
                run_entries(pool, body)
                finish(B - 1)
                add(B - 1)

            @block.sync
            def _(sp):
                for tile, src in later_weights:
                    sp.dma_start(tile[...], src).then_inc(later_weights_loaded, 16)
                sp.wait_ge(later_weights_loaded, 16 * len(later_weights))


def l0_ffn(nc, psum, X, X2, XN, stats6, mean, rstd, mhalf, small, ident, ones, weights):
    with ExitStack() as sems, ExitStack() as st:
        def sb(name, shape, dt=F32):
            return st.enter_context(nc.sbuf_tensor(name, shape, dt))

        wm, wp, wc1, wc2 = (weights[k] for k in ("wm", "wp", "wc1", "wc2"))
        pooledT = sb("pooledT", [D, B])
        same_entry = sb("same_entry", [P, P])
        earlier = sb("earlier", [P, P])
        history = sb("history", [P, Q4])
        maskT = sb("maskT", [P, 3, P])
        done = sb("done", [P, 1], I32)
        bufs = dict(
            zn=sb("zn", [P, GB, D]), zT=sb("zT", [D, GB * P]), hT=[sb(f"hT{i}", [P, GB * P]) for i in range(4)],
            yT=sb("yT", [D, GB * P]), pool4=sb("pool4", [D, GB]))

        with signals(nc, "ffn") as sem:
            var_ready, router_consts = sem("var_ready"), sem("router_consts")
            powed, moments_step = sem("powed"), sem("moments_step")
            with nc.Block() as block:
                @block.vector
                def _(dve):
                    moments(dve, stats6, mean, small, moments_step)
                    dve.tensor_scalar(small[:, 0, :], small[:, 3, :], LN_EPS, None, ALU.add).then_inc(var_ready, 1)
                    dve.memset(done[:, :], 0)
                    dve.memset(history[:, :], 0.0).then_inc(moments_step, 1)
                    dve.wait_ge(moments_step, 7)
                    dve.memset(history[0:32, :], 1.0)
                    dve.memset(history[32:64, 0:F_ITER - Q4], 1.0)

                @block.gpsimd
                def _(pool):
                    pool.memset(same_entry[:, :], 0.0).then_inc(router_consts, 1)
                    pool.memset(earlier[:, :], 0.0).then_inc(router_consts, 1)
                    pool.wait_ge(var_ready, 1)
                    inverse_roots(pool, rstd, small[:, 0, :], mhalf, slice(0, GB)).then_inc(powed, 1)
                    n = 2
                    for q in range(4):
                        pool.wait_ge(router_consts, n)
                        v = same_entry[:, :].rearrange("p (a c) -> p a c", a=4)
                        pool.affine_select(out=v, in_=v, compare_op=ALU.not_equal, fill=1.0, base=-32 * q,
                                           pattern=[[0, 4], [-1, 32]], channel_multiplier=1).then_inc(router_consts, 1)
                        n += 1
                        if q < 3:
                            later, pattern = earlier[:, 32 * (q + 1):], [[-1, 32]]
                            if q < 2:
                                later = later.rearrange("p (a c) -> p a c", a=3 - q)
                                pattern = [[0, 3 - q], [-1, 32]]
                            pool.affine_select(out=later, in_=later, compare_op=ALU.not_equal, fill=1.0, base=-32 * q,
                                               pattern=pattern, channel_multiplier=1).then_inc(router_consts, 1)
                            n += 1
                    pool.wait_ge(router_consts, n)

        ffn_step(nc, psum, bufs, X, X, X2, XN, stats6, mean, (rstd, small, mhalf), wm, wp, None, pooledT, ident, None, 1)
        route(nc, psum, pooledT, wc1, wc2, same_entry, earlier, history, maskT, done, ident, ones, None, 1)
        for step in (2, 3):
            ffn_step(nc, psum, bufs, XN, X, X2, XN, stats6, None, None, wm, wp, maskT, pooledT, ident, done, step)
            if step == 2:
                route(nc, psum, pooledT, wc1, wc2, same_entry, earlier, history, maskT, done, ident, ones, done, step)


def moments(dve, stats6, mean, small, step):
    m_even, v_even, m_odd, v_odd = (stats6[:, :, i] for i in (1, 2, 4, 5))
    dve.tensor_tensor(small[:, 0, :], m_even, m_odd, ALU.add)
    dve.tensor_tensor(small[:, 1, :], m_even, m_odd, ALU.subtract)
    dve.tensor_tensor(small[:, 2, :], v_even, v_odd, ALU.add).then_inc(step, 3)
    dve.wait_ge(step, 3)
    dve.tensor_scalar(mean[:, :], small[:, 0, :], 0.5, None, ALU.mult).then_inc(step, 1)
    dve.scalar_tensor_tensor(small[:, 3, :], small[:, 1, :], 0.25, small[:, 1, :], ALU.mult, ALU.mult).then_inc(step, 1)
    dve.wait_ge(step, 5)
    dve.scalar_tensor_tensor(small[:, 3, :], small[:, 2, :], 1.0 / D, small[:, 3, :], ALU.mult, ALU.add).then_inc(step, 1)
    dve.wait_ge(step, 6)


def entries(n, count=1):
    return slice(n, n + count) if isinstance(n, int) else bass.ds(n, count)


@contextmanager
def where_not_done(eng, done):
    if done is None:
        yield
    else:
        flag = eng.value_load(done[0:1, 0:1], min_val=0, max_val=1)
        with eng.If(flag == 0):
            yield


def ffn_step(nc, psum, bufs, SRC, X, X2, XN, stats6, mean, scales, wm, wp, maskT, pooledT, ident, done, step):
    chunks = 4 if maskT is None else F_FULL // P
    zn, zT, hT, yT, pool4 = (bufs[k] for k in ("zn", "zT", "hT", "yT", "pool4"))
    ring = 3
    with ExitStack() as sems, ExitStack() as st:
        sem = sems.enter_context(signals(nc, f"ffn_step{step}"))
        in_ready = sem("in_ready")
        in_turned = sem("in_turned")
        in_copied = sem("in_copied")
        hidden = [sem(f"hidden{f}") for f in range(chunks)]
        activated = [sem(f"activated{f}") for f in range(chunks)]
        multiplied = [sem(f"multiplied{f}") for f in range(chunks)]
        out_copied = sem("out_copied")
        out_summed = sem("out_summed")
        out_pooled = sem("out_pooled")
        out_turned = sem("out_turned")
        xn_written = sem("xn_written")
        x_added = sem("ffn_x_added")
        x_stats = sem("ffn_x_stats")
        all_scales = sem("all_scales")
        rstd = scales[0] if scales else None

        def last_in_ring(f, size):
            return (f - size, 0) if f >= size else (max(c for c in range(chunks) if c % size == f % size), 1)

        block = st.enter_context(nc.Block())

        @block.tensor
        def _(pe):
            def turn_back(g):
                wait(pe, out_copied, g + 1)
                wait(pe, x_added, g)
                for b in range(GB):
                    tr = pe.transpose(psum[:, 7, b * P:(b + 1) * P], yT[:, b * P:(b + 1) * P], ident[:, :])
                tr.then_inc(out_turned, 1)

            def up(g, f):
                before, back = last_in_ring(f, ring)
                wait(pe, activated[before], g + 1 - back)
                pe.matmul(psum[:, f % ring, :], wm[:, f * P:(f + 1) * P], zT[:, :], start=True, stop=True).then_inc(hidden[f], 1)

            def down(g, f):
                wait(pe, activated[f], g + 1)
                if f == 0:
                    wait(pe, out_copied, g)
                    wait(pe, out_summed, g)
                pe.matmul(psum[:, 4, :], wp[:, f, :], hT[f % 4][:, :], start=(f == 0), stop=(f == chunks - 1)).then_inc(multiplied[f], 1)

            def turn_in(g):
                wait(pe, in_ready, g + 1)
                wait(pe, in_copied, g)
                for b in range(GB):
                    tr = pe.transpose(psum[:, 6, b * P:(b + 1) * P], zn[:, b, :], ident[:, :])
                tr.then_inc(in_turned, 1)

            def body(g, first=False, final=False):
                wait(pe, in_copied, g + 1)
                up(g, 0)
                up(g, 1)
                if not first:
                    turn_back(g - 1)
                for f in range(chunks):
                    if f + 2 < chunks:
                        up(g, f + 2)
                    if f == chunks - 2 and not final:
                        turn_in(g + 1)
                    down(g, f)

            with where_not_done(pe, done):
                turn_in(0)
                body(0, first=True)
                with pe.Fori(0, NG - 2) as i:
                    body(i + 1)
                body(NG - 1, final=True)
                turn_back(NG - 1)

        @block.scalar
        def _(act):
            def copy_in(g):
                wait(act, in_turned, g + 1)
                wait(act, hidden[chunks - 1], g)
                act.copy(zT[:, :], psum[:, 6, :]).then_inc(in_copied, 1)

            def body(g, final=False):
                if maskT is None:
                    for f in range(0, chunks, 2):
                        wait(act, hidden[f], g + 1)
                        before, back = last_in_ring(f, 4)
                        wait(act, multiplied[before], g + 1 - back)
                        act.activation(hT[f % 4][:, :], psum[:, f % ring, :], ACT.Relu).then_inc(activated[f], 1)
                if not final:
                    copy_in(g + 1)
                wait(act, multiplied[chunks - 1], g + 1)
                wait(act, out_turned, g)
                wait(act, out_summed, g)
                act.copy(yT[:, :], psum[:, 4, :]).then_inc(out_copied, 1)

            with where_not_done(act, done):
                copy_in(0)
                body(0)
                with act.Fori(0, NG - 2) as i:
                    body(i + 1)
                body(NG - 1, final=True)

        if scales:
            @block.gpsimd
            def _(pool):
                inverse_roots(pool, rstd, scales[1][:, 0, :], scales[2], slice(GB, B)).then_inc(all_scales, 1)

        @block.vector
        def _(dve):
            def load_in(g):
                wait(dve, in_turned, g)
                for b in range(GB):
                    n = g * GB + b
                    src = SRC[:, entries(n), :].rearrange("p a d -> p (a d)")
                    if mean is None:
                        i = dve.tensor_scalar(zn[:, b, :], src, 1.0, None, ALU.mult)
                    else:
                        i = dve.tensor_scalar(zn[:, b, :], src, mean[:, entries(n)], rstd[:, entries(n)], ALU.subtract, ALU.mult)
                i.then_inc(in_ready, 1)

            def activate(g, f):
                wait(dve, hidden[f], g + 1)
                before, back = last_in_ring(f, 4)
                wait(dve, multiplied[before], g + 1 - back)
                if maskT is None:
                    i = dve.tensor_scalar(hT[f % 4][:, :], psum[:, f % ring, :], 0.0, None, ALU.max)
                else:
                    active = maskT[:, f % 3, entries(g * GB + (f // 3) * B, GB)].unsqueeze(2).broadcast_to([P, GB, P])
                    i = dve.scalar_tensor_tensor(hT[f % 4][:, :].rearrange("p (b t) -> p b t", b=GB),
                                                 psum[:, f % ring, :].rearrange("p (b t) -> p b t", b=GB), 0.0, active,
                                                 ALU.max, ALU.mult)
                i.then_inc(activated[f], 1)

            def pool_out(g):
                wait(dve, out_copied, g + 1)
                wait(dve, out_pooled, g)
                dve.tensor_reduce(pool4[:, :], yT[:, :].rearrange("p (b t) -> p b t", b=GB), AX.X,
                                  ALU.add).then_inc(out_summed, 1)
                wait(dve, out_summed, g + 1)
                dve.tensor_scalar(pooledT[:, entries(g * GB, GB)], pool4[:, :], 1.0 / P, None, ALU.mult).then_inc(out_pooled, 1)

            def write_out(g):
                o = psum[:, 7, :].rearrange("p (b d) -> p b d", b=GB)
                wait(dve, out_turned, g + 1)
                dve.tensor_scalar(XN[:, entries(g * GB, GB), :], o, 1.0, None, ALU.mult).then_inc(xn_written, 1)
                wait(dve, xn_written, g + 1)
                dve.tensor_tensor(X2[:, entries(g * GB, GB), :], o, X[:, entries(g * GB, GB), :], ALU.add).then_inc(x_added, 1)
                wait_apart(dve, x_added, g + 1, in_ready)
                for b in range(GB):
                    n = g * GB + b
                    i = dve.bn_stats(stats6[:, entries(n), :].rearrange("p a d -> p (a d)"),
                                     X2[:, entries(n), :].rearrange("p a d -> p (a d)"))
                i.then_inc(x_stats, 1)

            def body(g, first=False, final=False):
                for k, f in enumerate(range(1, chunks, 2) if maskT is None else range(chunks)):
                    activate(g, f)
                    if k == 0 and not final:
                        load_in(g + 1)
                if not first:
                    write_out(g - 1)
                pool_out(g)

            with where_not_done(dve, done):
                load_in(0)
                if scales:
                    wait(dve, all_scales, 1)
                body(0, first=True)
                with dve.Fori(0, NG - 2) as i:
                    body(i + 1)
                body(NG - 1, final=True)
                write_out(NG - 1)


def wait_apart(eng, sem, value, met):
    eng.wait_ge(met, 1)
    wait(eng, sem, value)


def route(nc, psum, pooledT, wc1, wc2, same_entry, earlier, history, maskT, done, ident, ones, flag, step):
    with ExitStack() as sems, ExitStack() as st:
        def sb(name, shape, dt=F32):
            return st.enter_context(nc.sbuf_tensor(f"{name}_{step}", shape, dt))

        sem = sems.enter_context(signals(nc, f"route{step}"))
        zr = sb("zr", [32, B])
        logits = sb("logits", [P, Q4])
        u = sb("u", [P, Q4])
        hits = [sb(f"hit{d}", [P, Q4]) for d in range(3)]
        hit = hits[0]
        equal = sb("equal", [P, Q4])
        rank = sb("rank", [P, Q4])
        chosen = sb("chosen", [P, Q4])
        combined = sb("combined", [P, Q4])
        count = sb("count", [P, 3])
        positive = sb("positive", [P, 1])
        sign = sb("sign", [P, 1])
        wanted = sb("wanted", [P, 1])
        bits = sb("bits", [P, 3], I32)
        found = sb("found", [P, 1], I32)
        trial = sb("trial", [P, 3], I32)
        enough = sb("enough", [P, 3])
        digit = sb("digit", [P, 1])
        gained = sb("gained", [P, 1], I32)
        threshold = sb("threshold", [P, 1])
        offset = sb("offset", [P, 1])
        need = sb("need", [P, 1])
        novelty = sb("novelty", [P, 1])
        little = sb("little", [P, 1], I32)

        z_done = sem("z_done")
        z_taken = sem("z_taken")
        logits_done = sem("logits_done")
        counted = sem("counted")
        totalled = sem("totalled")
        dve_step = sem("dve_step")
        mask_ready = sem("mask_ready")
        mask_turned = sem("mask_turned")
        DIGITS = 15
        UNROLL = 5
        total = psum[:, 2, 0:1]

        block = st.enter_context(nc.Block())

        @block.tensor
        def _(pe):
            with where_not_done(pe, flag):
                pe.matmul(psum[0:32, 0, 0:B], wc1[:, :], pooledT[:, :], start=True, stop=True).then_inc(z_done, 1)
                pe.wait_ge(z_taken, 1)
                for q in range(4):
                    mm = pe.matmul(psum[32 * q:32 * q + 32, 1, 0:Q4], zr[:, :], wc2[:, q * Q4:(q + 1) * Q4], start=True, stop=True)
                mm.then_inc(logits_done, 1)
                pe.wait_ge(counted, 1)
                pe.matmul(total, same_entry[:, :], count[:, 0:1], start=True, stop=True).then_inc(totalled, 1)
                def total_trials(round_):
                    pe.wait_ge(counted, round_ + 2)
                    pe.matmul(psum[:, 2, 0:3], same_entry[:, :], count[:, :], start=True, stop=True).then_inc(totalled, 1)

                with pe.Fori(0, DIGITS // UNROLL) as i:
                    for k in range(UNROLL):
                        total_trials(i * UNROLL + k)
                total_trials(DIGITS)
                pe.wait_ge(counted, DIGITS + 3)
                pe.matmul(total, same_entry[:, :], count[:, 0:1], start=True, stop=True)
                pe.matmul(psum[:, 3, 0:1], earlier[:, :], count[:, 1:2], start=True, stop=True).then_inc(totalled, 1)
                pe.wait_ge(mask_ready, 1)
                for j in range(3):
                    pe.transpose(psum[:, 5, j * P:(j + 1) * P], chosen[:, j * P:(j + 1) * P], ident[:, :])
                pe.matmul(psum[:, 6, 0:1], ones[:, :], count[:, 0:1], start=True, stop=True).then_inc(mask_turned, 1)

        @block.scalar
        def _(act):
            with where_not_done(act, flag):
                act.wait_ge(z_done, 1)
                act.activation(zr[:, :], psum[0:32, 0, 0:B], ACT.Relu).then_inc(z_taken, 1)

        @block.vector
        def _(dve):
            at = [0]

            def then(ins):
                at[0] += 1
                ins.then_inc(dve_step, 1)
                dve.wait_ge(dve_step, at[0])

            with where_not_done(dve, flag):
                dve.wait_ge(logits_done, 1)
                dve.memset(count[:, :], 0.0)
                then(dve.tensor_copy(logits[:, :], psum[:, 1, 0:Q4]))
                dve.tensor_scalar(hit[:, :], logits[:, :], 0.0, None, ALU.is_ge, ALU.add, accum_out=count[:, 0:1]).then_inc(counted, 1)
                for d in range(3):
                    dve.memset(bits[:, d:d + 1], (d + 1) << (2 * DIGITS - 1))
                dve.memset(found[:, :], 0)
                dve.wait_ge(totalled, 1)
                then(dve.tensor_scalar(positive[:, :], total, float(F_ITER), None, ALU.is_ge))
                dve.tensor_scalar(sign[:, :], positive[:, :], 2.0, -1.0, ALU.mult, ALU.add)
                then(dve.tensor_scalar(wanted[:, :], positive[:, :], float(2 * F_ITER - F_FULL - 1), float(F_FULL - F_ITER + 1),
                                       ALU.mult, ALU.add))
                then(dve.tensor_scalar(u[:, :], logits[:, :], sign[:, :], None, ALU.mult))
                done_so_far = at[0]


                def count_trials(base, trials, round_):
                    dve.tensor_tensor(trial[:, 0:trials], found[:, :].broadcast_to([P, trials]), bits[:, 0:trials],
                                      ALU.bitwise_or).then_inc(dve_step, 1)
                    dve.wait_ge(dve_step, base + 1)
                    for d in range(trials):
                        c = dve.tensor_scalar(hits[d][:, :], u[:, :], trial[:, d:d + 1].bitcast(F32), None, ALU.is_ge, ALU.add,
                                              accum_out=count[:, d:d + 1])
                    c.then_inc(counted, 1)
                    dve.wait_ge(totalled, round_ + 2)
                    dve.tensor_scalar(enough[:, 0:trials], psum[:, 2, 0:trials], wanted[:, :], None, ALU.is_ge, ALU.add,
                                      accum_out=digit[:, :]).then_inc(dve_step, 1)
                    dve.wait_ge(dve_step, base + 2)
                    dve.tensor_tensor(gained[:, :], digit[:, :], bits[:, 0:1], ALU.mult).then_inc(dve_step, 1)
                    dve.wait_ge(dve_step, base + 3)
                    dve.tensor_tensor(found[:, :], found[:, :], gained[:, :], ALU.bitwise_or)

                per_digit = 4
                with dve.Fori(0, DIGITS // UNROLL) as i:
                    for k in range(UNROLL):
                        base = i * (UNROLL * per_digit) + (k * per_digit + done_so_far)
                        count_trials(base, 3, i * UNROLL + k)
                        dve.tensor_scalar(bits[:, :], bits[:, :], 2, None, ALU.logical_shift_right).then_inc(dve_step, 1)
                        dve.wait_ge(dve_step, base + 4)
                at[0] += DIGITS * per_digit
                then(dve.memset(bits[:, 0:1], 1))
                count_trials(at[0], 1, DIGITS)
                at[0] += 3
                then(dve.memset(digit[:, :], 0.0))
                then(dve.tensor_tensor(threshold[:, :], found[:, :].bitcast(F32), sign[:, :], ALU.mult))
                then(dve.tensor_scalar(equal[:, :], logits[:, :], threshold[:, :], None, ALU.is_equal, ALU.add, accum_out=count[:, 1:2]))
                dve.tensor_scalar(hit[:, :], logits[:, :], threshold[:, :], None, ALU.is_gt, ALU.add,
                                  accum_out=count[:, 0:1]).then_inc(counted, 1)
                dve.wait_ge(totalled, DIGITS + 3)
                dve.tensor_scalar(need[:, :], total, -1.0, float(F_ITER), ALU.mult, ALU.add)
                then(dve.tensor_copy(offset[:, :], psum[:, 3, 0:1]))
                then(dve.memset(u[:, :], 1.0))
                then(dve.tensor_tensor_scan(rank[:, :], u[:, :], equal[:, :], offset[:, :], ALU.mult, ALU.add))
                then(dve.scalar_tensor_tensor(equal[:, :], rank[:, :], need[:, :], equal[:, :], ALU.is_le, ALU.mult))
                then(dve.tensor_tensor(chosen[:, :], hit[:, :], equal[:, :], ALU.add))
                then(dve.tensor_tensor(combined[:, :], history[:, :], chosen[:, :], ALU.max))
                then(dve.tensor_tensor(hit[:, :], combined[:, :], history[:, :], ALU.subtract))
                then(dve.tensor_copy(history[:, :], combined[:, :]))
                dve.tensor_scalar(combined[:, :], hit[:, :], 1.0, None, ALU.mult, ALU.add, accum_out=count[:, 0:1]).then_inc(mask_ready, 1)
                dve.wait_ge(mask_turned, 1)
                dve.tensor_copy(maskT[:, :, :], psum[:, 5, 0:3 * P].rearrange("p (j c) -> p j c", j=3))
                then(dve.tensor_scalar(novelty[:, :], psum[:, 6, 0:1], 1.0 / (B * F_ITER), None, ALU.mult))
                then(dve.tensor_scalar(little[:, :], novelty[:, :], 0.7, None, ALU.is_lt))
                then(dve.tensor_copy(done[:, :], little[:, :]))


def attention16(nc, kind, psum, XI, XO, stats6, mean, rstd, mhalf, small, ident, ident_bf, ones, cols,
                weights, ctxT_in, moe_weights):
    l1 = kind == "l1"
    H, HD = 16, 8
    K = C if l1 else P
    G1 = cols[:, 6:7]
    with ExitStack() as sems, ExitStack() as st:
        def sb(name, shape, dt=F32):
            return st.enter_context(nc.sbuf_tensor(f"{kind}_{name}", shape, dt))

        sem = sems.enter_context(signals(nc, kind))
        wq, wk, wv, wo = (weights[k] for k in ("wq", "wk", "wv", "wo"))
        wdkv = None if l1 else weights["wdkv"]
        bias = sb("bias", [P, K], BF16)
        own_rows = sb("own_rows", [P, H])
        scale = sb("scale", [P, B])
        step = sem("moments_step")
        var_ready = sem("var_ready")
        all_scales = sem("all_scales")
        made = sem("made")
        with nc.Block() as block:
            @block.vector
            def _(dve):
                moments(dve, stats6, mean, small, step)
                dve.tensor_scalar(small[:, 0, :], small[:, 3, :], LN_EPS, None, ALU.add).then_inc(var_ready, 1)
                if l1:
                    dve.tensor_scalar(bias[:, :], weights["mask"][:, :], 0.0, -2e9, ALU.is_equal, ALU.mult)
                    return
                dve.tensor_scalar(small[:, 1, :], small[:, 3, :], 1.0 + RMS_EPS, RMS_EPS * LN_EPS, ALU.mult,
                                  ALU.add).then_inc(var_ready, 1)

            @block.gpsimd
            def _(pool):
                if not l1:
                    pool.memset(bias[:, :], 0.0).then_inc(made, 1)
                pool.memset(own_rows[:, :], 1.0).then_inc(made, 1)
                n = 1 if l1 else 2
                pool.wait_ge(made, n)
                if not l1:
                    pool.affine_select(out=bias[:, :], in_=bias[:, :], compare_op=ALU.is_ge, fill=-1e9, base=0,
                                       pattern=[[-1, K]], channel_multiplier=1)
                pool.affine_select(out=own_rows[:, :], in_=own_rows[:, :], compare_op=ALU.is_ge, fill=0.0, base=0,
                                   pattern=[[-HD, H]], channel_multiplier=1).then_inc(made, 1)
                pool.wait_ge(made, n + 1)
                pool.affine_select(out=own_rows[:, :], in_=own_rows[:, :], compare_op=ALU.is_ge, fill=0.0, base=HD - 1,
                                   pattern=[[HD, H]], channel_multiplier=-1)
                pool.wait_ge(var_ready, 1 if l1 else 2)
                inverse_roots(pool, rstd, small[:, 0, :], mhalf, slice(0, FIRST))
                if not l1:
                    inverse_roots(pool, scale, small[:, 1, :], mhalf, slice(0, FIRST))

        zn = sb("zn16", [P, D])
        zT = sb("zT16", [D, P])
        cT = [sb(f"cT{i}", [D, C]) for i in range(2)]
        latT = sb("latT", [LAT, P])
        kT = sb("kT", [P, K])
        QT = [sb(f"QT{i}", [P, P]) for i in range(2)]
        KX = [sb(f"KX{i}", [P, H, K]) for i in range(2)]

        V = [sb(f"V{i}", [P, 4 * (P + HD)]) for i in range(2)]
        names = ("z_made z_turned z_copied q_proj q_copied lat_copied k_proj v_proj k_copied v_copied k_spread x_added x_stats "
                 "v_zeroed").split()
        s = {name: sem(name) for name in names}
        c_loaded = [sem(f"c_loaded{i}") for i in range(2)]
        moe_weights_loaded = sem("moe_weights_loaded")
        cell = {}

        def score(pe, n, u, c):
            par = cell["par"]
            wait(pe, s["q_copied"], n + 1)
            wait(pe, s["k_spread"], n + 1)
            pe.matmul(psum[:, 2 * u + c, 0:4 * K], ident_bf[:, :], bias[:, :].unsqueeze(1).broadcast_to([P, 4, K]),
                      start=True, stop=False, skip_group_check=True)
            h = 8 * u + 4 * c
            return pe.matmul(psum[:, 2 * u + c, 0:4 * K], QT[par][:, :], KX[par][:, h:h + 4, :].rearrange("p h k -> p (h k)"),
                             start=False, stop=True, skip_group_check=True)

        pt_plan = ([(j, 0, K) for j in range(4)], [(4 + j, 0, K) for j in range(4)])
        r_wide = sb("r_wide", [P, 4, 4, HD])
        r_spread = sb("r_spread", [P, P])
        first_half = sb("first_half", [P, P])
        both_halves = sb("both_halves", [P, P])
        outT = sb("outT", [P, P])
        sum_repeated = [sem(f"sum_repeated{u}") for u in range(2)]
        r_turned = sem("r_turned")
        r_copied = sem("r_copied")
        half_taken = sem("half_taken")
        halves_added = sem("halves_added")
        out_scaled = sem("out_scaled")
        projected = sem("projected")
        projection_taken = sem("projection_taken")

        def bank4_free(pe, n, u):
            if u == 0:
                wait(pe, r_copied, n)
            else:
                wait(pe, t["pt0_copied"][0], n + 1)

        def bank5_free(pe, n, u):
            if u == 0:
                wait(pe, projection_taken, n)
            else:
                wait(pe, half_taken, n + 1)

        t = softmax_units(nc, st, sem, psum, 8, K, pt_plan, score, bank4_free, bank5_free, ident, kind)
        pv_done, probsT = t["pv_done"], t["probsT"]

        def invert_sums(dve, n, u):
            t["dve_invert"](dve, n, u)
            wait(dve, r_turned, n)
            by_tile = t["r_sums"][u][:, :].rearrange("p (s t) -> p t s", t=4).unsqueeze(3).broadcast_to([P, 4, 2, HD])
            dve.tensor_copy(r_wide[:, :, 2 * u:2 * u + 2, :], by_tile).then_inc(sum_repeated[u], 1)

        def turn_sums(pe, n):
            for u in range(2):
                wait(pe, sum_repeated[u], n + 1)
            wait(pe, t["pt0_copied"][1], n + 1)
            pe.transpose(psum[:, 4, 0:P], r_wide[:, :, :, :].rearrange("p t s d -> p (t s d)"), ident[:, :]).then_inc(r_turned, 1)

        def copy_sums(dve, n):
            wait(dve, r_turned, n + 1)
            wait(dve, out_scaled, n)
            dve.tensor_copy(r_spread[:, :], psum[:, 4, 0:P]).then_inc(r_copied, 1)

        def multiply_v(pe, n, u, par):
            wait(pe, t["pt0_copied"][u], n + 1)
            wait(pe, t["pt1_copied"][u], n + 1)
            for slot in (2 * u, 2 * u + 1):
                for tile in range(4):
                    mm = pe.matmul(psum[32 * tile:32 * tile + 32, 5, 0:P], V[par][0:K, slot * P + 32 * tile:slot * P + 32 * tile + 32],
                                   probsT[u][0:K, slot - 2 * u, tile, :], start=(slot == 2 * u), stop=(slot == 2 * u + 1),
                                   skip_group_check=True)
            mm.then_inc(pv_done[u], 1)

        def take_first_half(dve, n):
            wait(dve, pv_done[0], n + 1)
            wait(dve, halves_added, n)
            dve.tensor_copy(first_half[:, :], psum[:, 5, 0:P]).then_inc(half_taken, 1)

        def scale_out(dve, n):
            wait(dve, pv_done[1], n + 1)
            wait(dve, half_taken, n + 1)
            wait(dve, out_scaled, n)
            dve.tensor_tensor(both_halves[:, :], psum[:, 5, 0:P], first_half[:, :], ALU.add).then_inc(halves_added, 1)
            wait(dve, halves_added, n + 1)
            wait(dve, r_copied, n + 1)
            wait(dve, projected, n)
            dve.tensor_tensor(outT[:, :], both_halves[:, :], r_spread[:, :], ALU.mult).then_inc(out_scaled, 1)

        def project(pe, n):
            wait(pe, out_scaled, n + 1)
            pe.matmul(psum[:, 5, 0:D], outT[:, :], wo[:, :], start=True, stop=True).then_inc(projected, 1)

        with nc.Block() as block:
            @block.tensor
            def _(pe):
                def turn_input(m):
                    wait(pe, s["z_made"], m + 1)
                    wait(pe, s["k_copied"], m)
                    pe.transpose(psum[:, 6, 0:P], zn[:, :], ident[:, :]).then_inc(s["z_turned"], 1)

                def project_q(m):
                    wait(pe, s["z_copied"], m + 1)
                    wait(pe, s["v_copied"], m)
                    if not l1:
                        pe.matmul(psum[0:LAT, 7, P:2 * P], wdkv[:, :], zT[:, :], start=True, stop=True)
                    pe.matmul(psum[:, 7, 0:P], wq[:, :], zT[:, :], start=True, stop=True).then_inc(s["q_proj"], 1)

                def project_k(m, par):
                    if l1:
                        wait(pe, c_loaded[par], m // 2 * 16 + 16)
                        pe.matmul(psum[:, 6, 0:K], wk[:, :], cT[par][:, :], start=True, stop=True).then_inc(s["k_proj"], 1)
                    else:
                        wait(pe, s["lat_copied"], m + 1)
                        pe.matmul(psum[:, 6, 0:K], wk[:, :], latT[:, :], start=True, stop=True).then_inc(s["k_proj"], 1)

                def values(m, par):
                    wait(pe, s["q_copied"], m + 1)
                    pe.matmul(psum[0:K, 7, 0:P], cT[par][:, :] if l1 else latT[:, :], wv[:, :], start=True,
                              stop=True).then_inc(s["v_proj"], 1)

                def scores(n, u, par, banks=(0, 1)):
                    cell["par"] = par
                    for bank in banks:
                        t["pe_scores"](pe, n, u, bank)

                def body(n, par, first=False, next_=True, after=True):
                    if after:
                        turn_input(n + 2)
                    if next_:
                        values(n + 1, 1 - par)
                    t["pe_turn_probs0"](pe, n, 0)
                    if not first:
                        project(pe, n - 1)
                    if next_:
                        scores(n + 1, 0, 1 - par, (0,))
                    t["pe_turn_probs1"](pe, n, 0)
                    if next_:
                        scores(n + 1, 0, 1 - par, (1,))
                    if after:
                        project_q(n + 2)
                    multiply_v(pe, n, 0, par)
                    t["pe_turn_probs0"](pe, n, 1)
                    if after:
                        project_k(n + 2, par)
                    if next_:
                        scores(n + 1, 1, 1 - par, (0,))
                    t["pe_turn_probs1"](pe, n, 1)
                    if next_:
                        scores(n + 1, 1, 1 - par, (1,))
                    turn_sums(pe, n)
                    multiply_v(pe, n, 1, par)

                def prepare(m):
                    turn_input(m)
                    project_q(m)
                    project_k(m, m)

                prepare(0)
                values(0, 0)
                scores(0, 0, 0)
                scores(0, 1, 0)
                prepare(1)
                wait(pe, s["k_copied"], 2)
                run_entries(pe, body)
                project(pe, B - 1)

            @block.scalar
            def _(act):
                def copy_input(m):
                    wait(act, s["z_turned"], m + 1)
                    wait(act, s["q_proj"], m)
                    act.activation(zT[:, :], psum[:, 6, 0:P], ACT.Copy, scale=1.0 if l1 else G1).then_inc(s["z_copied"], 1)

                def copy_q(m, par):
                    wait(act, s["q_proj"], m + 1)
                    if not l1:
                        wait(act, s["v_proj"], m)
                        act.copy(latT[:, :], psum[0:LAT, 7, P:2 * P]).then_inc(s["lat_copied"], 1)
                    wait(act, t["scored"][1], m - 1)
                    act.mul(QT[par][:, :], psum[:, 7, 0:P], float(HD) ** -0.5).then_inc(s["q_copied"], 1)

                def copy_k(m):
                    wait(act, s["k_proj"], m + 1)
                    wait(act, s["k_spread"], m)
                    act.copy(kT[:, :], psum[:, 6, 0:K]).then_inc(s["k_copied"], 1)

                def copy_values(m, par):
                    wait(act, s["v_proj"], m + 1)
                    wait(act, t["pv_done"][1], m - 1)
                    placed = V[par][0:K, :].rearrange("k (s c) -> k s c", s=4)[:, :, 0:P].rearrange("k s (t w) -> k s t w", w=32)
                    act.copy(placed[:, :, :, 0:HD], psum[0:K, 7, 0:P].rearrange("k (s t d) -> k s t d", s=4, d=HD)).then_inc(s["v_copied"], 1)

                def body(n, par, first=False, next_=True, after=True):
                    if after:
                        copy_input(n + 2)
                    if next_:
                        copy_values(n + 1, 1 - par)
                    t["act_copy_pt0"](act, n, 0)
                    t["act_exp"](act, n, 1)
                    if after:
                        copy_q(n + 2, par)
                    if after:
                        copy_k(n + 2)
                    t["act_copy_pt0"](act, n, 1)
                    if next_:
                        t["act_exp"](act, n + 1, 0)

                def prepare(m):
                    copy_input(m)
                    copy_q(m, m)
                    copy_k(m)

                wait(act, s["v_zeroed"], 2)
                prepare(0)
                copy_values(0, 0)
                t["act_exp"](act, 0, 0)
                prepare(1)
                run_entries(act, body)

            @block.vector
            def _(dve):
                def norm_input(m):
                    src = XI[:, entries(m), :].rearrange("p a d -> p (a d)")
                    wait(dve, s["z_turned"], m)
                    dve.tensor_scalar(zn[:, :], src, mean[:, entries(m)], (rstd if l1 else scale)[:, entries(m)], ALU.subtract,
                                      ALU.mult).then_inc(s["z_made"], 1)
                    if not l1:
                        dve.tensor_scalar(XO[:, entries(m), :].rearrange("p a d -> p (a d)"), src, mean[:, entries(m)],
                                          rstd[:, entries(m)], ALU.subtract, ALU.mult)

                def add_projection(n):
                    wait(dve, projected, n + 1)
                    xs = XO[:, entries(n), :].rearrange("p a d -> p (a d)")
                    dve.tensor_tensor(xs, psum[:, 5, 0:D], xs, ALU.add).then_inc(projection_taken, 1)
                    wait_apart(dve, projection_taken, n + 1, s["z_made"])
                    dve.bn_stats(stats6[:, entries(n), :].rearrange("p a d -> p (a d)"), xs).then_inc(s["x_stats"], 1)

                def body(n, par, first=False, next_=True, after=True):
                    if after:
                        norm_input(n + 2)
                    if not first:
                        copy_sums(dve, n - 1)
                        scale_out(dve, n - 1)
                    t["dve_max"](dve, n, 1)
                    if not first:
                        add_projection(n - 1)
                    invert_sums(dve, n, 0)
                    t["dve_copy_pt1"](dve, n, 0)
                    take_first_half(dve, n)
                    if next_:
                        t["dve_max"](dve, n + 1, 0)
                    invert_sums(dve, n, 1)
                    t["dve_copy_pt1"](dve, n, 1)

                for q in range(2):
                    dve.memset(V[q][:, :], 0.0).then_inc(s["v_zeroed"], 1)
                norm_input(0)
                t["dve_max"](dve, 0, 0)
                norm_input(1)
                run_entries(dve, body, before_loop=lambda: wait(dve, all_scales, 1 if l1 else 2))
                copy_sums(dve, B - 1)
                scale_out(dve, B - 1)
                add_projection(B - 1)

            @block.gpsimd
            def _(pool):
                def spread_k(m, par):
                    wait(pool, s["k_copied"], m + 1)
                    wait(pool, t["scored"][1], m - 1)
                    pool.tensor_tensor(KX[par][:, :, :], kT[:, :].unsqueeze(1).broadcast_to([P, H, K]),
                                       own_rows[:, :].unsqueeze(2).broadcast_to([P, H, K]), ALU.mult).then_inc(s["k_spread"], 1)

                spread_k(0, 0)
                if not l1:
                    inverse_roots(pool, scale, small[:, 1, :], mhalf, slice(FIRST, B)).then_inc(all_scales, 1)
                spread_k(1, 1)
                inverse_roots(pool, rstd, small[:, 0, :], mhalf, slice(FIRST, B)).then_inc(all_scales, 1)
                with pool.Fori(0, B // 2 - 1) as i:
                    spread_k(2 * i + 2, 0)
                    spread_k(2 * i + 3, 1)

            if not l1:
                @block.sync
                def _(sp):
                    for tile, src in moe_weights:
                        sp.dma_start(tile[...], src).then_inc(moe_weights_loaded, 16)
                    sp.wait_ge(moe_weights_loaded, 16 * len(moe_weights))
            else:
                @block.sync
                def _(sp):
                    def load(m, par):
                        wait(sp, s["v_proj"], m - 1)
                        sp.dma_start(cT[par][:, :], ctxT_in[entries(m)].rearrange("a d t -> (a d) t")).then_inc(c_loaded[par], 16)

                    load(0, 0)
                    load(1, 1)
                    with sp.Fori(0, B // 2 - 1) as i:
                        load(2 * i + 2, 0)
                        load(2 * i + 3, 1)


def moe(nc, psum, X2, X3, stats6, mean, rms, mhalf, small, ident, cols, weights, out):
    NE, HID, HALVES = 8, 256, 2
    G2 = cols[:, 7:8]
    N = GB * P
    with ExitStack() as sems, ExitStack() as st:
        def sb(name, shape, dt=F32):
            return st.enter_context(nc.sbuf_tensor(name, shape, dt))

        sem = sems.enter_context(signals(nc, "moe"))
        w1, w2, gate = (weights[k] for k in ("w1", "w2", "gate"))
        index = sb("index", [P, NE])
        step, var_ready, iota_made = sem("moments_step"), sem("var_ready"), sem("iota_made")
        index_i = sb("index_i", [P, NE], I32)
        with nc.Block() as block:
            @block.vector
            def _(dve):
                moments(dve, stats6, mean, small, step)
                dve.tensor_tensor(small[:, 0, :], mean[:, :], mean[:, :], ALU.mult).then_inc(var_ready, 1)
                dve.wait_ge(var_ready, 1)
                dve.tensor_tensor(small[:, 1, :], small[:, 0, :], small[:, 3, :], ALU.add).then_inc(var_ready, 1)
                dve.wait_ge(var_ready, 2)
                dve.tensor_scalar(small[:, 2, :], small[:, 1, :], RMS_EPS, None, ALU.add).then_inc(var_ready, 1)
                dve.wait_ge(iota_made, 1)
                dve.tensor_copy(index[:, :], index_i[:, :])

            @block.gpsimd
            def _(pool):
                pool.iota(index_i[:, :], pattern=[[1, NE]], base=0, channel_multiplier=0).then_inc(iota_made, 1)
                pool.wait_ge(var_ready, 3)
                inverse_roots(pool, rms, small[:, 2, :], mhalf, slice(0, GB))

        hn = sb("hn", [P, GB, D])
        hT = [sb(f"moe_hT{i}", [D, N]) for i in range(2)]
        logits = sb("moe_logits", [P, GB, NE])
        best = sb("best", [P, GB, NE])
        best_at = sb("best_at", [P, GB, NE], U32)
        best_at_f = sb("best_at_f", [P, GB, NE])
        margin = sb("margin", [P, GB])
        tanh_half = sb("tanh_half", [P, GB])
        gates = sb("gates", [P, 2, GB])
        first_part = sb("first_part", [P, GB, NE])
        second_part = sb("second_part", [P, GB, NE])
        combine = [sb(f"combine{i}", [P, GB, NE]) for i in range(2)]
        RING = 4
        hid = [sb(f"hid{i}", [P, N]) for i in range(RING)]
        prod = [sb(f"prod{i}", [P, GB, D]) for i in range(2)]
        acc = [sb(f"acc{i}", [P, GB, D]) for i in range(2)]
        names = ("h_made h_turned h_copied gated logits_copied best_done index_done index_copied margin_done tanh_done gates_done "
                 "parts_made combined x_summed all_scales").split()
        s = {name: sem(name) for name in names}
        NC_ = NE * HALVES
        hidden = [sem(f"hidden{i}") for i in range(NC_)]
        activated = [sem(f"activated{i}") for i in range(NC_)]
        expert = [sem(f"expert{e}") for e in range(NE)]
        weighted = [sem(f"weighted{e}") for e in range(NE)]
        summed = [sem(f"summed{e}") for e in range(NE)]
        BANKS = 3
        stored = [sem("stored0"), sem("stored1")]
        def last_in_ring(i, size, n):
            return (i - size, 0) if i >= size else (max(c for c in range(n) if c % size == i % size), 1)

        with nc.Block() as block:
            @block.tensor
            def _(pe):
                def turn_input(g):
                    wait(pe, s["h_made"], g + 1)
                    wait(pe, s["h_copied"], g)
                    for b in range(GB):
                        tr = pe.transpose(psum[:, 0, b * P:(b + 1) * P], hn[:, b, :], ident[:, :])
                    tr.then_inc(s["h_turned"], 1)

                def ask_gate(g, par):
                    wait(pe, s["h_copied"], g + 1)
                    wait(pe, s["logits_copied"], g)
                    for b in range(GB):
                        mm = pe.matmul(psum[:, 1, b * NE:(b + 1) * NE], hT[par][:, b * P:(b + 1) * P], gate[:, :],
                                       start=True, stop=True)
                    mm.then_inc(s["gated"], 1)

                def up(g, par, i):
                    before, back = last_in_ring(i, BANKS, NC_)
                    wait(pe, activated[before], g + 1 - back)
                    e, half = divmod(i, HALVES)
                    pe.matmul(psum[:, 2 + i % BANKS, :], w1[:, e, half * P:(half + 1) * P], hT[par][:, :],
                              start=True, stop=True).then_inc(hidden[i], 1)

                def down(g, e):
                    before, back = last_in_ring(e, 2, NE)
                    wait(pe, weighted[before], g + 1 - back)
                    wait(pe, activated[2 * e + 1], g + 1)
                    for b in range(GB):
                        for half in range(HALVES):
                            i = 2 * e + half
                            mm = pe.matmul(psum[:, 5 + e % 2, b * D:(b + 1) * D], hid[i % RING][:, b * P:(b + 1) * P], w2[:, i, :],
                                           start=(half == 0), stop=(half == HALVES - 1))
                    mm.then_inc(expert[e], 1)

                def body(g, par, final=False):
                    for i in range(NC_):
                        up(g, par, i)
                        if i % 2 == 1 and i >= 3:
                            down(g, (i - 3) // 2)
                        if i == 7 and not final:
                            turn_input(g + 1)
                        if i == 9 and not final:
                            ask_gate(g + 1, 1 - par)
                    down(g, NE - 1)

                turn_input(0)
                ask_gate(0, 0)
                body(0, 0)
                with pe.Fori(0, NG // 2 - 1) as i:
                    body(2 * i + 1, 1)
                    body(2 * i + 2, 0)
                body(NG - 1, 1, final=True)

            @block.scalar
            def _(act):
                def copy_h(g, par):
                    wait(act, s["h_turned"], g + 1)
                    wait(act, hidden[NC_ - 1], g - 1)
                    act.activation(hT[par][:, :], psum[:, 0, :], ACT.Copy, scale=G2).then_inc(s["h_copied"], 1)

                def squash(g):
                    wait(act, s["margin_done"], g + 1)
                    wait(act, s["gates_done"], g)
                    act.activation(tanh_half[:, :], margin[:, :], ACT.Tanh, scale=0.5).then_inc(s["tanh_done"], 1)

                def body(g, par, final=False):
                    for i in range(NC_):
                        wait(act, hidden[i], g + 1)
                        if i >= RING:
                            wait(act, expert[(i - RING) // 2], g + 1)
                        else:
                            wait(act, expert[(NC_ - RING + i) // 2], g)
                        act.activation(hid[i % RING][:, :], psum[:, 2 + i % BANKS, :], ACT.Silu).then_inc(activated[i], 1)
                        if i == 7 and not final:
                            copy_h(g + 1, 1 - par)
                        if i == 13 and not final:
                            squash(g + 1)

                copy_h(0, 0)
                squash(0)
                body(0, 0)
                with act.Fori(0, NG // 2 - 1) as i:
                    body(2 * i + 1, 1)
                    body(2 * i + 2, 0)
                body(NG - 1, 1, final=True)

            @block.vector
            def _(dve):
                def norm(g):
                    wait(dve, s["h_turned"], g)
                    for b in range(GB):
                        n = g * GB + b
                        i = dve.tensor_scalar(hn[:, b, :], X3[:, entries(n), :].rearrange("p a d -> p (a d)"), rms[:, entries(n)],
                                              None, ALU.mult)
                    i.then_inc(s["h_made"], 1)

                def choose(g):
                    wait(dve, s["gated"], g + 1)
                    dve.tensor_copy(logits[:, :, :], psum[:, 1, 0:GB * NE].rearrange("p (b e) -> p b e", e=NE)).then_inc(s["logits_copied"], 1)
                    wait_apart(dve, s["logits_copied"], g + 1, s["h_made"])
                    for b in range(GB):
                        i = dve.max(best[:, b, :], logits[:, b, :])
                    i.then_inc(s["best_done"], 1)
                    wait_apart(dve, s["best_done"], g + 1, s["h_made"])
                    for b in range(GB):
                        i = dve.max_index(best_at[:, b, :], best[:, b, :], logits[:, b, :])
                    dve.tensor_tensor(margin[:, :], best[:, :, 0], best[:, :, 1], ALU.subtract).then_inc(s["margin_done"], 1)
                    wait(dve, s["margin_done"], g + 1)
                    dve.tensor_copy(best_at_f[:, :, :], best_at[:, :, :]).then_inc(s["index_copied"], 1)

                def weigh(g, par):
                    wait(dve, s["tanh_done"], g + 1)
                    dve.tensor_scalar(gates[:, 0, :], tanh_half[:, :], 0.5, 0.5, ALU.mult, ALU.add)
                    dve.tensor_scalar(gates[:, 1, :], tanh_half[:, :], -0.5, 0.5, ALU.mult, ALU.add).then_inc(s["gates_done"], 1)
                    wait(dve, s["gates_done"], g + 1)
                    wait(dve, s["index_copied"], g + 1)
                    for b in range(GB):
                        dve.tensor_scalar(first_part[:, b, :], index[:, :], best_at_f[:, b, 0:1], gates[:, 0, b:b + 1],
                                          ALU.is_equal, ALU.mult)
                        i = dve.tensor_scalar(second_part[:, b, :], index[:, :], best_at_f[:, b, 1:2], gates[:, 1, b:b + 1],
                                              ALU.is_equal, ALU.mult)
                    i.then_inc(s["parts_made"], 1)
                    wait(dve, s["parts_made"], g + 1)
                    dve.tensor_tensor(combine[par][:, :, :], first_part[:, :, :], second_part[:, :, :], ALU.add).then_inc(s["combined"], 1)

                def body(g, par, final=False):
                    for e in range(NE):
                        wait(dve, expert[e], g + 1)
                        wait(dve, s["combined"], g + 1)
                        before, back = last_in_ring(e, 2, NE)
                        wait(dve, summed[before], g + 1 - back)
                        dve.tensor_tensor(prod[e % 2][:, :, :], psum[:, 5 + e % 2, :].rearrange("p (b d) -> p b d", b=GB),
                                          combine[par][:, :, e:e + 1].broadcast_to([P, GB, D]), ALU.mult).then_inc(weighted[e], 1)
                        if e == 1 and not final:
                            norm(g + 1)
                        if e == 4 and not final:
                            choose(g + 1)
                        if e == 6 and not final:
                            weigh(g + 1, 1 - par)

                norm(0)
                wait(dve, s["all_scales"], 1)
                choose(0)
                weigh(0, 0)
                body(0, 0)
                with dve.Fori(0, NG // 2 - 1) as i:
                    body(2 * i + 1, 1)
                    body(2 * i + 2, 0)
                body(NG - 1, 1, final=True)

            @block.gpsimd
            def _(pool):
                def body(g, par, final=False):
                    a = acc[par]
                    xs = entries(g * GB, GB)
                    wait(pool, stored[par], 8 * GB * (g - par))
                    pool.tensor_tensor(a[:, :, :], X2[:, xs, :], X3[:, xs, :], ALU.add).then_inc(s["x_summed"], 1)
                    wait(pool, s["x_summed"], g + 1)
                    for e in range(NE):
                        wait(pool, weighted[e], g + 1)
                        if e:
                            wait(pool, summed[e - 1], g + 1)
                        pool.tensor_tensor(a[:, :, :], a[:, :, :], prod[e % 2][:, :, :], ALU.add).then_inc(summed[e], 1)

                inverse_roots(pool, rms, small[:, 2, :], mhalf, slice(GB, B)).then_inc(s["all_scales"], 1)
                body(0, 0)
                body(1, 1)
                with pool.Fori(0, NG // 2 - 1) as i:
                    body(2 * i + 2, 0)
                    body(2 * i + 3, 1)

            @block.sync
            def _(sp):
                def store(g, par):
                    wait(sp, summed[NE - 1], g + 1)
                    for b in range(GB):
                        sp.dma_start(out[entries(g * GB + b)].rearrange("a t d -> (a t) d"), acc[par][:, b, :]).then_inc(stored[par], 16)

                store(0, 0)
                with sp.Fori(0, NG // 2 - 1) as i:
                    store(2 * i + 1, 1)
                    store(2 * i + 2, 0)
                store(NG - 1, 1)
                sp.wait_ge(stored[0], 16 * GB * (NG // 2))
                sp.wait_ge(stored[1], 16 * GB * (NG // 2))


def lay_out(np, i):
    f = lambda a: np.ascontiguousarray(np.asarray(a))
    def by_tile(w_inT):
        return f(np.transpose(f(w_inT).reshape(4, 4, 8, D), (1, 0, 2, 3)).reshape(P, D))
    cols = np.stack([f(i[n]) for n in ("L0_xattn_ln_x_w", "L0_xattn_ln_x_b", "L0_xattn_ln_l_w", "L0_xattn_ln_l_b")]
                    + [np.concatenate([f(i[n]), f(i[n])]) for n in ("L0_xattn_q_scale", "L0_xattn_k_scale")]
                    + [f(i["L1_ffn_g1"]), f(i["L1_ffn_g2"])], axis=1)
    T = lambda n: f(np.asarray(i[n]).T)
    return {
        "x_in": f(i["x"]), "ctx_in": f(i["ctx_1024"]), "ctxT_in": f(np.transpose(np.asarray(i["ctx_1024"]), (0, 2, 1))),
        "keep_in": f(i["mask_BxS2_bk0"]).reshape(1, B * C),
        "qk_mask_in": f(i["mask_1x1xSxS2_ik0"]).reshape(P, C), "cols_in": f(cols),
        "lnow_in": f(i["L0_xattn_ln_o_w"]).reshape(1, D), "lnob_in": f(i["L0_xattn_ln_o_b"]).reshape(1, D),
        "wq0_in": f(i["L0_xattn_Wq"]), "wkv0_in": f(i["L0_xattn_Wkv"]), "wo0_in": f(i["L0_xattn_Wo"]),
        "wm_in": T("L0_ffn_Wm"), "wp_in": T("L0_ffn_Wp"), "wc1_in": T("L0_ffn_Wc1"), "wc2_in": T("L0_ffn_Wc2"),
        "wq1_in": T("L1_xattn_w_q"), "wk1_in": T("L1_xattn_w_k"), "wv1_in": T("L1_xattn_w_v"),
        "wo1_in": by_tile(np.asarray(i["L1_xattn_w_o"]).T),
        "wq2_in": f(i["L1_ffn_Wq"]), "wdkv_in": f(i["L1_ffn_Wdkv"]), "wuk_in": f(i["L1_ffn_Wuk"]),
        "wuv_in": f(i["L1_ffn_Wuv"]), "wo2_in": by_tile(i["L1_ffn_Wo"]),
        "gate_in": f(i["L1_ffn_gate_w"]), "w1_in": f(np.transpose(np.asarray(i["L1_ffn_w1"]), (1, 0, 2))),
        "w2_in": f(i["L1_ffn_w2"]).reshape(8 * 256, D),
    }


def kernel(**inputs):
    import numpy as _np
    import concourse.bacc as _bacc
    from concourse import mybir as _mybir
    from concourse.bass_utils import run_bass_kernel_spmd as _run

    nc = _bacc.Bacc("TRN2", target_bir_lowering=False, num_devices=1)
    arrays = lay_out(_np, inputs)
    args = [nc.dram_tensor(n, a.shape, _mybir.dt.from_np(a.dtype), kind="ExternalInput").ap() for n, a in arrays.items()]
    out = nc.dram_tensor("out_dram", (B, P, D), _mybir.dt.float32, kind="ExternalOutput").ap()
    mega_kernel(nc, *args, out)
    r = _run(nc, [arrays], core_ids=[0])
    return r.results[0]["out_dram"]
```
